# Optimizing a Trainium2 kernel written in Bass

```python
import numpy as np
import jax
import jax.numpy as jnp

def _softmax(x, axis=-1):
    return jax.nn.softmax(x, axis=axis)

def _gelu(x):
    return jax.nn.gelu(x, approximate=True)

def _silu(x):
    return jax.nn.silu(x)

def _sigmoid(x):
    return jax.nn.sigmoid(x)

def _layernorm(x, axis=-1, eps=1e-05):
    m = jnp.mean(x, axis=axis, keepdims=True)
    v = jnp.var(x, axis=axis, keepdims=True)
    return (x - m) / jnp.sqrt(v + eps)

def _scatter_add(tgt, idx, src, axis=0):
    return tgt.at[idx].add(src)

def _segment_sum(src, seg, n):
    return jax.ops.segment_sum(src, seg, n)
kernel_name = 'mk_early_fusion_d2_tok_img768_r4_008214'

def setup_inputs(seed: int=0):
    np.random.seed(seed)
    _w = jnp.asarray

    def _rec_inputs():
        import jax
        import jax.numpy as jnp
        _rk = jax.random.key(seed)
        x = -0.00040386 + 0.999972 * jax.random.normal(jax.random.fold_in(_rk, 1), (64, 64, 64, 3), jnp.float32)
        txt = -0.000238947 + 0.999946 * jax.random.normal(jax.random.fold_in(_rk, 2), (64, 128, 192), jnp.float32)
        return (x, txt)
    x, txt = _rec_inputs()

    def _L0_tok_setup():
        import jax, jax.numpy as jnp
        import numpy as np
        IMG = 64
        PATCH = 16
        C = 3
        D = 192
        NP_ = (IMG // PATCH) ** 2
        B = 64

        def _patchify(x):
            Bn, H, Wd, Cn = x.shape
            hp, wp = (H // PATCH, Wd // PATCH)
            x = x.reshape(Bn, hp, PATCH, wp, PATCH, Cn)
            x = x.transpose(0, 1, 3, 2, 4, 5)
            return x.reshape(Bn, hp * wp, PATCH * PATCH * Cn)
        key = jax.random.key(seed)
        k1, k2, k3 = jax.random.split(key, 3)
        x = jax.random.normal(k1, (B, IMG, IMG, C), dtype=jnp.float32)
        patch_dim = C * PATCH * PATCH
        W = jax.random.normal(k2, (patch_dim, D), dtype=jnp.float32) / np.sqrt(patch_dim)
        b = jnp.zeros((D,), dtype=jnp.float32)
        pos_emb = jax.random.normal(k3, (NP_, D), dtype=jnp.float32) * 0.02
        return {'x': x, 'W': W, 'b': b, 'pos_emb': pos_emb}
    _L0_tok_all = _L0_tok_setup()
    _L0_tok_in = {k: v for k, v in _L0_tok_all.items() if k in ('W', 'b', 'pos_emb')}
    del _L0_tok_all

    def _L0_attn_setup():
        import jax, jax.numpy as jnp
        import numpy as np
        DIM = 192
        HEADS = 12
        HEAD_DIM = DIM // HEADS
        SCALE = HEAD_DIM ** (-0.5)
        H_CONST = 4
        key = jax.random.key(seed)
        ks = jax.random.split(key, 9)
        B, N = (4, 256)
        s = DIM ** (-0.5)
        return {'x': jax.random.normal(ks[0], (B, N, DIM), dtype=jnp.float32), 'qkv_w': jax.random.normal(ks[1], (3 * DIM, DIM), dtype=jnp.float32) * s, 'proj_l_w': jax.random.normal(ks[2], (HEADS, HEADS), dtype=jnp.float32) * HEADS ** (-0.5), 'proj_l_b': jax.random.normal(ks[3], (HEADS,), dtype=jnp.float32) * 0.02, 'proj_w_w': jax.random.normal(ks[4], (HEADS, HEADS), dtype=jnp.float32) * HEADS ** (-0.5), 'proj_w_b': jax.random.normal(ks[5], (HEADS,), dtype=jnp.float32) * 0.02, 'lamb': jax.random.normal(ks[6], (HEADS,), dtype=jnp.float32) * 0.1, 'proj_out_w': jax.random.normal(ks[7], (DIM, DIM), dtype=jnp.float32) * s, 'proj_out_b': jax.random.normal(ks[8], (DIM,), dtype=jnp.float32) * 0.02}
    _L0_attn_all = _L0_attn_setup()
    _L0_attn_in = {k: v for k, v in _L0_attn_all.items() if k in ('qkv_w', 'proj_l_w', 'proj_l_b', 'proj_w_w', 'proj_w_b', 'lamb', 'proj_out_w', 'proj_out_b')}
    del _L0_attn_all

    def _L0_ffn_setup():
        import jax, jax.numpy as jnp
        import numpy as np
        NUM_EXPERTS = 8
        TOP_K = 2
        CAPACITY_FACTOR = 1.25
        MAX_GROUP_SIZE = 1024
        MIN_EXPERT_CAPACITY = 4

        def _moe_forward(x, w_router, wi, wo):
            B, T, D = x.shape
            E = NUM_EXPERTS
            num_tokens = B * T
            G = max(num_tokens // MAX_GROUP_SIZE, E)
            while num_tokens % G != 0 or G % E != 0:
                G += 1
            S = num_tokens // G
            C = max(int(TOP_K * CAPACITY_FACTOR * S / E), MIN_EXPERT_CAPACITY)
            xg = x.reshape(G, S, D)
            logits = jnp.einsum('gsd,de->gse', xg.astype(jnp.float32), w_router.astype(jnp.float32))
            probs = jax.nn.softmax(logits, axis=-1)
            gate, idx = jax.lax.top_k(probs, TOP_K)
            idx_kf = jnp.swapaxes(idx, 1, 2).reshape(G, TOP_K * S)
            mask = jax.nn.one_hot(idx_kf, E, dtype=jnp.int32)
            prio = jnp.cumsum(mask, axis=1) * mask - 1
            prio = jnp.swapaxes(prio.reshape(G, TOP_K, S, E), 1, 2)
            prio_se = prio.max(axis=2)
            gate_se = jnp.einsum('gsk,gske->gse', gate, jax.nn.one_hot(idx, E, dtype=gate.dtype))
            dispatch = jax.nn.one_hot(prio_se, C, dtype=x.dtype)
            combine = dispatch * gate_se[..., None].astype(x.dtype)
            expert_in = jnp.einsum('gsec,gsd->egcd', dispatch, xg)
            h = jax.nn.relu(jnp.einsum('egcd,edf->egcf', expert_in, wi))
            expert_out = jnp.einsum('egcf,efd->egcd', h, wo)
            out = jnp.einsum('gsec,egcd->gsd', combine, expert_out)
            return out.reshape(B, T, D)
        key = jax.random.key(seed)
        k1, k2, k3, k4 = jax.random.split(key, 4)
        B, T, D, F = (8, 256, 192, 768)
        x = jax.random.normal(k1, (B, T, D), jnp.float32)
        w_router = jax.random.normal(k2, (D, NUM_EXPERTS), jnp.float32) * D ** (-0.5)
        wi = jax.random.normal(k3, (NUM_EXPERTS, D, F), jnp.float32) * D ** (-0.5)
        wo = jax.random.normal(k4, (NUM_EXPERTS, F, D), jnp.float32) * F ** (-0.5)
        return {'x': x, 'w_router': w_router, 'wi': wi, 'wo': wo}
    _L0_ffn_all = _L0_ffn_setup()
    _L0_ffn_in = {k: v for k, v in _L0_ffn_all.items() if k in ('w_router', 'wi', 'wo')}
    del _L0_ffn_all

    def _L1_attn_setup():
        import jax, jax.numpy as jnp
        import numpy as np
        B, N, DIM, H, DH = (64, 197, 192, 12, 64)
        key = jax.random.key(seed)
        k1, k2, k3, k4 = jax.random.split(key, 4)
        x = jax.random.normal(k1, (B, N, DIM), dtype=jnp.float32)
        W_qkv = jax.random.normal(k2, (DIM, 3 * H * DH), dtype=jnp.float32) * (2.0 / (DIM + 3 * H * DH)) ** 0.5
        scale = jax.random.uniform(k3, (H,), dtype=jnp.float32)
        W_out = jax.random.normal(k4, (H * DH, DIM), dtype=jnp.float32) * (2.0 / (H * DH + DIM)) ** 0.5
        b_out = jnp.zeros((DIM,), dtype=jnp.float32)
        return {'x': x, 'W_qkv': W_qkv, 'scale': scale, 'W_out': W_out, 'b_out': b_out}
    _L1_attn_all = _L1_attn_setup()
    _L1_attn_in = {k: v for k, v in _L1_attn_all.items() if k in ('W_qkv', 'scale', 'W_out', 'b_out')}
    del _L1_attn_all

    def _L1_ffn_setup():
        import jax, jax.numpy as jnp
        import numpy as np
        DIM = 192
        HEADS = 12
        HD = DIM // HEADS
        MLP = 768
        RHD = 128
        RANK = 64
        BS = 2
        RESERVE = 1
        EPS = 1e-05

        def _ln(x, g, b):
            m = jnp.mean(x, axis=-1, keepdims=True)
            v = jnp.var(x, axis=-1, keepdims=True)
            return (x - m) / jnp.sqrt(v + EPS) * g + b

        def _gelu(t):
            return jax.nn.gelu(t, approximate=False)

        def _forward(x, wq, bq, wk, bk, wv, bv, wo, bo, ln1_g, ln1_b, ln2_g, ln2_b, fc1_w, fc1_b, fc2_w, fc2_b, r_ln_g, r_ln_b, r_in_w, r_in_b, r_o1_w, r_o1_b, r_o2_w, r_o2_b, r_o3_w, r_o3_b, lra_down, lra_up):
            B, N, _ = x.shape
            e = _gelu(_ln(x, r_ln_g, r_ln_b) @ r_in_w.T + r_in_b)
            g = jnp.mean(e[:, RESERVE:, :], axis=1, keepdims=True)
            f = jnp.concatenate([e, jnp.broadcast_to(g, e.shape)], axis=-1)
            h1 = _gelu(f @ r_o1_w.T + r_o1_b)
            h2 = _gelu(h1 @ r_o2_w.T + r_o2_b)
            logits = (h2 @ r_o3_w.T + r_o3_b).reshape(B, N, BS, 2)
            hard = jax.nn.one_hot(jnp.argmax(logits, axis=-1), 2, dtype=x.dtype)
            keep = jnp.broadcast_to(jnp.array([0.0, 1.0], dtype=x.dtype), hard[:, :RESERVE].shape)
            hard = hard.at[:, :RESERVE].set(keep)
            hard = jax.lax.stop_gradient(hard)
            bits = hard[..., 1]
            indices = (bits * jnp.array([2.0, 1.0], dtype=x.dtype)).sum(-1).astype(jnp.int32)
            indices = jax.lax.stop_gradient(indices)
            xa = _ln(x, ln1_g, ln1_b)
            q = (xa @ wq.T + bq).reshape(B, N, HEADS, HD).transpose(0, 2, 1, 3)
            k = (xa @ wk.T + bk).reshape(B, N, HEADS, HD).transpose(0, 2, 1, 3)
            v = (xa @ wv.T + bv).reshape(B, N, HEADS, HD).transpose(0, 2, 1, 3)
            s = jax.nn.softmax(jnp.einsum('bhqd,bhkd->bhqk', q, k) / np.float32(np.sqrt(HD)), axis=-1)
            o = jnp.einsum('bhqk,bhkd->bhqd', s, v).transpose(0, 2, 1, 3).reshape(B, N, DIM)
            o = o @ wo.T + bo
            h = x + bits[:, :, 0:1] * o
            xf = _ln(h, ln2_g, ln2_b)
            ff = _gelu(xf @ fc1_w.T + fc1_b) @ fc2_w.T + fc2_b
            out = h + bits[:, :, 1:2] * ff
            down = jnp.einsum('bnd,krd->bknr', out, lra_down)
            up = jnp.einsum('bknr,kdr->bknd', down, lra_up)
            sel = jax.nn.one_hot(indices, 3, dtype=x.dtype)
            out = out + jnp.einsum('bknd,bnk->bnd', up, sel)
            return out
        key = jax.random.key(seed)
        ks = iter(jax.random.split(key, 40))

        def w(shape, std=0.02):
            return (jax.random.normal(next(ks), shape) * std).astype(jnp.float32)
        B, N = (128, 197)
        inp = {'x': jax.random.normal(next(ks), (B, N, DIM), dtype=jnp.float32)}
        inp.update(wq=w((DIM, DIM)), bq=jnp.zeros((DIM,), jnp.float32), wk=w((DIM, DIM)), bk=jnp.zeros((DIM,), jnp.float32), wv=w((DIM, DIM)), bv=jnp.zeros((DIM,), jnp.float32), wo=w((DIM, DIM)), bo=jnp.zeros((DIM,), jnp.float32), ln1_g=jnp.ones((DIM,), jnp.float32), ln1_b=jnp.zeros((DIM,), jnp.float32), ln2_g=jnp.ones((DIM,), jnp.float32), ln2_b=jnp.zeros((DIM,), jnp.float32), fc1_w=w((MLP, DIM)), fc1_b=jnp.zeros((MLP,), jnp.float32), fc2_w=w((DIM, MLP)), fc2_b=jnp.zeros((DIM,), jnp.float32), r_ln_g=jnp.ones((DIM,), jnp.float32), r_ln_b=jnp.zeros((DIM,), jnp.float32), r_in_w=w((RHD, DIM)), r_in_b=jnp.zeros((RHD,), jnp.float32), r_o1_w=w((RHD, 2 * RHD)), r_o1_b=jnp.zeros((RHD,), jnp.float32), r_o2_w=w((RHD // 2, RHD)), r_o2_b=jnp.zeros((RHD // 2,), jnp.float32), r_o3_w=w((2 * BS, RHD // 2), 0.01), r_o3_b=jnp.array([0.0, 5.0, 0.0, 5.0], dtype=jnp.float32), lra_down=w((3, RANK, DIM), 0.01), lra_up=w((3, DIM, RANK), 0.01))
        return inp
    _L1_ffn_all = _L1_ffn_setup()
    _L1_ffn_in = {k: v for k, v in _L1_ffn_all.items() if k in ('wq', 'bq', 'wk', 'bk', 'wv', 'bv', 'wo', 'bo', 'ln1_g', 'ln1_b', 'ln2_g', 'ln2_b', 'fc1_w', 'fc1_b', 'fc2_w', 'fc2_b', 'r_ln_g', 'r_ln_b', 'r_in_w', 'r_in_b', 'r_o1_w', 'r_o1_b', 'r_o2_w', 'r_o2_b', 'r_o3_w', 'r_o3_b', 'lra_down', 'lra_up')}
    del _L1_ffn_all
    return {'x': x, 'txt': txt, 'L0_tok_W': _L0_tok_in['W'], 'L0_tok_b': _L0_tok_in['b'], 'L0_tok_pos_emb': _L0_tok_in['pos_emb'], 'L0_attn_qkv_w': _L0_attn_in['qkv_w'], 'L0_attn_proj_l_w': _L0_attn_in['proj_l_w'], 'L0_attn_proj_l_b': _L0_attn_in['proj_l_b'], 'L0_attn_proj_w_w': _L0_attn_in['proj_w_w'], 'L0_attn_proj_w_b': _L0_attn_in['proj_w_b'], 'L0_attn_lamb': _L0_attn_in['lamb'], 'L0_attn_proj_out_w': _L0_attn_in['proj_out_w'], 'L0_attn_proj_out_b': _L0_attn_in['proj_out_b'], 'L0_ffn_w_router': _L0_ffn_in['w_router'], 'L0_ffn_wi': _L0_ffn_in['wi'], 'L0_ffn_wo': _L0_ffn_in['wo'], 'L1_attn_W_qkv': _L1_attn_in['W_qkv'], 'L1_attn_scale': _L1_attn_in['scale'], 'L1_attn_W_out': _L1_attn_in['W_out'], 'L1_attn_b_out': _L1_attn_in['b_out'], 'L1_ffn_wq': _L1_ffn_in['wq'], 'L1_ffn_bq': _L1_ffn_in['bq'], 'L1_ffn_wk': _L1_ffn_in['wk'], 'L1_ffn_bk': _L1_ffn_in['bk'], 'L1_ffn_wv': _L1_ffn_in['wv'], 'L1_ffn_bv': _L1_ffn_in['bv'], 'L1_ffn_wo': _L1_ffn_in['wo'], 'L1_ffn_bo': _L1_ffn_in['bo'], 'L1_ffn_ln1_g': _L1_ffn_in['ln1_g'], 'L1_ffn_ln1_b': _L1_ffn_in['ln1_b'], 'L1_ffn_ln2_g': _L1_ffn_in['ln2_g'], 'L1_ffn_ln2_b': _L1_ffn_in['ln2_b'], 'L1_ffn_fc1_w': _L1_ffn_in['fc1_w'], 'L1_ffn_fc1_b': _L1_ffn_in['fc1_b'], 'L1_ffn_fc2_w': _L1_ffn_in['fc2_w'], 'L1_ffn_fc2_b': _L1_ffn_in['fc2_b'], 'L1_ffn_r_ln_g': _L1_ffn_in['r_ln_g'], 'L1_ffn_r_ln_b': _L1_ffn_in['r_ln_b'], 'L1_ffn_r_in_w': _L1_ffn_in['r_in_w'], 'L1_ffn_r_in_b': _L1_ffn_in['r_in_b'], 'L1_ffn_r_o1_w': _L1_ffn_in['r_o1_w'], 'L1_ffn_r_o1_b': _L1_ffn_in['r_o1_b'], 'L1_ffn_r_o2_w': _L1_ffn_in['r_o2_w'], 'L1_ffn_r_o2_b': _L1_ffn_in['r_o2_b'], 'L1_ffn_r_o3_w': _L1_ffn_in['r_o3_w'], 'L1_ffn_r_o3_b': _L1_ffn_in['r_o3_b'], 'L1_ffn_lra_down': _L1_ffn_in['lra_down'], 'L1_ffn_lra_up': _L1_ffn_in['lra_up']}

def reference(x, txt, L0_tok_W, L0_tok_b, L0_tok_pos_emb, L0_attn_qkv_w, L0_attn_proj_l_w, L0_attn_proj_l_b, L0_attn_proj_w_w, L0_attn_proj_w_b, L0_attn_lamb, L0_attn_proj_out_w, L0_attn_proj_out_b, L0_ffn_w_router, L0_ffn_wi, L0_ffn_wo, L1_attn_W_qkv, L1_attn_scale, L1_attn_W_out, L1_attn_b_out, L1_ffn_wq, L1_ffn_bq, L1_ffn_wk, L1_ffn_bk, L1_ffn_wv, L1_ffn_bv, L1_ffn_wo, L1_ffn_bo, L1_ffn_ln1_g, L1_ffn_ln1_b, L1_ffn_ln2_g, L1_ffn_ln2_b, L1_ffn_fc1_w, L1_ffn_fc1_b, L1_ffn_fc2_w, L1_ffn_fc2_b, L1_ffn_r_ln_g, L1_ffn_r_ln_b, L1_ffn_r_in_w, L1_ffn_r_in_b, L1_ffn_r_o1_w, L1_ffn_r_o1_b, L1_ffn_r_o2_w, L1_ffn_r_o2_b, L1_ffn_r_o3_w, L1_ffn_r_o3_b, L1_ffn_lra_down, L1_ffn_lra_up):
    import jax
    import jax.numpy as jnp

    def _L0_tok_ref(x, W, b, pos_emb):
        import jax, jax.numpy as jnp
        import numpy as np
        IMG = 64
        PATCH = 16
        C = 3
        D = 192
        NP_ = (IMG // PATCH) ** 2
        B = 64

        def _patchify(x):
            Bn, H, Wd, Cn = x.shape
            hp, wp = (H // PATCH, Wd // PATCH)
            x = x.reshape(Bn, hp, PATCH, wp, PATCH, Cn)
            x = x.transpose(0, 1, 3, 2, 4, 5)
            return x.reshape(Bn, hp * wp, PATCH * PATCH * Cn)
        patches = _patchify(x)
        proj = jnp.einsum('bnd,de->bne', patches, W) + b
        return proj + pos_emb[None, :, :]

    def _L0_attn_ref(x, qkv_w, proj_l_w, proj_l_b, proj_w_w, proj_w_b, lamb, proj_out_w, proj_out_b):
        import jax, jax.numpy as jnp
        import numpy as np
        DIM = 192
        HEADS = 12
        HEAD_DIM = DIM // HEADS
        SCALE = HEAD_DIM ** (-0.5)
        H_CONST = 4
        B, N, C = x.shape
        qkv = (x @ qkv_w.T).reshape(B, N, 3, HEADS, HEAD_DIM)
        qkv = jnp.transpose(qkv, (2, 0, 3, 1, 4))
        q, k, v = (qkv[0] * SCALE, qkv[1], qkv[2])
        attn = jnp.einsum('bhnd,bhmd->bhnm', q, k)
        attn = jnp.einsum('bhnm,gh->bgnm', attn, proj_l_w) + proj_l_b[:, None, None]
        attn = jax.nn.softmax(attn, axis=-1)
        attn = jnp.einsum('bhnm,gh->bgnm', attn, proj_w_w) + proj_w_b[:, None, None]
        eye = jnp.eye(N, dtype=attn.dtype)[None, None]
        reaction = (H_CONST - 1) * jnp.einsum('bhnk,bhkm->bhnm', attn - eye, attn) + attn
        attn = attn + lamb[None, :, None, None] * reaction
        out = jnp.einsum('bhnm,bhmd->bhnd', attn, v)
        out = jnp.transpose(out, (0, 2, 1, 3)).reshape(B, N, C)
        return out @ proj_out_w.T + proj_out_b

    def _L0_ffn_ref(x, w_router, wi, wo):
        import jax, jax.numpy as jnp
        import numpy as np
        NUM_EXPERTS = 8
        TOP_K = 2
        CAPACITY_FACTOR = 1.25
        MAX_GROUP_SIZE = 1024
        MIN_EXPERT_CAPACITY = 4

        def _moe_forward(x, w_router, wi, wo):
            B, T, D = x.shape
            E = NUM_EXPERTS
            num_tokens = B * T
            G = max(num_tokens // MAX_GROUP_SIZE, E)
            while num_tokens % G != 0 or G % E != 0:
                G += 1
            S = num_tokens // G
            C = max(int(TOP_K * CAPACITY_FACTOR * S / E), MIN_EXPERT_CAPACITY)
            xg = x.reshape(G, S, D)
            logits = jnp.einsum('gsd,de->gse', xg.astype(jnp.float32), w_router.astype(jnp.float32))
            probs = jax.nn.softmax(logits, axis=-1)
            gate, idx = jax.lax.top_k(probs, TOP_K)
            idx_kf = jnp.swapaxes(idx, 1, 2).reshape(G, TOP_K * S)
            mask = jax.nn.one_hot(idx_kf, E, dtype=jnp.int32)
            prio = jnp.cumsum(mask, axis=1) * mask - 1
            prio = jnp.swapaxes(prio.reshape(G, TOP_K, S, E), 1, 2)
            prio_se = prio.max(axis=2)
            gate_se = jnp.einsum('gsk,gske->gse', gate, jax.nn.one_hot(idx, E, dtype=gate.dtype))
            dispatch = jax.nn.one_hot(prio_se, C, dtype=x.dtype)
            combine = dispatch * gate_se[..., None].astype(x.dtype)
            expert_in = jnp.einsum('gsec,gsd->egcd', dispatch, xg)
            h = jax.nn.relu(jnp.einsum('egcd,edf->egcf', expert_in, wi))
            expert_out = jnp.einsum('egcf,efd->egcd', h, wo)
            out = jnp.einsum('gsec,egcd->gsd', combine, expert_out)
            return out.reshape(B, T, D)
        return _moe_forward(x, w_router, wi, wo)

    def _L1_attn_ref(x, W_qkv, scale, W_out, b_out):
        import jax, jax.numpy as jnp
        import numpy as np
        B, N, DIM, H, DH = (64, 197, 192, 12, 64)
        b, n, _ = x.shape
        h = scale.shape[0]
        d = W_qkv.shape[1] // (3 * h)
        qkv = x @ W_qkv
        q, k, v = jnp.split(qkv, 3, axis=-1)
        to_heads = lambda t: t.reshape(b, n, h, d).transpose(0, 2, 1, 3)
        q, k, v = (to_heads(q), to_heads(k), to_heads(v))
        dots = jnp.einsum('bhid,bhjd->bhij', q, k) * scale[None, :, None, None]
        diag = jnp.eye(n, dtype=bool)
        dots = jnp.where(diag[None, None], -jnp.inf, dots)
        scores = jax.nn.softmax(dots, axis=-1)
        out = jnp.einsum('bhij,bhjd->bhid', scores, v)
        out = out.transpose(0, 2, 1, 3).reshape(b, n, h * d)
        return out @ W_out + b_out

    def _L1_ffn_ref(x, wq, bq, wk, bk, wv, bv, wo, bo, ln1_g, ln1_b, ln2_g, ln2_b, fc1_w, fc1_b, fc2_w, fc2_b, r_ln_g, r_ln_b, r_in_w, r_in_b, r_o1_w, r_o1_b, r_o2_w, r_o2_b, r_o3_w, r_o3_b, lra_down, lra_up):
        import jax, jax.numpy as jnp
        import numpy as np
        DIM = 192
        HEADS = 12
        HD = DIM // HEADS
        MLP = 768
        RHD = 128
        RANK = 64
        BS = 2
        RESERVE = 1
        EPS = 1e-05

        def _ln(x, g, b):
            m = jnp.mean(x, axis=-1, keepdims=True)
            v = jnp.var(x, axis=-1, keepdims=True)
            return (x - m) / jnp.sqrt(v + EPS) * g + b

        def _gelu(t):
            return jax.nn.gelu(t, approximate=False)

        def _forward(x, wq, bq, wk, bk, wv, bv, wo, bo, ln1_g, ln1_b, ln2_g, ln2_b, fc1_w, fc1_b, fc2_w, fc2_b, r_ln_g, r_ln_b, r_in_w, r_in_b, r_o1_w, r_o1_b, r_o2_w, r_o2_b, r_o3_w, r_o3_b, lra_down, lra_up):
            B, N, _ = x.shape
            e = _gelu(_ln(x, r_ln_g, r_ln_b) @ r_in_w.T + r_in_b)
            g = jnp.mean(e[:, RESERVE:, :], axis=1, keepdims=True)
            f = jnp.concatenate([e, jnp.broadcast_to(g, e.shape)], axis=-1)
            h1 = _gelu(f @ r_o1_w.T + r_o1_b)
            h2 = _gelu(h1 @ r_o2_w.T + r_o2_b)
            logits = (h2 @ r_o3_w.T + r_o3_b).reshape(B, N, BS, 2)
            hard = jax.nn.one_hot(jnp.argmax(logits, axis=-1), 2, dtype=x.dtype)
            keep = jnp.broadcast_to(jnp.array([0.0, 1.0], dtype=x.dtype), hard[:, :RESERVE].shape)
            hard = hard.at[:, :RESERVE].set(keep)
            hard = jax.lax.stop_gradient(hard)
            bits = hard[..., 1]
            indices = (bits * jnp.array([2.0, 1.0], dtype=x.dtype)).sum(-1).astype(jnp.int32)
            indices = jax.lax.stop_gradient(indices)
            xa = _ln(x, ln1_g, ln1_b)
            q = (xa @ wq.T + bq).reshape(B, N, HEADS, HD).transpose(0, 2, 1, 3)
            k = (xa @ wk.T + bk).reshape(B, N, HEADS, HD).transpose(0, 2, 1, 3)
            v = (xa @ wv.T + bv).reshape(B, N, HEADS, HD).transpose(0, 2, 1, 3)
            s = jax.nn.softmax(jnp.einsum('bhqd,bhkd->bhqk', q, k) / np.float32(np.sqrt(HD)), axis=-1)
            o = jnp.einsum('bhqk,bhkd->bhqd', s, v).transpose(0, 2, 1, 3).reshape(B, N, DIM)
            o = o @ wo.T + bo
            h = x + bits[:, :, 0:1] * o
            xf = _ln(h, ln2_g, ln2_b)
            ff = _gelu(xf @ fc1_w.T + fc1_b) @ fc2_w.T + fc2_b
            out = h + bits[:, :, 1:2] * ff
            down = jnp.einsum('bnd,krd->bknr', out, lra_down)
            up = jnp.einsum('bknr,kdr->bknd', down, lra_up)
            sel = jax.nn.one_hot(indices, 3, dtype=x.dtype)
            out = out + jnp.einsum('bknd,bnk->bnd', up, sel)
            return out
        return _forward(x, wq, bq, wk, bk, wv, bv, wo, bo, ln1_g, ln1_b, ln2_g, ln2_b, fc1_w, fc1_b, fc2_w, fc2_b, r_ln_g, r_ln_b, r_in_w, r_in_b, r_o1_w, r_o1_b, r_o2_w, r_o2_b, r_o3_w, r_o3_b, lra_down, lra_up)
    h = _L0_tok_ref(x, L0_tok_W, L0_tok_b, L0_tok_pos_emb)
    h = jnp.concatenate([h, txt], axis=1)
    h = h + _L0_attn_ref(_layernorm(h, axis=-1), L0_attn_qkv_w, L0_attn_proj_l_w, L0_attn_proj_l_b, L0_attn_proj_w_w, L0_attn_proj_w_b, L0_attn_lamb, L0_attn_proj_out_w, L0_attn_proj_out_b)
    h = h + _L0_ffn_ref(_layernorm(h, axis=-1), L0_ffn_w_router, L0_ffn_wi, L0_ffn_wo)
    h = h + _L1_attn_ref(_layernorm(h, axis=-1), L1_attn_W_qkv, L1_attn_scale, L1_attn_W_out, L1_attn_b_out)
    h = h + _L1_ffn_ref(_layernorm(h, axis=-1), L1_ffn_wq, L1_ffn_bq, L1_ffn_wk, L1_ffn_bk, L1_ffn_wv, L1_ffn_bv, L1_ffn_wo, L1_ffn_bo, L1_ffn_ln1_g, L1_ffn_ln1_b, L1_ffn_ln2_g, L1_ffn_ln2_b, L1_ffn_fc1_w, L1_ffn_fc1_b, L1_ffn_fc2_w, L1_ffn_fc2_b, L1_ffn_r_ln_g, L1_ffn_r_ln_b, L1_ffn_r_in_w, L1_ffn_r_in_b, L1_ffn_r_o1_w, L1_ffn_r_o1_b, L1_ffn_r_o2_w, L1_ffn_r_o2_b, L1_ffn_r_o3_w, L1_ffn_r_o3_b, L1_ffn_lra_down, L1_ffn_lra_up)
    return h

_drawn_inputs = setup_inputs


def setup_inputs(seed=0):
    import zlib

    import numpy as np

    out = dict(_drawn_inputs(seed))
    spreads = {'L0_tok_b': (0.0, 0.1),
     'L1_attn_b_out': (0.0, 0.1),
     'L1_ffn_bq': (0.0, 0.8),
     'L1_ffn_bk': (0.0, 0.8),
     'L1_ffn_bv': (0.0, 0.679),
     'L1_ffn_bo': (0.0, 0.1),
     'L1_ffn_ln1_g': (1.0, 0.6),
     'L1_ffn_ln1_b': (0.0, 0.8),
     'L1_ffn_ln2_g': (1.0, 0.6),
     'L1_ffn_ln2_b': (0.0, 0.8),
     'L1_ffn_fc1_b': (0.0, 0.586),
     'L1_ffn_fc2_b': (0.0, 0.1),
     'L1_ffn_r_ln_g': (1.0, 0.2),
     'L1_ffn_r_ln_b': (0.0, 0.1),
     'L1_ffn_r_in_b': (0.0, 0.1),
     'L1_ffn_r_o1_b': (0.0, 0.1),
     'L1_ffn_r_o2_b': (0.0, 0.1)}
    factors = {'L0_tok_pos_emb': 4.906,
     'L0_attn_proj_l_b': 8.0,
     'L1_attn_scale': 3.157,
     'L1_ffn_wq': 8.0,
     'L1_ffn_wk': 8.0,
     'L1_ffn_wv': 4.001,
     'L1_ffn_wo': 3.222}
    for name, (base, spread) in spreads.items():
        noise = np.random.default_rng([zlib.crc32(name.encode()), seed]).standard_normal(out[name].shape)
        drawn = base * np.exp(spread * noise) if base else spread * noise
        out[name] = jnp.asarray(drawn.astype(out[name].dtype))
    for name, factor in factors.items():
        out[name] = (out[name] * factor).astype(out[name].dtype)
    return out
```

```python
from contextlib import ExitStack

import numpy as np
import concourse.bass as bass
from concourse import mybir

F32 = mybir.dt.float32
BF16 = mybir.dt.bfloat16
U32 = mybir.dt.uint32
ALU = mybir.AluOpType
ACT = mybir.ActivationFunctionType
AX = mybir.AxisListType

SEQS, TOK, IMG_TOK, DIM = 64, 144, 16, 192
TXT_TOK = TOK - IMG_TOK
GB = 4
GROUPS = SEQS // GB
GT = GB * TOK
HT = 96
NT = GT // HT
CH = 2 * TOK
T72 = TOK // 2
N72 = GT // T72
HEADS = 12
D0 = DIM // HEADS
D1 = 64
RN = 9
RP = RN * HEADS
PACK = 4
PN = RN * PACK
PACKS = TOK // PN
EXPERTS, FF = 8, 768
FT = FF // 128
CAP = 180
SLOTS = EXPERTS * CAP
SLOT_P = 120
RHD, RANK = 128, 64
EPS = 1e-5
STEPS = 6 * GB
MASKED = -1.0e30
E_TILES = SEQS * IMG_TOK // 128


def psum_units():
    u = [("LN", 0, 0), ("LN", 0, 1)]
    u += [("V0", 0), ("V0", 1)] + [("Q0", 0), ("Q0", 1), ("K0", 0), ("K0", 1)]
    for t in range(GB * PACKS + 4):
        if t < GB * PACKS:
            u.append(("S0", t))
        if t >= 6 and t % 4 == 2:
            u += [("Y0", (t - 6) // 4), ("Z0", (t - 6) // 4)]
        if 2 <= t < GB * PACKS + 2:
            u.append(("M0", t - 2))
        if t >= 7 and t % 4 == 3:
            u.append(("OT0", (t - 7) // 4))
    u += [("P0", 0), ("P0", 1)]
    u += [("LN", 1, 0), ("LN", 1, 1), ("LG",), ("CT",)]
    u += [("XT", i) for i in range(3)]
    for e in range(EXPERTS + 1):
        if e < EXPERTS:
            u += [("H", e, 0), ("H", e, 1)]
        if e >= 1:
            u.append(("EO", e - 1))
    u += [("LN", 2, 0), ("LN", 2, 1)]
    for s in range(STEPS + 3):
        if s % 4 == 0 and s < STEPS:
            u += [("Q1", s // 4), ("K1", s // 4), ("V1", s // 4)]
        if s < STEPS:
            u.append(("S1", s))
        if 2 <= s < STEPS + 2:
            u.append(("T1", s - 2))
        if s >= 3:
            u.append(("O1", s - 3))
        if s >= 6 and s % 4 == 2:
            u.append(("OT1", (s - 6) // 4))
    u += [("P1", 0), ("P1", 1), ("LN", 4, 0), ("LN", 4, 1)]
    u += [("E1",), ("Q2", 0), ("Q2", 1), ("GC",), ("V2", 0), ("H1",), ("V2", 1), ("H2",), ("K2", 0), ("K2", 1), ("RL",)]
    for t in range(GB * PACKS + 4):
        if t < GB * PACKS:
            u.append(("S2", t))
        if t >= 6 and t % 4 == 2:
            u.append(("Y2", (t - 6) // 4))
        if 2 <= t < GB * PACKS + 2:
            u.append(("M2", t - 2))
        if t >= 7 and t % 4 == 3:
            u.append(("OT2", (t - 7) // 4))
    u += [("P2", 0), ("P2", 1), ("LN", 5, 0), ("LN", 5, 1)]
    u += [("F1", i) for i in range(FT)] + [("F2", 0), ("F2", 1)]
    u += [("OUT", 0), ("OUT", 1), ("DN", 0), ("DN", 1), ("DT", 0), ("DT", 1), ("UP", 0), ("UP", 1)]
    return u


UNITS = psum_units()
UNIT = {key: i for i, key in enumerate(UNITS)}
SLOT_USES = [len(range(s, len(UNITS), 4)) for s in range(4)]
VEC_STEPS = 121
W_L0 = 16 * 36
W_FFN = 16 * 21
W_MOE = 16 * (1 + 2 * EXPERTS)
HALF = NT // 2
TILES_OF = [range(0, HALF), range(HALF, NT)]
TS = 256


def program(nc, a, out):
    with ExitStack() as ctx:
        def sb(name, shape, dt=F32):
            return ctx.enter_context(nc.sbuf_tensor(name, shape, dt))

        def sem(name):
            return ctx.enter_context(nc.semaphore(name))

        img_rows = nc.dram_tensor("img_rows", (SEQS, IMG_TOK, DIM), F32, kind="Internal").ap()
        expert_rows = nc.dram_tensor("expert_rows", (SLOTS, DIM), F32, kind="Internal").ap()
        result_rows = nc.dram_tensor("result_rows", (SLOTS + 1, DIM), F32, kind="Internal").ap()

        moe_wi = sb("moe_wi", [HT, 2, EXPERTS, FF])
        moe_wo = sb("moe_wo", [128, EXPERTS, FT, DIM])
        router_w = sb("router_w", [HT, 2, EXPERTS])
        qkv0_w = sb("qkv0_w", [HT, 2, 3 * DIM])
        proj0_w = sb("proj0_w", [HT + 1, 2, DIM])
        mix_in = sb("mix_in", [HT, 2, HEADS])
        mix_out = sb("mix_out", [RP + 1, RP])
        coef_y = sb("coef_y", [T72, HEADS])
        coef_z = sb("coef_z", [T72, HEADS])
        qkv1_w = sb("qkv1_w", [HT, 2, 3, HEADS * D1])
        scale1 = sb("scale1", [128, 6])
        proj1_w = sb("proj1_w", [128, 6, DIM])
        bias1 = sb("bias1", [HT, DIM])
        wq2 = sb("wq2", [HT, 2, DIM])
        wk2 = sb("wk2", [HT, 2, DIM])
        bq2 = sb("bq2", [HT, 2])
        bk2 = sb("bk2", [HT, 2])
        own_head = sb("own_head", [HT, 2, HEADS])
        wv2 = sb("wv2", [HT, 2, DIM])
        bv2 = sb("bv2", [T72, DIM])
        wo2 = sb("wo2", [HT + 1, 2, DIM])
        ln_gb = sb("ln_gb", [HT, 2, 6])
        fc1_w = sb("fc1_w", [HT, 2, FF])
        fc1_b = sb("fc1_b", [128, FT])
        fc2_w = sb("fc2_w", [128, FT, DIM])
        fc2_b = sb("fc2_b", [HT, DIM])
        r_in_w = sb("r_in_w", [HT, 2, RHD])
        r_o1_w = sb("r_o1_w", [RHD, 2, RHD])
        r_o2_w = sb("r_o2_w", [RHD, RHD // 2])
        r_o3_w = sb("r_o3_w", [RHD // 2 + 1, 4])
        r_b = sb("r_b", [RHD, 3])
        lra_dn = sb("lra_dn", [HT, 2, DIM])
        lra_up = sb("lra_up", [HT, 2, DIM])

        ident = sb("ident", [128, 128])
        ident_bf = sb("ident_bf", [T72, T72], BF16)
        diag_bf = sb("diag_bf", [T72, 2, TOK], BF16)
        before_bf = sb("before_bf", [HT, HT], BF16)
        ones_bf = sb("ones_bf", [HT, HT], BF16)
        first_e = sb("first_e", [HT, EXPERTS])
        base_e = sb("base_e", [HT, EXPERTS])
        reserved = sb("reserved", [HT, NT])
        eps_pow = sb("eps_pow", [HT, NT])

        h = sb("h", [HT, NT, DIM])
        AR = 15456
        arena = sb("arena", [128, AR])

        def view(at, rows, *shape):
            n = int(np.prod(shape))
            v = arena[0:rows, at:at + n]
            names = "abcd"[:len(shape)]
            if len(shape) == 1:
                return v
            return v.rearrange(f"p ({' '.join(names)}) -> p {' '.join(names)}",
                               **{c: s for c, s in zip(names, shape)})

        R0, R1, R2, R3, R4, R5, R6, R7 = 0, 1152, 2304, 3456, 4608, 5760, 8352, 10080
        tm_x = view(R0, HT, NT, DIM)
        fm_x = view(R1, HT, 2, GT)
        tm_z = view(R2, HT, NT, DIM)
        fm_o = view(R3, HT + 1, 2, GT)
        k0 = view(R4, HT + 1, 2, GT)
        qg0 = [view(R5 + 864 * i, HT + 1, 2, PN * HEADS) for i in range(3)]
        probs0 = [view(R6 + 576 * i, RP + 1, PACK, TOK) for i in range(3)]
        q0 = view(R7, HT, 2, GT)
        v0 = view(R7 + 1152, T72, N72, DIM)
        y0, t0, u0, o0 = [view(R7 + 2688 + 384 * i, T72, 2, DIM) for i in range(4)]
        at0 = view(R0, T72, 2, HEADS, TOK)
        xe_tok = view(R0, SLOT_P, SLOTS // SLOT_P, DIM)
        xe = view(R3, HT, 2, SLOTS)
        eo = view(R3 + 2880, CAP // 2, 2 * EXPERTS, DIM)
        hid = [view(R7 + 1080 * i, 128, FT, CAP) for i in range(2)]
        back = view(R0, HT, NT, 2 * DIM)
        pt1 = [view(R0 + 576 * i, T72, 2, 2, TOK) for i in range(2)]
        q1 = [view(R2, 128, GT), view(R7 + 3456, 128, GT)]
        k1 = [view(R2 + 576, 128, GT), view(R7 + 4032, 128, GT)]
        v1 = [view(R5 + 1040 * i, T72, N72, 2, D1 + 1) for i in range(2)]
        p12 = [view(R6 + 576 * i, T72, 2, 2, TOK) for i in range(3)]
        o1 = [view(R3 + 1024 * i, T72, N72, 2 * D1) for i in range(2)]
        ot1 = view(R7, 128, 6, GT)
        fm_r = view(R4, HT, 2, GT)
        e_t = view(R7, RHD, GT)
        h1_t = view(R7 + 576, RHD, GT)
        h2_t = view(R7 + 1152, RHD // 2 + 1, GT)
        q2 = view(R2, HT, 2, GT)
        k2 = view(R4, HT, 2, GT)
        v2 = view(R7 + 3456, T72, N72, DIM)
        at2 = view(R7, T72, 2, HEADS, TOK)
        o2 = [view(R1 + 384 * i, T72, 2, DIM) for i in range(2)]
        ff = view(R7, 128, FT, GT)
        emb_w = view(R7, 128, 6, DIM)
        emb_x = [view(R0 + 768 * i, 128, 6, 128) for i in range(2)]
        emb_xt = view(R2, 128, 6, 128)
        emb_bias = view(1536, 128, DIM)
        emb_b = view(1536 + 192, 128, DIM)
        emb_out = [view(1920 + 192 * i, 128, DIM) for i in range(2)]
        zero_rows = view(R7 + 1152, SLOT_P, SLOTS // SLOT_P, DIM)
        ones_row = view(R7 + 3456, 1, PACK * TOK)

        stats = sb("stats", [HT, NT, 6])
        mean = sb("mean", [HT, NT])
        idle = sb("idle", [HT, NT])
        idle2 = sb("idle2", [HT, NT])
        mean2 = sb("mean2", [HT, NT])
        diff = sb("diff", [HT, NT])
        diff2 = sb("diff2", [HT, NT])
        var = sb("var", [HT, NT])
        var2 = sb("var2", [HT, NT])
        var_eps = sb("var_eps", [HT, NT])
        rstd = sb("rstd", [HT, NT])
        negmax = [sb(f"negmax{i}", [RP, 4]) for i in range(3)]
        rowsum = [sb(f"rowsum{i}", [RP, 4]) for i in range(3)]
        rinv = [sb(f"rinv{i}", [RP, 4]) for i in range(3)]
        o_inv = [sb(f"o_inv{i}", [T72, 2, 2]) for i in range(2)]
        lg = sb("lg", [HT, NT, EXPERTS])
        lg2 = sb("lg2", [HT, NT, EXPERTS])
        lgm = sb("lgm", [HT, NT])
        lgs = sb("lgs", [HT, NT])
        gate = sb("gate", [HT, NT, 2])
        key = sb("key", [HT, NT])
        picked = sb("picked", [HT, NT, 2, EXPERTS])
        picked_bf = sb("picked_bf", [HT, NT, 2 * EXPERTS], BF16)
        place = sb("place", [HT, NT, 2, EXPERTS])
        pos = sb("pos", [HT, NT, 2])
        row_of = sb("row_of", [HT, NT, 2])
        row_idx = sb("row_idx", [HT, NT, 2], U32)
        g_mean = sb("g_mean", [RHD, GB])
        g_bias = sb("g_bias", [RHD, GB])
        rl = sb("rl", [HT, NT, 2, 2])
        bits = sb("bits", [HT, NT, 2])
        nbits = sb("nbits", [HT, NT, 2])
        sel = sb("sel", [HT, NT, 3])

        ps_flat = [ctx.enter_context(nc.psum_tensor(f"ps{i}", [128, 1024], F32)) for i in range(4)]
        ps = [v[:, :].rearrange("p (a n) -> p a n", a=2) for v in ps_flat]

        psum_filled = sem("psum_filled")
        psum_emptied = [sem(f"psum_emptied{i}") for i in range(4)]
        w_tok, w_l0, w_moe, w_l1, w_ffn = (sem(n) for n in ("w_tok", "w_l0", "w_moe", "w_l1", "w_ffn"))
        mix_zeroed = sem("mix_zeroed")
        ones_set = sem("ones_set")
        mix_ready = sem("mix_ready")
        vec_setup = sem("vec_setup")
        pool_setup = sem("pool_setup")
        patches_in = [sem(f"patches_in{i}") for i in range(2)]
        emb_filled = sem("emb_filled")
        emb_emptied = sem("emb_emptied")
        emb_stored = [sem(f"emb_stored{i}") for i in range(2)]
        zeros_stored = sem("zeros_stored")
        h_loaded = sem("h_loaded")
        out_stored = sem("out_stored")
        var_ready = sem("var_ready")
        rstd_ready = sem("rstd_ready")
        ln_ready = sem("ln_ready")
        vec_step = sem("vec_step")
        pool_step = sem("pool_step")
        qg_ready = sem("qg_ready")
        max_ready = [sem(f"max_ready{i}") for i in range(3)]
        probs_ready = [sem(f"probs_ready{i}") for i in range(2)]
        qg2_ready = sem("qg2_ready")
        z_scaled = sem("z_scaled")
        o0_ready = sem("o0_ready")
        rows_chosen = sem("rows_chosen")
        picked_ready = sem("picked_ready")
        logit_exp = sem("logit_exp")
        scattered = sem("scattered")
        experts_in = sem("experts_in")
        results_out = sem("results_out")
        gathered = [sem(f"gathered{i}") for i in range(2)]
        bias1_added = sem("bias1_added")
        g_mean_ready = sem("g_mean_ready")
        h2_ones = sem("h2_ones")
        bits_ready = sem("bits_ready")
        ffn_base = sem("ffn_base")
        out_added = sem("out_added")

        def slot(key_):
            return ps[UNIT[key_] % 4]

        def tiles(key_, n=HALF):
            return ps_flat[UNIT[key_] % 4][0:HT, 0:n * TS].rearrange("p (j d) -> p j d", d=TS)[:, :, 0:DIM]

        def filled(eng, g, key_):
            eng.wait_ge(psum_filled, g * len(UNITS) + (UNIT[key_] + 1))

        def emptied(eng, g, *keys, but=None):
            for s in range(4):
                n = max((UNIT[k] // 4 + 1 for k in keys if UNIT[k] % 4 == s), default=0)
                if n and s != but:
                    eng.wait_ge(psum_emptied[s], g * SLOT_USES[s] + (n + 1))

        def to_empty(key_):
            return psum_emptied[UNIT[key_] % 4]

        def combine0(g, pool, b):
            emptied(pool, g, ("Y0", b))
            nc.gpsimd.tensor_tensor(u0.rearrange("p a (g d) -> p a g d", d=D0), y0.rearrange("p a (g d) -> p a g d", d=D0),
                                    coef_y[:].unsqueeze(1).unsqueeze(3).to_broadcast([T72, 2, HEADS, D0]), ALU.mult)\
                .then_inc(z_scaled, 1)
            emptied(pool, g, ("Z0", b))
            pool.wait_ge(z_scaled, g * GB + (b + 1))
            nc.gpsimd.tensor_tensor(o0, t0, u0, ALU.add).then_inc(o0_ready, 1)

        def mixed_out(g, eng, copy, which, t):
            p = t % PACKS
            for mh in range(2):
                if mh == 0:
                    filled(eng, g, (f"M{which}", t))
                ins = copy((at0 if which == 0 else at2)[:, mh, :, p * PN:(p + 1) * PN].rearrange("p g n -> p n g"),
                           slot((f"M{which}", t))[0:T72, mh, 0:PN * HEADS].rearrange("p (n g) -> p n g", g=HEADS))
            ins.then_inc(to_empty((f"M{which}", t)), 1)

        def exp_tiles(g, act, which, t):
            act.wait_ge(max_ready[which], g * GB * PACKS + (t + 1))
            s = slot((f"S{which}", t))
            for i in range(PACK):
                ins = nc.scalar.activation(probs0[t % 3][0:RP, i, :], s[0:RP, i // 2, (i % 2) * TOK:(i % 2 + 1) * TOK],
                                           ACT.Exp, bias=negmax[t % 3][:, i:i + 1], accum_out=rowsum[t % 3][:, i:i + 1])
            ins.then_inc(to_empty((f"S{which}", t)), 1)

        def exp_pair(g, act, which, s):
            act.wait_ge(max_ready[which], g * STEPS + (s + 1))
            name = "S1"
            for i in range(4):
                ins = nc.scalar.activation(p12[s % 3][:, i // 2, i % 2, :],
                                           slot((name, s))[0:T72, i // 2, (i % 2) * TOK:(i % 2 + 1) * TOK], ACT.Exp,
                                           bias=negmax[s % 3][0:T72, i:i + 1])
            ins.then_inc(to_empty((name, s)), 1)

        block = ctx.enter_context(nc.Block())

        @block.sync
        def _(sp):
            sp.dma_start(emb_w, a["tok_w"]).then_inc(w_tok, 16)
            x_v = a["x"].rearrange("b (hp ph) (wp pc) -> (b hp) wp ph pc", ph=16, wp=4)
            for t in range(2):
                for wp in range(4):
                    sp.dma_start(emb_x[t][wp * 32:wp * 32 + 32].rearrange("p a b -> p (a b)").rearrange("p (ph pc) -> p ph pc", ph=16),
                                 x_v[t * 32:t * 32 + 32, wp]).then_inc(patches_in[t], 16)
            for wp in range(4):
                sp.dma_start(emb_bias[wp * 32:wp * 32 + 32], a["pos"][:, wp]).then_inc(w_tok, 16)
            sp.dma_start(emb_b, a["tok_b"].to_broadcast([128, DIM])).then_inc(w_tok, 16)
            for j in range(6):
                for hf in range(2):
                    sp.dma_start(mix_in[16 * j:16 * j + 16, hf, :],
                                 a["proj_l_w"][6 * hf + j:6 * hf + j + 1, :].to_broadcast([16, HEADS])).then_inc(w_l0, 16)
            sp.dma_start(qkv0_w[:], a["qkv0_w"]).then_inc(w_l0, 16)
            sp.dma_start(proj0_w[0:HT], a["proj0_w"]).then_inc(w_l0, 16)
            sp.dma_start(proj0_w[HT:HT + 1, 0, :], a["proj0_b"]).then_inc(w_l0, 16)
            sp.dma_start(coef_y[:], a["lamb"].to_broadcast([T72, HEADS])).then_inc(w_l0, 16)
            sp.dma_start(coef_z[:], a["lamb"].to_broadcast([T72, HEADS])).then_inc(w_l0, 16)
            for i in range(3):
                for hf in range(2):
                    sp.dma_start(qg0[i][HT:HT + 1, hf, :].rearrange("p (n g) -> p n g", g=HEADS),
                                 a["proj_l_b"].rearrange("o (n g) -> o n g", n=1).to_broadcast([1, PN, HEADS])).then_inc(w_l0, 16)
            sp.wait_ge(mix_zeroed, 1)
            for n in range(RN):
                sp.dma_start(mix_out[n * HEADS:(n + 1) * HEADS, n * HEADS:(n + 1) * HEADS], a["proj_w_w"]).then_inc(w_l0, 16)
            sp.dma_start(mix_out[RP:RP + 1, :].rearrange("p (n g) -> p n g", g=HEADS),
                         a["proj_w_b"].rearrange("o (n g) -> o n g", n=1).to_broadcast([1, RN, HEADS])).then_inc(w_l0, 16)
            sp.wait_ge(ones_set, 1)
            for i in range(3):
                sp.dma_start(probs0[i][RP:RP + 1].rearrange("p a b -> p (a b)"),
                             ones_row).then_inc(w_l0, 16)
            with sp.Fori(1, E_TILES // 2) as i:
                for t in range(2):
                    sp.wait_ge(emb_filled, i * 4 + (2 * t - 3))
                    for wp in range(4):
                        sp.dma_start(emb_x[t][wp * 32:wp * 32 + 32].rearrange("p a b -> p (a b)").rearrange("p (ph pc) -> p ph pc", ph=16),
                                     x_v[bass.ds(i * 64 + t * 32, 32), wp]).then_inc(patches_in[t], 16)
            out_v = out.rearrange("(g j p) d -> g p j d", g=GROUPS, p=HT)
            img_v = img_rows.rearrange("(g c b) t d -> g b t c d", g=GROUPS, b=2)
            txt_v = a["txt"].rearrange("(g c b) t d -> g b t c d", g=GROUPS, b=2)
            exp_v = expert_rows.rearrange("(c p) d -> p c d", p=SLOT_P)
            for t in range(2):
                sp.wait_ge(emb_stored[t], 16 * 4 * E_TILES // 2)

            def load(g):
                hv = h[:].rearrange("p (c j) d -> p c j d", c=2)
                sp.dma_start(hv[0:16, :, 0], img_v[g, 0]).then_inc(h_loaded, 16)
                sp.dma_start(hv[16:96, :, 0], txt_v[g, 0, 0:80]).then_inc(h_loaded, 16)
                sp.dma_start(hv[0:48, :, 1], txt_v[g, 0, 80:128]).then_inc(h_loaded, 16)
                sp.dma_start(hv[48:64, :, 1], img_v[g, 1]).then_inc(h_loaded, 16)
                sp.dma_start(hv[64:96, :, 1], txt_v[g, 1, 0:32]).then_inc(h_loaded, 16)
                sp.dma_start(hv[0:96, :, 2], txt_v[g, 1, 32:128]).then_inc(h_loaded, 16)

            def group(g):
                sp.wait_ge(scattered, g * 192 + 192)
                filled(sp, g, ("LN", 1, 1))
                sp.dma_start(xe_tok, exp_v).then_inc(experts_in, 16)
                for e in range(EXPERTS):
                    emptied(sp, g, ("EO", e))
                    sp.dma_start(result_rows[e * CAP:(e + 1) * CAP].rearrange("(c p) d -> p c d", c=2),
                                 eo[:, 2 * e:2 * e + 2]).then_inc(results_out, 16)
                emptied(sp, g, ("UP", 0), ("UP", 1))
                sp.dma_start(out_v[g], h[:]).then_inc(out_stored, 16)

            load(0)
            with sp.Fori(0, GROUPS - 1) as g:
                group(g)
                sp.wait_ge(out_stored, g * 16 + 16)
                load(g + 1)
            group(GROUPS - 1)
            sp.wait_ge(out_stored, GROUPS * 16)
            sp.wait_ge(results_out, GROUPS * EXPERTS * 16)

        @block.gpsimd
        def _(pool):
            done = [0]

            def link(ins):
                ins.then_inc(pool_setup, 1)
                done[0] += 1
                pool.wait_ge(pool_setup, done[0])

            nc.gpsimd.memset(mix_out[:], 0.0).then_inc(mix_zeroed, 1)
            nc.gpsimd.memset(own_head[:], float(D0) ** -0.5)
            nc.gpsimd.memset(ident[:], 0.0)
            nc.gpsimd.memset(ident_bf[:], 0.0)
            nc.gpsimd.memset(diag_bf[:], 0.0)
            nc.gpsimd.memset(ones_bf[:], 1.0)
            nc.gpsimd.memset(before_bf[:], 1.0)
            nc.gpsimd.memset(reserved[:], 0.0)
            nc.gpsimd.memset(eps_pow[:], -0.5)
            link(nc.gpsimd.memset(zero_rows, 0.0))
            nc.gpsimd.affine_select(out=ident[:], in_=ident[:], compare_op=ALU.not_equal, fill=1.0, base=0,
                                    pattern=[[-1, 128]], channel_multiplier=1)
            nc.gpsimd.affine_select(out=ident_bf[:], in_=ident_bf[:], compare_op=ALU.not_equal, fill=1.0, base=0,
                                    pattern=[[-1, T72]], channel_multiplier=1)
            nc.gpsimd.affine_select(out=diag_bf[:], in_=diag_bf[:], compare_op=ALU.not_equal, fill=MASKED, base=0,
                                    pattern=[[T72, 2], [-1, TOK]], channel_multiplier=1)
            nc.gpsimd.affine_select(out=before_bf[:], in_=before_bf[:], compare_op=ALU.is_gt, fill=0.0, base=0,
                                    pattern=[[1, HT]], channel_multiplier=-1)
            oh = own_head[:]
            nc.gpsimd.affine_select(out=oh, in_=oh, compare_op=ALU.is_ge, fill=0.0, base=0,
                                    pattern=[[HT, 2], [-D0, HEADS]], channel_multiplier=1)
            rv = reserved[:].rearrange("p (c j) -> p c j", c=2)
            nc.gpsimd.affine_select(out=rv[:, :, 0:2], in_=rv[:, :, 0:2], compare_op=ALU.not_equal, fill=1.0, base=0,
                                    pattern=[[0, 2], [-48, 2]], channel_multiplier=1)
            nc.gpsimd.iota(first_e[:], pattern=[[-1, EXPERTS]], base=EXPERTS, channel_multiplier=0,
                           allow_small_or_imprecise_dtypes=True)
            link(nc.gpsimd.iota(base_e[:], pattern=[[CAP, EXPERTS]], base=0, channel_multiplier=0,
                                allow_small_or_imprecise_dtypes=True))
            nc.gpsimd.affine_select(out=oh, in_=oh, compare_op=ALU.is_ge, fill=0.0, base=D0 - 1,
                                    pattern=[[-HT, 2], [D0, HEADS]], channel_multiplier=-1)
            pool.dma_start(expert_rows.rearrange("(c p) d -> p c d", p=SLOT_P), zero_rows).then_inc(zeros_stored, 16)
            pool.dma_start(result_rows[SLOTS:SLOTS + 1], zero_rows[0:1, 0, :]).then_inc(zeros_stored, 16)
            pool.wait_ge(zeros_stored, 32)
            nc.gpsimd.memset(fm_o[HT:HT + 1], 1.0)
            link(nc.gpsimd.memset(k0[HT:HT + 1], 1.0))
            pool.dma_start(router_w[:], a["router_w"]).then_inc(w_moe, 16)
            for e in range(EXPERTS):
                pool.dma_start(moe_wi[:, :, e], a["moe_wi"][e]).then_inc(w_moe, 16)
                pool.dma_start(moe_wo[:, e], a["moe_wo"][e]).then_inc(w_moe, 16)
            pool.dma_start(qkv1_w[:], a["qkv1_w"]).then_inc(w_l1, 16)
            for j in range(2):
                pool.dma_start(scale1[64 * j:64 * j + 64], a["scale1"][j:j + 1].to_broadcast([64, 6])).then_inc(w_l1, 16)
            pool.dma_start(proj1_w[:], a["proj1_w"]).then_inc(w_l1, 16)
            pool.dma_start(bias1[:], a["bias1"].to_broadcast([HT, DIM])).then_inc(w_l1, 16)
            for t_, n in ((wq2[:], "wq2"), (wk2[:], "wk2"), (bq2[:], "bq2"), (bk2[:], "bk2"), (wv2[:], "wv2"), (wo2[0:HT], "wo2"), (wo2[HT:HT + 1, 0, :], "bo2"), (ln_gb[:], "ln_gb"),
                          (fc1_w[:], "fc1_w"), (fc1_b[:], "fc1_b"), (fc2_w[:], "fc2_w"), (r_in_w[:], "r_in_w"),
                          (r_o1_w[:], "r_o1_w"), (r_o2_w[:], "r_o2_w"), (r_o3_w[:], "r_o3_w"),
                          (r_b[:, 0:2], "r_b"), (r_b[0:RHD // 2, 2:3], "r_o2_b"), (lra_dn[:], "lra_dn"), (lra_up[:], "lra_up")):
                pool.dma_start(t_, a[n]).then_inc(w_ffn, 16)
            pool.dma_start(bv2[:], a["bv2"].to_broadcast([T72, DIM])).then_inc(w_ffn, 16)
            pool.dma_start(fc2_b[:], a["fc2_b"].to_broadcast([HT, DIM])).then_inc(w_ffn, 16)

            last_slot = pool.to_reg(SLOTS - 1)
            zero_row = pool.to_reg(SLOTS)
            with pool.Fori(0, GROUPS) as g:
                n_ln = [0]

                def rsqrt():
                    for part in range(2):
                        n_ln[0] += 1
                        pool.wait_ge(var_ready, g * 12 + n_ln[0])
                        c = slice(HALF * part, HALF * part + HALF)
                        nc.gpsimd.tensor_tensor(rstd[:, c], var_eps[:, c], eps_pow[:, c], ALU.pow).then_inc(rstd_ready, 1)

                def expand(which, t):
                    if t >= 3:
                        filled(pool, g, (f"S{which}", t - 3))
                    elif t == 0:
                        emptied(pool, g, (f"Q{which}", 0), (f"Q{which}", 1))
                    c0 = t * PN
                    for hf in range(2):
                        ins = nc.gpsimd.tensor_tensor(
                            qg0[t % 3][0:HT, hf, :].rearrange("p (n g) -> p n g", g=HEADS),
                            (q0 if which == 0 else q2)[:, hf, c0:c0 + PN].unsqueeze(2).to_broadcast([HT, PN, HEADS]),
                            (mix_in if which == 0 else own_head)[:, hf, :].unsqueeze(1).to_broadcast([HT, PN, HEADS]), ALU.mult)
                    ins.then_inc(qg_ready if which == 0 else qg2_ready, 1)

                rsqrt()
                pool.wait_ge(mix_ready, 1)
                for t in range(GB * PACKS + 4):
                    if t < GB * PACKS:
                        expand(0, t)
                    if t >= 7 and t % 4 == 3:
                        combine0(g, pool, (t - 7) // 4)
                rsqrt()
                pool.wait_ge(rows_chosen, g + 1)
                nc.gpsimd.tensor_tensor(idle[:], eps_pow[:], eps_pow[:], ALU.add)
                for j in range(NT):
                    for k in range(2):
                        pool.indirect_dma_start(
                            expert_rows[:, :], bass.IndirectOffsetOnAxis(ap=row_idx[:, j, k:k + 1], axis=0),
                            tm_x[:, j, :], None, bounds_check=last_slot, oob_is_err=False).then_inc(scattered, 16)
                pool.wait_ge(results_out, g * EXPERTS * 16 + EXPERTS * 16)
                nc.gpsimd.tensor_tensor(idle2[:], eps_pow[:], eps_pow[:], ALU.add)
                for j in range(NT):
                    for k in range(2):
                        pool.indirect_dma_start(
                            back[:, j, k * DIM:(k + 1) * DIM], None,
                            result_rows[:, :], bass.IndirectOffsetOnAxis(ap=row_idx[:, j, k:k + 1], axis=0),
                            bounds_check=zero_row, oob_is_err=False).then_inc(gathered[j // HALF], 16)
                rsqrt()
                pool.wait_ge(ln_ready, g * 12 + 6)
                pool.wait_ge(w_l1, 80)
                nc.gpsimd.tensor_tensor(h[:], h[:], bias1[:].unsqueeze(1).to_broadcast([HT, NT, DIM]), ALU.add)\
                    .then_inc(bias1_added, 1)
                rsqrt()
                rsqrt()
                for t in range(GB * PACKS):
                    expand(2, t)
                rsqrt()
                filled(pool, g, ("LN", 5, 1))
                pool.wait_ge(bits_ready, g + 1)
                nc.gpsimd.tensor_tensor(tm_x, bits[:, :, 1:2].to_broadcast([HT, NT, DIM]),
                                        fc2_b[:].unsqueeze(1).to_broadcast([HT, NT, DIM]), ALU.mult).then_inc(pool_step, 1)
                pool.wait_ge(pool_step, g + 1)
                nc.gpsimd.tensor_tensor(tm_x, tm_x, tm_z, ALU.add).then_inc(ffn_base, 1)
                emptied(pool, g, ("F2", 1))
                emptied(pool, g, ("F2", 0))
                nc.gpsimd.tensor_tensor(h[:], h[:], tm_z, ALU.add).then_inc(out_added, 1)

        @block.scalar
        def _(act):
            img_t = img_rows.rearrange("b (hp wp) d -> (b hp) wp d", wp=4)
            with act.Fori(0, E_TILES // 2) as i:
                for t in range(2):
                    act.wait_ge(emb_emptied, i * 4 + (2 * t + 2))
                    for wp in range(4):
                        act.dma_start(img_t[bass.ds(i * 64 + t * 32, 32), wp], emb_out[t][wp * 32:wp * 32 + 32])\
                            .then_inc(emb_stored[t], 16)
            with act.Fori(0, GROUPS) as g:
                def copy(key_, out_, in_):
                    filled(act, g, key_)
                    nc.scalar.copy(out_, in_).then_inc(to_empty(key_), 1)

                c288 = lambda key_, m: slot(key_)[0:m, :, 0:CH]
                fm = lambda buf, hf: buf[0:HT, hf].rearrange("p (c n) -> p c n", c=2)
                def chunk(key_, c):
                    copy(key_, fm_x[:, :, c * CH:(c + 1) * CH], slot(key_)[0:HT, :, 0:CH])

                def mixed(which):
                    for t in range(GB * PACKS + 2):
                        if t < GB * PACKS:
                            exp_tiles(g, act, which, t)
                        if t >= 2 and t % 2 == 0:
                            mixed_out(g, act, nc.scalar.copy, which, t - 2)

                chunk(("LN", 0, 1), 1)
                copy(("V0", 1), v0[:, 4:8].rearrange("p (c j) d -> p c (j d)", c=2),
                     slot(("V0", 1))[0:T72, :, 0:2 * DIM])
                copy(("Q0", 1), fm(q0, 1), c288(("Q0", 1), HT))
                copy(("K0", 1), fm(k0, 1), c288(("K0", 1), HT))
                mixed(0)
                chunk(("LN", 1, 1), 1)
                emptied(act, g, ("LG",))
                nc.scalar.activation(lg2[:], lg[:], ACT.Exp).then_inc(logit_exp, 1)
                copy(("XT", 1), xe[:, :, 480:960], slot(("XT", 1))[0:HT, :, 0:480])
                for e in range(EXPERTS):
                    filled(act, g, ("H", e, 0))
                    nc.scalar.activation(hid[e % 2][:, 0:4].rearrange("p (c j) n -> p c (j n)", c=2),
                                         slot(("H", e, 0))[:, :, 0:2 * CAP], ACT.Relu).then_inc(to_empty(("H", e, 0)), 1)
                chunk(("LN", 2, 1), 1)
                for s in range(STEPS + 3):
                    if s % 4 == 0 and s < STEPS:
                        hp = s // 4
                        copy(("K1", hp), k1[hp % 2].rearrange("p (c n) -> p c n", c=2), c288(("K1", hp), 128))
                    if s < STEPS:
                        exp_pair(g, act, 1, s)
                    if 2 <= s < STEPS + 2 and s % 2 == 0:
                        copy(("T1", s - 2), pt1[s % 2].rearrange("p a b n -> p a (b n)"), c288(("T1", s - 2), T72))
                    if s >= 6 and s % 4 == 2:
                        hp = (s - 6) // 4
                        copy(("OT1", hp), ot1[:, hp].rearrange("p (c n) -> p c n", c=2), c288(("OT1", hp), 128))
                def affine(key_, dst, c, gain, last):
                    for hf in range(2):
                        ins = nc.scalar.activation(dst[0:HT, hf, c * CH:(c + 1) * CH], slot(key_)[0:HT, hf, 0:CH], ACT.Identity,
                                                   bias=ln_gb[:, hf, gain + 1:gain + 2], scale=ln_gb[:, hf, gain:gain + 1])
                    if last:
                        ins.then_inc(to_empty(key_), 1)

                filled(act, g, ("LN", 4, 1))
                affine(("LN", 4, 1), fm_r, 1, 4, False)
                affine(("LN", 4, 1), fm_x, 1, 0, True)
                filled(act, g, ("E1",))
                nc.scalar.activation(e_t.rearrange("p (c n) -> p c n", c=2), c288(("E1",), RHD), ACT.Gelu,
                                     bias=r_b[:, 0:1]).then_inc(to_empty(("E1",)), 1)
                filled(act, g, ("H1",))
                emptied(act, g, ("GC",))
                for b in range(GB):
                    ins = nc.scalar.activation(h1_t[:, b * TOK:(b + 1) * TOK],
                                               slot(("H1",))[:, b // 2, (b % 2) * TOK:(b % 2 + 1) * TOK], ACT.Gelu,
                                               bias=g_bias[:, b:b + 1])
                ins.then_inc(to_empty(("H1",)), 1)
                filled(act, g, ("H2",))
                nc.scalar.activation(h2_t[0:RHD // 2].rearrange("p (c n) -> p c n", c=2), c288(("H2",), RHD // 2),
                                     ACT.Gelu, bias=r_b[0:RHD // 2, 2:3]).then_inc(to_empty(("H2",)), 1)
                for half in range(2):
                    filled(act, g, ("K2", half))
                    nc.scalar.activation(fm(k2, half), c288(("K2", half), HT), ACT.Identity,
                                         bias=bk2[:, half:half + 1]).then_inc(to_empty(("K2", half)), 1)
                mixed(2)
                filled(act, g, ("LN", 5, 1))
                affine(("LN", 5, 1), fm_x, 1, 2, True)
                for i in range(FT):
                    filled(act, g, ("F1", i))
                    nc.scalar.activation(ff[:, i].rearrange("p (c n) -> p c n", c=2), c288(("F1", i), 128), ACT.Gelu,
                                         bias=fc1_b[:, i:i + 1]).then_inc(to_empty(("F1", i)), 1)
                chunk(("OUT", 1), 1)
                copy(("DT", 1), fm_o[0:HT, :, CH:2 * CH], slot(("DT", 1))[0:HT, :, 0:CH])

        @block.vector
        def _(dve):
            done = [0]

            def link_setup(ins):
                ins.then_inc(vec_setup, 1)
                done[0] += 1
                dve.wait_ge(vec_setup, done[0])

            nc.vector.memset(ones_row, 1.0).then_inc(ones_set, 1)
            dve.wait_ge(w_tok, 96)
            link_setup(nc.vector.tensor_tensor(emb_bias, emb_bias, emb_b, ALU.add))
            for s in range(4):
                nc.vector.memset(negmax[0][:, s:s + 1], 0.0).then_inc(psum_emptied[s], 1)
            with dve.Fori(0, E_TILES // 2) as i:
                for t in range(2):
                    for hf in range(2):
                        dve.wait_ge(emb_filled, i * 4 + (2 * t + 1))
                        ins = nc.vector.tensor_copy(emb_xt[:, 3 * hf:3 * hf + 3], ps[0][:, hf, 0:384].rearrange("p (a b) -> p a b", a=3))
                    ins.then_inc(emb_emptied, 1)
                    dve.wait_ge(emb_filled, i * 4 + (2 * t + 2))
                    nc.vector.tensor_tensor(emb_out[t], ps[1][:, 0, 0:DIM], emb_bias, ALU.add).then_inc(emb_emptied, 1)
                for t in range(2):
                    dve.wait_ge(emb_stored[t], i * 64 + 64)
            dve.wait_ge(w_l0, W_L0)
            link_setup(nc.vector.tensor_scalar(coef_y[:], coef_y[:], -2.0, 1.0, ALU.mult, ALU.add))
            link_setup(nc.vector.tensor_scalar(coef_z[:], coef_z[:], 3.0, None, ALU.mult))
            nc.vector.tensor_scalar(mix_in[:], mix_in[:], float(D0) ** -0.5, None, ALU.mult).then_inc(mix_ready, 1)

            with dve.Fori(0, GROUPS) as g:
                n_step = [0]
                n_ln = [0]

                def link(ins):
                    n_step[0] += 1
                    ins.then_inc(vec_step, 1)
                    dve.wait_ge(vec_step, g * VEC_STEPS + n_step[0])

                def ln_stats(src, part):
                    c = slice(HALF * part, HALF * part + HALF)
                    for j in TILES_OF[part]:
                        ins = nc.vector.bn_stats(stats[:, j, :], src[:, j, :])
                    link(ins)
                    even, odd = stats[:, c, 0:3], stats[:, c, 3:6]
                    nc.vector.tensor_tensor(mean2[:, c], even[:, :, 1], odd[:, :, 1], ALU.add)
                    nc.vector.tensor_tensor(diff[:, c], even[:, :, 1], odd[:, :, 1], ALU.subtract)
                    link(nc.vector.tensor_tensor(var[:, c], even[:, :, 2], odd[:, :, 2], ALU.add))
                    nc.vector.tensor_scalar(mean[:, c], mean2[:, c], 0.5, None, ALU.mult)
                    nc.vector.tensor_scalar(var2[:, c], var[:, c], 1.0 / DIM, EPS, ALU.mult, ALU.add)
                    link(nc.vector.scalar_tensor_tensor(diff2[:, c], diff[:, c], 0.25, diff[:, c], ALU.mult, ALU.mult))
                    nc.vector.tensor_tensor(var_eps[:, c], var2[:, c], diff2[:, c], ALU.add).then_inc(var_ready, 1)

                def ln_apply(src, dst, part):
                    n_ln[0] += 1
                    dve.wait_ge(rstd_ready, g * 12 + n_ln[0])
                    for j in TILES_OF[part]:
                        ins = nc.vector.tensor_scalar(dst[:, j, :], src[:, j, :], mean[:, j:j + 1], rstd[:, j:j + 1],
                                                      ALU.subtract, ALU.mult)
                    ins.then_inc(ln_ready, 1)

                def layernorm(src, dst):
                    for part in range(2):
                        ln_stats(src, part)
                    for part in range(2):
                        ln_apply(src, dst, part)

                c288 = lambda key_, m: slot(key_)[0:m, :, 0:CH]
                fm = lambda buf, hf: buf[0:HT, hf].rearrange("p (c n) -> p c n", c=2)

                def copy(key_, out_, in_):
                    filled(dve, g, key_)
                    nc.vector.tensor_copy(out_, in_).then_inc(to_empty(key_), 1)

                def add_to(key_, i, dst, base):
                    filled(dve, g, key_)
                    c = slice(HALF * i, HALF * i + HALF)
                    nc.vector.tensor_tensor(dst[:, c], tiles(key_), base[:, c], ALU.add).then_inc(to_empty(key_), 1)

                def residual(name, src, dst):
                    for i in range(2):
                        add_to((name, i), i, h, h)
                        emptied(dve, g, (name, i))
                        ln_stats(src, i)
                    for i in range(2):
                        ln_apply(src, dst, i)

                def chunk(key_, c):
                    copy(key_, fm_x[:, :, c * CH:(c + 1) * CH], slot(key_)[0:HT, :, 0:CH])

                def gated(name, bit, base):
                    for i in range(2):
                        filled(dve, g, (name, i))
                        for j in TILES_OF[i]:
                            ins = nc.vector.scalar_tensor_tensor(tm_z[:, j, :], tiles((name, i))[:, j % HALF], bits[:, j, bit:bit + 1],
                                                                 base[:, j, :], ALU.mult, ALU.add)
                        ins.then_inc(to_empty((name, i)), 1)
                        if name == "P2":
                            emptied(dve, g, (name, i))
                            ln_stats(tm_z, i)

                def mixed(which):
                    y, src_o = (y0, None) if which == 0 else (None, o2)
                    for t in range(GB * PACKS + 4):
                        if t < GB * PACKS:
                            filled(dve, g, (f"S{which}", t))
                            nc.vector.tensor_reduce(negmax[t % 3][:].rearrange("p (a b) -> p a b", a=2),
                                                    slot((f"S{which}", t))[0:RP, :, 0:CH].rearrange("p a (b n) -> p a b n", b=2),
                                                    AX.X, ALU.max, negate=True).then_inc(max_ready[which], 1)
                        if 1 <= t <= GB * PACKS:
                            emptied(dve, g, (f"S{which}", t - 1))
                            link(nc.vector.reciprocal(rinv[(t - 1) % 3][:], rowsum[(t - 1) % 3][:]))
                            e = probs0[(t - 1) % 3][0:RP]
                            nc.vector.tensor_tensor(e, e, rinv[(t - 1) % 3][:].unsqueeze(2).to_broadcast([RP, PACK, TOK]),
                                                    ALU.mult).then_inc(probs_ready[which // 2], 1)
                        if t >= 6 and t % 4 == 2:
                            b = (t - 6) // 4
                            if which == 0:
                                copy(("Y0", b), y0, slot(("Y0", b))[0:T72, :, 0:DIM])
                                filled(dve, g, ("Z0", b))
                                nc.vector.tensor_tensor(t0.rearrange("p a (g d) -> p a g d", d=D0),
                                                        slot(("Z0", b))[0:T72, :, 0:DIM].rearrange("p a (g d) -> p a g d", d=D0),
                                                        coef_z[:].unsqueeze(1).unsqueeze(3).to_broadcast([T72, 2, HEADS, D0]),
                                                        ALU.mult).then_inc(to_empty(("Z0", b)), 1)
                            else:
                                copy(("Y2", b), o2[b % 2], slot(("Y2", b))[0:T72, :, 0:DIM])
                        if 2 <= t < GB * PACKS + 2 and t % 2 == 1:
                            mixed_out(g, dve, nc.vector.tensor_copy, which, t - 2)
                        if t >= 7 and t % 4 == 3:
                            b = (t - 7) // 4
                            key_ = (f"OT{which}", b)
                            copy(key_, fm_o[0:HT, :, b * TOK:(b + 1) * TOK], slot(key_)[0:HT, :, 0:TOK])

                dve.wait_ge(h_loaded, g * 96 + 96)
                layernorm(h, tm_x)
                chunk(("LN", 0, 0), 0)
                copy(("V0", 0), v0[:, 0:4].rearrange("p (c j) d -> p c (j d)", c=2), slot(("V0", 0))[0:T72, :, 0:2 * DIM])
                copy(("Q0", 0), fm(q0, 0), c288(("Q0", 0), HT))
                copy(("K0", 0), fm(k0, 0), c288(("K0", 0), HT))
                mixed(0)
                residual("P0", h, tm_x)

                chunk(("LN", 1, 0), 0)
                filled(dve, g, ("LG",))
                logits = slot(("LG",))[0:HT, 0, 0:NT * EXPERTS].rearrange("p (j e) -> p j e", e=EXPERTS)
                link(nc.vector.tensor_reduce(lgm[:], logits, AX.X, ALU.max))
                wide = lambda v: v.unsqueeze(2).to_broadcast([HT, NT, EXPERTS])
                nc.vector.tensor_tensor(lg[:], logits, wide(lgm[:]), ALU.subtract).then_inc(to_empty(("LG",)), 1)
                dve.wait_ge(logit_exp, g + 1)
                link(nc.vector.tensor_reduce(lgs[:], lg2[:], AX.X, ALU.add))
                link(nc.vector.reciprocal(lgs[:], lgs[:]))
                link(nc.vector.tensor_tensor(lg2[:], lg2[:], wide(lgs[:]), ALU.mult))
                by_e = lambda v: v.unsqueeze(1).to_broadcast([HT, NT, EXPERTS])
                for k in range(2):
                    link(nc.vector.tensor_reduce(gate[:, :, k], lg2[:], AX.X, ALU.max))
                    link(nc.vector.tensor_tensor(lg[:], lg2[:], wide(gate[:, :, k]), ALU.is_equal))
                    link(nc.vector.tensor_tensor(lg[:], lg[:], by_e(first_e[:]), ALU.mult))
                    link(nc.vector.tensor_reduce(key[:], lg[:], AX.X, ALU.max))
                    link(nc.vector.tensor_tensor(picked[:, :, k, :], lg[:], wide(key[:]), ALU.is_equal))
                    if k == 0:
                        link(nc.vector.scalar_tensor_tensor(lg2[:], picked[:, :, 0, :], -2.0, lg2[:], ALU.mult, ALU.add))
                nc.vector.tensor_copy(picked_bf[:], picked[:].rearrange("p j k e -> p j (k e)")).then_inc(picked_ready, 1)
                filled(dve, g, ("CT",))
                counts = slot(("CT",))[0:HT, 0, 0:NT * 2 * EXPERTS].rearrange("p (j k e) -> p j k e", k=2, e=EXPERTS)
                nc.vector.tensor_tensor(place[:], counts, picked[:], ALU.mult).then_inc(to_empty(("CT",)), 1)
                emptied(dve, g, ("CT",))
                link(nc.vector.tensor_reduce(pos[:], place[:], AX.X, ALU.add))
                for k in range(2):
                    ins = nc.vector.tensor_tensor(place[:, :, k], picked[:, :, k], by_e(base_e[:]), ALU.mult)
                link(ins)
                link(nc.vector.tensor_reduce(row_of[:], place[:], AX.X, ALU.add))
                link(nc.vector.tensor_tensor(row_of[:], row_of[:], pos[:], ALU.add))
                link(nc.vector.tensor_scalar(pos[:], pos[:], float(CAP) - 0.5, float(2 * SLOTS), ALU.is_gt, ALU.mult))
                link(nc.vector.tensor_tensor(row_of[:], row_of[:], pos[:], ALU.add))
                nc.vector.tensor_scalar(row_idx[:], row_of[:], float(SLOTS), None, ALU.min).then_inc(rows_chosen, 1)

                for i in (0, 2):
                    copy(("XT", i), xe[:, :, 480 * i:480 * i + 480], slot(("XT", i))[0:HT, :, 0:480])
                for e in range(EXPERTS + 1):
                    if e < EXPERTS:
                        filled(dve, g, ("H", e, 1))
                        nc.vector.tensor_scalar(hid[e % 2][:, 4:6].rearrange("p j n -> p (j n)"),
                                                slot(("H", e, 1))[:, 0, 0:2 * CAP], 0.0, None, ALU.max)\
                            .then_inc(to_empty(("H", e, 1)), 1)
                    if e >= 1:
                        copy(("EO", e - 1), eo[:, 2 * e - 2:2 * e].rearrange("p c d -> p (c d)"),
                             slot(("EO", e - 1))[0:CAP // 2, 0, 0:2 * DIM])
                for part in range(2):
                    dve.wait_ge(gathered[part], g * 96 + 96)
                    for k in range(2):
                        for j in TILES_OF[part]:
                            ins = nc.vector.scalar_tensor_tensor(h[:, j, :], back[:, j, k * DIM:(k + 1) * DIM],
                                                                 gate[:, j, k:k + 1], h[:, j, :], ALU.mult, ALU.add)
                        link(ins)
                    ln_stats(h, part)
                for part in range(2):
                    ln_apply(h, tm_x, part)
                chunk(("LN", 2, 0), 0)

                def max_pair(which, s):
                    name = "S1" if which == 1 else "S2"
                    filled(dve, g, (name, s))
                    nc.vector.tensor_reduce(negmax[s % 3][0:T72].rearrange("p (a b) -> p a b", a=2),
                                            slot((name, s))[0:T72, :, 0:CH].rearrange("p a (b n) -> p a b n", b=2),
                                            AX.X, ALU.max, negate=True).then_inc(max_ready[which], 1)

                def divide_out(key_, dst, width, inv):
                    filled(dve, g, key_)
                    src = slot(key_)[0:T72, :, 0:2 * (width + 1)].rearrange("p a (b d) -> p a b d", b=2)
                    link(nc.vector.reciprocal(inv[:], src[:, :, :, width]))
                    nc.vector.tensor_tensor(dst, src[:, :, :, 0:width],
                                            inv[:].unsqueeze(3).to_broadcast([T72, 2, 2, width]), ALU.mult)\
                        .then_inc(to_empty(key_), 1)

                for s in range(STEPS + 3):
                    if s % 4 == 0 and s < STEPS:
                        hp = s // 4
                        filled(dve, g, ("Q1", hp))
                        nc.vector.tensor_scalar(q1[hp % 2].rearrange("p (c n) -> p c n", c=2), c288(("Q1", hp), 128),
                                                scale1[:, hp:hp + 1], None, ALU.mult).then_inc(to_empty(("Q1", hp)), 1)
                        filled(dve, g, ("V1", hp))
                        nc.vector.memset(v1[hp % 2][:, :, :, D1:D1 + 1], 1.0)
                        for c in range(2):
                            ins = nc.vector.tensor_copy(v1[hp % 2][:, 4 * c:4 * c + 4, :, 0:D1],
                                                        slot(("V1", hp))[0:T72, c, :].rearrange("p (j a d) -> p j a d", j=4, a=2))
                        ins.then_inc(to_empty(("V1", hp)), 1)
                    if s < STEPS:
                        max_pair(1, s)
                    if 2 <= s < STEPS + 2 and s % 2 == 1:
                        copy(("T1", s - 2), pt1[s % 2].rearrange("p a b n -> p a (b n)"), c288(("T1", s - 2), T72))
                    if s >= 3:
                        hp, b = divmod(s - 3, 4)
                        divide_out(("O1", s - 3), o1[hp % 2][:, 2 * b:2 * b + 2, :].rearrange("p b (a d) -> p a b d", a=2), D1, o_inv[s % 2])
                dve.wait_ge(bias1_added, g + 1)
                residual("P1", h, tm_x)

                for part in range(2):
                    dve.wait_ge(ln_ready, g * 12 + (7 + part))
                    ln_stats(tm_x, part)
                for part in range(2):
                    ln_apply(tm_x, tm_z, part)
                def affine(key_, dst, c, gain, last):
                    for hf in range(2):
                        ins = nc.vector.tensor_scalar(dst[0:HT, hf, c * CH:(c + 1) * CH], slot(key_)[0:HT, hf, 0:CH],
                                                      ln_gb[:, hf, gain:gain + 1], ln_gb[:, hf, gain + 1:gain + 2],
                                                      ALU.mult, ALU.add)
                    if last:
                        ins.then_inc(to_empty(key_), 1)

                filled(dve, g, ("LN", 4, 0))
                affine(("LN", 4, 0), fm_r, 0, 4, False)
                affine(("LN", 4, 0), fm_x, 0, 0, True)

                def queries(half):
                    filled(dve, g, ("Q2", half))
                    nc.vector.tensor_scalar(fm(q2, half), c288(("Q2", half), HT), bq2[:, half:half + 1], None, ALU.add)\
                        .then_inc(to_empty(("Q2", half)), 1)

                def values(i):
                    filled(dve, g, ("V2", i))
                    for c in range(2):
                        ins = nc.vector.tensor_tensor(v2[:, 4 * i + 2 * c:4 * i + 2 * c + 2],
                                                      slot(("V2", i))[0:T72, c, 0:2 * DIM].rearrange("p (j d) -> p j d", j=2),
                                                      bv2[:].unsqueeze(1).to_broadcast([T72, 2, DIM]), ALU.add)
                    ins.then_inc(to_empty(("V2", i)), 1)

                queries(0)
                emptied(dve, g, ("E1",))
                link(nc.vector.tensor_reduce(g_mean[:], e_t.rearrange("p (b n) -> p b n", b=GB)[:, :, 1:TOK], AX.X, ALU.add))
                nc.vector.tensor_scalar(g_mean[:], g_mean[:], 1.0 / (TOK - 1), None, ALU.mult).then_inc(g_mean_ready, 1)
                queries(1)
                filled(dve, g, ("GC",))
                nc.vector.tensor_scalar(g_bias[:], slot(("GC",))[0:RHD, 0, 0:GB], r_b[:, 1:2], None, ALU.add)\
                    .then_inc(to_empty(("GC",)), 1)
                nc.vector.memset(h2_t[RHD // 2:RHD // 2 + 1, :], 1.0).then_inc(h2_ones, 1)
                values(0)
                values(1)
                copy(("RL",), rl[:].rearrange("p j a b -> p (j a b)"), slot(("RL",))[0:HT, 0, 0:4 * NT])
                emptied(dve, g, ("RL",))
                link(nc.vector.tensor_tensor(bits[:], rl[:, :, :, 1], rl[:, :, :, 0], ALU.is_gt))
                link(nc.vector.tensor_tensor(bits[:], bits[:], reserved[:].unsqueeze(2).to_broadcast([HT, NT, 2]), ALU.max))
                link(nc.vector.tensor_scalar(nbits[:], bits[:], -1.0, 1.0, ALU.mult, ALU.add))
                nc.vector.tensor_tensor(sel[:, :, 0], nbits[:, :, 0], nbits[:, :, 1], ALU.mult)
                nc.vector.tensor_tensor(sel[:, :, 1], nbits[:, :, 0], bits[:, :, 1], ALU.mult)
                nc.vector.tensor_tensor(sel[:, :, 2], bits[:, :, 0], nbits[:, :, 1], ALU.mult).then_inc(bits_ready, 1)
                mixed(2)
                gated("P2", 0, tm_x)
                for part in range(2):
                    ln_apply(tm_z, tm_x, part)
                filled(dve, g, ("LN", 5, 0))
                affine(("LN", 5, 0), fm_x, 0, 2, True)
                dve.wait_ge(ffn_base, g + 1)
                gated("F2", 1, tm_x)
                chunk(("OUT", 0), 0)
                for i in range(2):
                    filled(dve, g, ("DN", i))
                    for j in TILES_OF[i]:
                        ins = nc.vector.tensor_tensor(tm_x[:, j].rearrange("p (k r) -> p k r", k=3),
                                                      tiles(("DN", i))[:, j % HALF].rearrange("p (k r) -> p k r", k=3),
                                                      sel[:, j].unsqueeze(2).to_broadcast([HT, 3, RANK]), ALU.mult)
                    ins.then_inc(to_empty(("DN", i)), 1)
                copy(("DT", 0), fm_o[0:HT, :, 0:CH], slot(("DT", 0))[0:HT, :, 0:CH])
                dve.wait_ge(out_added, g + 1)
                add_to(("UP", 0), 0, h, h)
                add_to(("UP", 1), 1, h, h)
                assert n_step[0] == VEC_STEPS, n_step[0]

        @block.tensor
        def _(pe):
            pe.wait_ge(w_tok, 96)
            pe.wait_ge(pool_setup, 3)
            with pe.Fori(0, E_TILES // 2) as i:
                for t in range(2):
                    pe.wait_ge(patches_in[t], i * 64 + 64)
                    for c in range(6):
                        ins = nc.tensor.transpose(ps[0][:, c // 3, (c % 3) * 128:(c % 3 + 1) * 128], emb_x[t][:, c, :], ident[:])
                    ins.then_inc(emb_filled, 1)
                    pe.wait_ge(emb_emptied, i * 4 + (2 * t + 1))
                    for c in range(6):
                        ins = nc.tensor.matmul(ps[1][:, 0, 0:DIM], emb_xt[:, c, :], emb_w[:, c, :], start=(c == 0), stop=(c == 5))
                    ins.then_inc(emb_filled, 1)
            pe.wait_ge(emb_emptied, 2 * E_TILES)

            with pe.Fori(0, GROUPS) as g:
                order = iter(UNITS)

                def begin(key_, reads=()):
                    assert next(order) == key_, key_
                    s, n = UNIT[key_] % 4, UNIT[key_] // 4
                    emptied(pe, g, *reads, but=s)
                    pe.wait_ge(psum_emptied[s], g * SLOT_USES[s] + (n + 1))
                    return slot(key_)

                def turn_tiles(k, src, reads=((), ()), after=None):
                    for c in range(2):
                        if after is not None:
                            pe.wait_ge(ln_ready, g * 12 + (2 * after + c + 1))
                        s = begin((*k, c), reads[c])
                        for hf in range(2):
                            for j in TILES_OF[c]:
                                ins = nc.tensor.transpose(s[0:HT, hf, (j % HALF) * HT:(j % HALF + 1) * HT],
                                                          src[:, j, hf * HT:(hf + 1) * HT], ident[0:HT, 0:HT])
                        ins.then_inc(psum_filled, 1)

                def by_feature(key_, w, m, x, reads=(), then=()):
                    s = begin(key_, reads)
                    for c in range(2):
                        if c == 1:
                            emptied(pe, g, *then)
                        for hf in range(2):
                            ins = nc.tensor.matmul(s[0:m, c, 0:CH], w(hf), x[0:HT, hf, c * CH:(c + 1) * CH],
                                                   start=(hf == 0), stop=(hf == 1))
                    ins.then_inc(psum_filled, 1)

                def by_token(key_, i, x, w, reads=(), bias=False, parts=2):
                    s = begin(key_, reads)
                    o = tiles(key_)
                    for j in TILES_OF[i]:
                        for f in range(parts):
                            k = 128 if parts > 2 else HT + 1 if bias and f == 0 else HT
                            ins = nc.tensor.matmul(o[:, j % HALF], x[0:k, f, j * HT:(j + 1) * HT], w[0:k, f, :],
                                                   start=(f == 0), stop=(f == parts - 1))
                    ins.then_inc(psum_filled, 1)

                def value_unit(name, i, w, reads):
                    s = begin((name, i), reads)
                    for j in range(4):
                        t = 4 * i + j
                        for hf in range(2):
                            ins = nc.tensor.matmul(s[0:T72, j // 2, (j % 2) * DIM:(j % 2 + 1) * DIM],
                                                   fm_x[:, hf, t * T72:(t + 1) * T72], w[:, hf, :],
                                                   start=(hf == 0), stop=(hf == 1))
                    ins.then_inc(psum_filled, 1)

                def mixed(which, k, v, at):
                    rows = HT + 1 if which == 0 else HT
                    for t in range(GB * PACKS + 4):
                        if t < GB * PACKS:
                            b = t // PACKS
                            pe.wait_ge(qg_ready if which == 0 else qg2_ready, g * GB * PACKS + (t + 1))
                            s = begin((f"S{which}", t), both(f"K{which}"))
                            for i in range(PACK):
                                for hf in range(2):
                                    r = rows if hf == 0 else HT
                                    ins = nc.tensor.matmul(s[0:RP, i // 2, (i % 2) * TOK:(i % 2 + 1) * TOK],
                                                           qg0[t % 3][0:r, hf, i * RP:(i + 1) * RP],
                                                           k[0:r, hf, b * TOK:(b + 1) * TOK], start=(hf == 0), stop=(hf == 1))
                            ins.then_inc(psum_filled, 1)
                        if t >= 6 and t % 4 == 2:
                            b = (t - 6) // 4
                            for name in ("Y", "Z") if which == 0 else ("Y",):
                                s = begin((f"{name}{which}", b), [(f"M{which}", 4 * b + p) for p in range(PACKS)] + both(f"V{which}")
                                          if name == "Y" else [("Y0", b)])
                                for nh in range(2):
                                    for hd in range(HEADS):
                                        for mh in range(2):
                                            src = v[:, 2 * b + mh] if name == "Y" else y0[:, mh]
                                            ins = nc.tensor.matmul(s[0:T72, nh, hd * D0:(hd + 1) * D0],
                                                                   at[:, mh, hd, nh * T72:(nh + 1) * T72],
                                                                   src[:, hd * D0:(hd + 1) * D0],
                                                                   start=(mh == 0), stop=(mh == 1))
                                ins.then_inc(psum_filled, 1)
                        if 2 <= t < GB * PACKS + 2:
                            pe.wait_ge(probs_ready[which // 2], g * GB * PACKS + (t - 1))
                            s = begin((f"M{which}", t - 2))
                            for mh in range(2):
                                for i in range(PACK):
                                    o = s[0:T72, mh, i * RP:(i + 1) * RP]
                                    p = probs0[(t - 2) % 3]
                                    if which == 0:
                                        ins = nc.tensor.matmul(o, p[:, i, mh * T72:(mh + 1) * T72], mix_out[:], start=True, stop=True)
                                    else:
                                        ins = nc.tensor.transpose(o, p[0:RP, i, mh * T72:(mh + 1) * T72], ident[0:RP, 0:RP])
                            ins.then_inc(psum_filled, 1)
                        if t >= 7 and t % 4 == 3:
                            b = (t - 7) // 4
                            if which == 0:
                                pe.wait_ge(o0_ready, g * GB + (b + 1))
                            s = begin((f"OT{which}", b), [] if which == 0 else [("Y2", b)])
                            for hf in range(2):
                                for nh in range(2):
                                    ins = nc.tensor.transpose(s[0:HT, hf, nh * T72:(nh + 1) * T72],
                                                              (o0 if which == 0 else o2[b % 2])[:, nh, hf * HT:(hf + 1) * HT],
                                                              ident[0:T72, 0:T72])
                            ins.then_inc(psum_filled, 1)

                def both(*k):
                    return [(*k, 0), (*k, 1)]

                turn_tiles(("LN", 0), tm_x, after=0)
                pe.wait_ge(w_l0, W_L0)
                for i in range(2):
                    value_unit("V0", i, qkv0_w[:, :, 2 * DIM:3 * DIM], [("LN", 0, i)])
                for o, k in ((0, "Q0"), (DIM, "K0")):
                    for half in range(2):
                        by_feature((k, half), lambda hf: qkv0_w[:, hf, o + half * HT:o + (half + 1) * HT], HT, fm_x)
                mixed(0, k0, v0, at0)
                for i in range(2):
                    by_token(("P0", i), i, fm_o, proj0_w, [("OT0", b) for b in range(GB)], bias=True)

                turn_tiles(("LN", 1), tm_x, after=1)
                pe.wait_ge(w_moe, W_MOE)
                s = begin(("LG",), both("LN", 1))
                for j in range(NT):
                    for hf in range(2):
                        ins = nc.tensor.matmul(s[0:HT, 0, j * EXPERTS:(j + 1) * EXPERTS], fm_x[:, hf, j * HT:(j + 1) * HT],
                                               router_w[:, hf, :], start=(hf == 0), stop=(hf == 1))
                ins.then_inc(psum_filled, 1)
                pe.wait_ge(picked_ready, g + 1)
                s = begin(("CT",))
                E2 = 2 * EXPERTS
                for j in range(NT):
                    for i in range(j + 1):
                        nc.tensor.matmul(s[0:HT, 0, j * E2:(j + 1) * E2], (before_bf if i == j else ones_bf)[:],
                                         picked_bf[:, i, :], start=(i == 0), stop=False)
                    for i in range(NT):
                        ins = nc.tensor.matmul(s[0:HT, 0, j * E2 + EXPERTS:(j + 1) * E2], ones_bf[:],
                                               picked_bf[:, i, 0:EXPERTS], start=False, stop=(i == NT - 1))
                ins.then_inc(psum_filled, 1)

                pe.wait_ge(experts_in, g * 16 + 16)
                for i in range(3):
                    s = begin(("XT", i))
                    for hf in range(2):
                        for c in range(4):
                            ins = nc.tensor.transpose(s[0:HT, hf, c * SLOT_P:(c + 1) * SLOT_P],
                                                      xe_tok[:, 4 * i + c, hf * HT:(hf + 1) * HT], ident[0:SLOT_P, 0:SLOT_P])
                    ins.then_inc(psum_filled, 1)
                for e in range(EXPERTS + 1):
                    if e < EXPERTS:
                        for part in range(2):
                            s = begin(("H", e, part), [("XT", i) for i in range(3)])
                            for f in (range(0, 4) if part == 0 else range(4, 6)):
                                for hf in range(2):
                                    ins = nc.tensor.matmul(s[:, (f % 4) // 2, (f % 2) * CAP:(f % 2 + 1) * CAP],
                                                           moe_wi[:, hf, e, f * 128:(f + 1) * 128],
                                                           xe[:, hf, e * CAP:(e + 1) * CAP], start=(hf == 0), stop=(hf == 1))
                            ins.then_inc(psum_filled, 1)
                    if e >= 1:
                        s = begin(("EO", e - 1), both("H", e - 1))
                        for c in range(2):
                            for f in range(FT):
                                ins = nc.tensor.matmul(s[0:CAP // 2, 0, c * DIM:(c + 1) * DIM],
                                                       hid[(e - 1) % 2][:, f, c * (CAP // 2):(c + 1) * (CAP // 2)],
                                                       moe_wo[:, e - 1, f, :], start=(f == 0), stop=(f == FT - 1))
                        ins.then_inc(psum_filled, 1)

                def score_pair(key_, q, k, rows, b, width, masked, reads):
                    s = begin(key_, reads)
                    for a_ in range(2):
                        r = rows[a_]
                        for nh in range(2):
                            o = s[0:T72, a_, nh * TOK:(nh + 1) * TOK]
                            ins = nc.tensor.matmul(o, q[r:r + width, b * TOK + nh * T72:b * TOK + (nh + 1) * T72],
                                                   k[r:r + width, b * TOK:(b + 1) * TOK], start=True, stop=not masked)
                            if masked:
                                ins = nc.tensor.matmul(o, ident_bf[:], diag_bf[:, nh, :], start=False, stop=True)
                    ins.then_inc(psum_filled, 1)

                def turn_probs(key_, p, scores):
                    s = begin(key_, [scores])
                    for a_ in range(2):
                        for mh in range(2):
                            for nh in range(2):
                                ins = nc.tensor.transpose(s[0:T72, a_, mh * TOK + nh * T72:mh * TOK + (nh + 1) * T72],
                                                          p[:, a_, nh, mh * T72:(mh + 1) * T72], ident[0:T72, 0:T72])
                    ins.then_inc(psum_filled, 1)

                def attend(key_, pt, v, b, width, reads):
                    s = begin(key_, reads)
                    for a_ in range(2):
                        for nh in range(2):
                            for mh in range(2):
                                ins = nc.tensor.matmul(s[0:T72, a_, nh * (width + 1):(nh + 1) * (width + 1)],
                                                       pt[:, a_, mh, nh * T72:(nh + 1) * T72], v(2 * b + mh, a_),
                                                       start=(mh == 0), stop=(mh == 1))
                    ins.then_inc(psum_filled, 1)

                turn_tiles(("LN", 2), tm_x, after=2)
                pe.wait_ge(w_l1, 80)
                for s_ in range(STEPS + 3):
                    if s_ % 4 == 0 and s_ < STEPS:
                        hp = s_ // 4
                        cols = slice(hp * 128, (hp + 1) * 128)
                        by_feature(("Q1", hp), lambda hf: qkv1_w[:, hf, 0, cols], 128, fm_x, [("LN", 2, 0)], [("LN", 2, 1)])
                        by_feature(("K1", hp), lambda hf: qkv1_w[:, hf, 1, cols], 128, fm_x)
                        s = begin(("V1", hp))
                        for t in range(N72):
                            for hf in range(2):
                                ins = nc.tensor.matmul(s[0:T72, t // 4, (t % 4) * 128:(t % 4 + 1) * 128],
                                                       fm_x[:, hf, t * T72:(t + 1) * T72], qkv1_w[:, hf, 2, cols],
                                                       start=(hf == 0), stop=(hf == 1))
                        ins.then_inc(psum_filled, 1)
                    if s_ < STEPS:
                        hp, b = divmod(s_, 4)
                        score_pair(("S1", s_), q1[hp % 2], k1[hp % 2], (0, D1), b, D1, True,
                                   [("Q1", hp), ("K1", hp)])
                    if 2 <= s_ < STEPS + 2:
                        turn_probs(("T1", s_ - 2), p12[(s_ - 2) % 3], ("S1", s_ - 2))
                    if s_ >= 3:
                        hp, b = divmod(s_ - 3, 4)
                        attend(("O1", s_ - 3), pt1[(s_ - 3) % 2], lambda t, a_: v1[hp % 2][:, t, a_, :], b, D1,
                               [("T1", s_ - 3), ("V1", hp)])
                    if s_ >= 6 and s_ % 4 == 2:
                        hp = (s_ - 6) // 4
                        s = begin(("OT1", hp), [("O1", 4 * hp + b) for b in range(GB)])
                        for t in range(N72):
                            ins = nc.tensor.transpose(s[:, t // 4, (t % 4) * T72:(t % 4 + 1) * T72],
                                                      o1[hp % 2][:, t, :], ident[0:T72, 0:T72])
                        ins.then_inc(psum_filled, 1)
                for i in range(2):
                    by_token(("P1", i), i, ot1, proj1_w, [("OT1", hp) for hp in range(6)], parts=6)

                turn_tiles(("LN", 4), tm_z, after=4)
                pe.wait_ge(w_ffn, W_FFN)
                half_of = lambda w, half: lambda hf: w[:, hf, half * HT:(half + 1) * HT]
                by_feature(("E1",), lambda hf: r_in_w[:, hf, :], RHD, fm_r, [("LN", 4, 0)], [("LN", 4, 1)])
                by_feature(("Q2", 0), half_of(wq2, 0), HT, fm_x)
                by_feature(("Q2", 1), half_of(wq2, 1), HT, fm_x)
                pe.wait_ge(g_mean_ready, g + 1)
                s = begin(("GC",))
                nc.tensor.matmul(s[0:RHD, 0, 0:GB], r_o1_w[:, 1, :], g_mean[:], start=True, stop=True).then_inc(psum_filled, 1)
                value_unit("V2", 0, wv2, [])
                s = begin(("H1",))
                for c in range(2):
                    ins = nc.tensor.matmul(s[0:RHD, c, 0:CH], r_o1_w[:, 0, :], e_t[:, c * CH:(c + 1) * CH], start=True, stop=True)
                ins.then_inc(psum_filled, 1)
                value_unit("V2", 1, wv2, [])
                s = begin(("H2",), [("H1",)])
                for c in range(2):
                    ins = nc.tensor.matmul(s[0:RHD // 2, c, 0:CH], r_o2_w[:], h1_t[:, c * CH:(c + 1) * CH], start=True, stop=True)
                ins.then_inc(psum_filled, 1)
                by_feature(("K2", 0), half_of(wk2, 0), HT, fm_x)
                by_feature(("K2", 1), half_of(wk2, 1), HT, fm_x)
                pe.wait_ge(h2_ones, g + 1)
                s = begin(("RL",), [("H2",)])
                for j in range(NT):
                    ins = nc.tensor.matmul(s[0:HT, 0, 4 * j:4 * j + 4], h2_t[:, j * HT:(j + 1) * HT], r_o3_w[:], start=True, stop=True)
                ins.then_inc(psum_filled, 1)
                mixed(2, k2, v2, at2)
                for i in range(2):
                    by_token(("P2", i), i, fm_o, wo2, [("OT2", b) for b in range(GB)], bias=True)

                turn_tiles(("LN", 5), tm_x, after=5)
                for i in range(FT):
                    by_feature(("F1", i), lambda hf: fc1_w[:, hf, i * 128:(i + 1) * 128], 128, fm_x,
                               [("LN", 5, 0)], [("LN", 5, 1)] if i == 0 else ())
                for i in range(2):
                    by_token(("F2", i), i, ff, fc2_w, [("F1", f) for f in range(FT)], parts=FT)
                turn_tiles(("OUT",), tm_z, ([("F2", 0)], [("F2", 1)]))
                for i in range(2):
                    by_token(("DN", i), i, fm_x, lra_dn, [("OUT", i)])
                turn_tiles(("DT",), tm_x, ([("DN", 0)], [("DN", 1)]))
                for i in range(2):
                    by_token(("UP", i), i, fm_o, lra_up, [("DT", i)])


_ORDER = ["x", "txt", "tok_w", "tok_b", "pos", "qkv0_w", "proj_l_w", "proj_l_b", "proj_w_w", "proj_w_b", "lamb", "proj0_w",
          "proj0_b", "router_w", "moe_wi", "moe_wo", "qkv1_w", "scale1", "proj1_w", "bias1", "wq2", "wk2", "bq2", "bk2",
          "wv2", "bv2", "wo2", "bo2", "ln_gb", "fc1_w", "fc1_b", "fc2_w", "fc2_b", "r_in_w", "r_o1_w", "r_o2_w", "r_o3_w",
          "r_b", "r_o2_b", "lra_dn", "lra_up"]


def laid_out(i):
    def by_part(w, p):
        return w.reshape(w.shape[0] // p, p, w.shape[1]).transpose(1, 0, 2)

    row = lambda v: v.reshape(1, -1)
    f = {k[len("L1_ffn_"):]: v for k, v in i.items() if k.startswith("L1_ffn_")}
    return {
        "x": i["x"].reshape(SEQS, 64, 192), "txt": i["txt"], "tok_w": by_part(i["L0_tok_W"], 128), "tok_b": row(i["L0_tok_b"]),
        "pos": np.tile(i["L0_tok_pos_emb"].reshape(4, 4, DIM), (8, 1, 1)),
        "qkv0_w": by_part(i["L0_attn_qkv_w"].T, HT), "proj_l_w": i["L0_attn_proj_l_w"].T, "proj_l_b": row(i["L0_attn_proj_l_b"]),
        "proj_w_w": i["L0_attn_proj_w_w"].T, "proj_w_b": row(i["L0_attn_proj_w_b"]), "lamb": row(i["L0_attn_lamb"]),
        "proj0_w": by_part(i["L0_attn_proj_out_w"].T, HT), "proj0_b": row(i["L0_attn_proj_out_b"]),
        "router_w": by_part(i["L0_ffn_w_router"], HT),
        "moe_wi": i["L0_ffn_wi"].reshape(EXPERTS, 2, HT, FF).transpose(0, 2, 1, 3),
        "moe_wo": i["L0_ffn_wo"].reshape(EXPERTS, FT, 128, DIM).transpose(0, 2, 1, 3),
        "qkv1_w": by_part(i["L1_attn_W_qkv"], HT).reshape(HT, 2, 3, HEADS * D1),
        "scale1": i["L1_attn_scale"].reshape(6, 2).T, "proj1_w": by_part(i["L1_attn_W_out"], 128), "bias1": row(i["L1_attn_b_out"]),
        "wq2": by_part(f["wq"].T, HT), "wk2": by_part(f["wk"].T, HT), "bq2": f["bq"].reshape(2, HT).T, "bk2": f["bk"].reshape(2, HT).T,
        "wv2": by_part(f["wv"].T, HT), "bv2": row(f["bv"]), "wo2": by_part(f["wo"].T, HT), "bo2": row(f["bo"]),
        "ln_gb": np.stack([f[n].reshape(2, HT).T for n in ("ln1_g", "ln1_b", "ln2_g", "ln2_b", "r_ln_g", "r_ln_b")], axis=2),
        "fc1_w": by_part(f["fc1_w"].T, HT), "fc1_b": f["fc1_b"].reshape(FT, 128).T, "fc2_w": by_part(f["fc2_w"].T, 128),
        "fc2_b": row(f["fc2_b"]), "r_in_w": by_part(f["r_in_w"].T, HT), "r_o1_w": by_part(f["r_o1_w"].T, RHD),
        "r_o2_w": f["r_o2_w"].T, "r_o3_w": np.concatenate([f["r_o3_w"].T, row(f["r_o3_b"])]),
        "r_b": np.stack([f["r_in_b"], f["r_o1_b"]], axis=1), "r_o2_b": f["r_o2_b"].reshape(-1, 1),
        "lra_dn": by_part(f["lra_down"].reshape(3 * RANK, DIM).T, HT),
        "lra_up": by_part(f["lra_up"].transpose(0, 2, 1).reshape(3 * RANK, DIM), HT),
    }


def kernel(**inputs):
    import concourse.bacc as bacc
    from concourse.bass_utils import run_bass_kernel_spmd

    nc = bacc.Bacc("TRN2", target_bir_lowering=False, num_devices=1)
    laid = laid_out({k: np.asarray(v) for k, v in inputs.items()})
    arrays, aps = {}, {}
    for name in _ORDER:
        v = np.ascontiguousarray(laid[name])
        arrays["in_" + name] = v
        aps[name] = nc.dram_tensor("in_" + name, v.shape, mybir.dt.from_np(v.dtype), kind="ExternalInput").ap()
    out = nc.dram_tensor("out", (SEQS, TOK, DIM), F32, kind="ExternalOutput").ap()
    program(nc, aps, out.rearrange("b n d -> (b n) d"))
    return run_bass_kernel_spmd(nc, [arrays], core_ids=[0]).results[0]["out"]
```

```python
from contextlib import ExitStack

import numpy as np
import concourse.bass as bass
from concourse import mybir

F32 = mybir.dt.float32
BF16 = mybir.dt.bfloat16
U32 = mybir.dt.uint32
ALU = mybir.AluOpType
ACT = mybir.ActivationFunctionType
AX = mybir.AxisListType

SEQS, TOK, IMG_TOK, DIM = 64, 144, 16, 192
TXT_TOK = TOK - IMG_TOK
GB = 4
GROUPS = SEQS // GB
GT = GB * TOK
HT = 96
NT = GT // HT
CH = 2 * TOK
T72 = TOK // 2
N72 = GT // T72
HEADS = 12
D0 = DIM // HEADS
D1 = 64
RN = 9
RP = RN * HEADS
PACK = 4
PN = RN * PACK
PACKS = TOK // PN
EXPERTS, FF = 8, 768
FT = FF // 128
CAP = 180
SLOTS = EXPERTS * CAP
SLOT_P = 120
RHD, RANK = 128, 64
EPS = 1e-5
STEPS = 6 * GB
MASKED = -1.0e30
E_TILES = SEQS * IMG_TOK // 128


def psum_units():
    u = [("LN", 0, 0), ("LN", 0, 1)]
    u += [("V0", 0), ("V0", 1)] + [("Q0", 0), ("Q0", 1), ("K0", 0), ("K0", 1)]
    for t in range(GB * PACKS + 5):
        if t >= 8 and t % 4 == 0:
            u.append(("YT", (t - 8) // 4))
        if t < GB * PACKS:
            u.append(("S0", t))
        if t >= 5 and t % 2 == 1 and t < GB * PACKS + 4:
            u.append(("Y0", (t - 5) // 2))
        if t >= 8 and t % 4 == 0:
            u.append(("Z0", (t - 8) // 4))
        if 2 <= t < GB * PACKS + 2:
            u.append(("M0", t - 2))
        if t == 14:
            u.append(("P0", 0))
    u.append(("P0", 1))
    u += [("LN", 1, 0), ("LN", 1, 1), ("LG",), ("CT",)]
    u += [("XT", i) for i in range(3)]
    for e in range(EXPERTS + 1):
        if e < EXPERTS:
            u += [("H", e, 0), ("H", e, 1)]
        if e >= 1:
            u.append(("EO", e - 1))
    u += [("LN", 2, 0), ("LN", 2, 1)]
    for s in range(STEPS + 3):
        if s % 4 == 0 and s < STEPS:
            u += [("Q1", s // 4), ("K1", s // 4), ("V1", s // 4)]
        if s < STEPS:
            u.append(("S1", s))
        if 2 <= s < STEPS + 2:
            u.append(("T1", s - 2))
        if s >= 3:
            u.append(("O1", s - 3))
    u += [("P1", 0), ("P1", 1), ("LN", 4, 0), ("LN", 4, 1)]
    u += [("E1",), ("Q2", 0), ("Q2", 1), ("GC",), ("V2", 0), ("H1",), ("V2", 1), ("H2",), ("K2", 0), ("K2", 1), ("RL",)]
    for t in range(GB * PACKS + 4):
        if t < GB * PACKS:
            u.append(("S2", t))
        if t >= 5 and t % 2 == 1 and t < GB * PACKS + 4:
            u.append(("Y2", (t - 5) // 2))
        if 2 <= t < GB * PACKS + 2:
            u.append(("M2", t - 2))
    u += [("P2", 0), ("P2", 1), ("LN", 5, 0), ("LN", 5, 1)]
    u += [("F1", i) for i in range(FT)] + [("F2", 0), ("F2", 1)]
    u += [("OUT", 0), ("OUT", 1), ("DN", 0), ("DN", 1), ("DT", 0), ("DT", 1), ("UP", 0), ("UP", 1)]
    return u


UNITS = psum_units()
UNIT = {key: i for i, key in enumerate(UNITS)}
SLOT_USES = [len(range(s, len(UNITS), 4)) for s in range(4)]
VEC_STEPS = 141
W_L0 = 16 * 36
W_FFN = 16 * 21
W_MOE = 16 * (1 + 2 * EXPERTS)
HALF = NT // 2
TILES_OF = [range(0, HALF), range(HALF, NT)]
TS = 256


def program(nc, a, out):
    with ExitStack() as ctx:
        def sb(name, shape, dt=F32):
            return ctx.enter_context(nc.sbuf_tensor(name, shape, dt))

        def sem(name):
            return ctx.enter_context(nc.semaphore(name))

        img_rows = nc.dram_tensor("img_rows", (SEQS, IMG_TOK, DIM), F32, kind="Internal").ap()
        expert_rows = nc.dram_tensor("expert_rows", (SLOTS, DIM), F32, kind="Internal").ap()
        result_rows = nc.dram_tensor("result_rows", (SLOTS + 1, DIM), F32, kind="Internal").ap()

        moe_wi = sb("moe_wi", [HT, 2, EXPERTS, FF])
        moe_wo = sb("moe_wo", [128, EXPERTS, FT, DIM])
        router_w = sb("router_w", [HT, 2, EXPERTS])
        qkv0_w = sb("qkv0_w", [HT, 2, 3 * DIM])
        proj0_w = sb("proj0_w", [HT + 1, 2, DIM])
        mix_in = sb("mix_in", [HT, 2, HEADS])
        mix_out = sb("mix_out", [RP + 1, RP])
        coef_y = sb("coef_y", [HT, HEADS])
        coef_z = sb("coef_z", [HT, HEADS])
        by_head = sb("by_head", [HT, 2, HEADS])
        feature_y = sb("feature_y", [HT, 2])
        feature_z = sb("feature_z", [HT, 2, 2])
        parity = sb("parity", [HT, 2, 2])
        qkv1_w = sb("qkv1_w", [HT, 2, 3, HEADS * D1])
        scale1 = sb("scale1", [128, 6])
        proj1_w = sb("proj1_w", [128, 6, DIM])
        bias1 = sb("bias1", [HT, DIM])
        wq2 = sb("wq2", [HT, 2, DIM])
        wk2 = sb("wk2", [HT, 2, DIM])
        bq2 = sb("bq2", [HT, 2])
        bk2 = sb("bk2", [HT, 2])
        own_head = sb("own_head", [HT, 2, HEADS])
        wv2 = sb("wv2", [HT, 2, DIM])
        bv2 = sb("bv2", [T72, DIM])
        wo2 = sb("wo2", [HT + 1, 2, DIM])
        ln_gb = sb("ln_gb", [HT, 2, 6])
        fc1_w = sb("fc1_w", [HT, 2, FF])
        fc1_b = sb("fc1_b", [128, FT])
        fc2_w = sb("fc2_w", [128, FT, DIM])
        fc2_b = sb("fc2_b", [HT, DIM])
        r_in_w = sb("r_in_w", [HT, 2, RHD])
        r_o1_w = sb("r_o1_w", [RHD, 2, RHD])
        r_o2_w = sb("r_o2_w", [RHD, RHD // 2])
        r_o3_w = sb("r_o3_w", [RHD // 2 + 1, 4])
        r_b = sb("r_b", [RHD, 3])
        lra_dn = sb("lra_dn", [HT, 2, DIM])
        lra_up = sb("lra_up", [HT, 2, DIM])

        ident = sb("ident", [128, 128])
        ident_bf = sb("ident_bf", [T72, T72], BF16)
        diag_bf = sb("diag_bf", [T72, 2, TOK], BF16)
        before_bf = sb("before_bf", [HT, HT], BF16)
        ones_bf = sb("ones_bf", [HT, HT], BF16)
        first_e = sb("first_e", [HT, EXPERTS])
        base_e = sb("base_e", [HT, EXPERTS])
        reserved = sb("reserved", [HT, NT])
        eps_pow = sb("eps_pow", [HT, NT])

        h = sb("h", [HT, NT, DIM])
        AR = 15456
        arena = sb("arena", [128, AR])

        def view(at, rows, *shape):
            n = int(np.prod(shape))
            v = arena[0:rows, at:at + n]
            names = "abcd"[:len(shape)]
            if len(shape) == 1:
                return v
            return v.rearrange(f"p ({' '.join(names)}) -> p {' '.join(names)}",
                               **{c: s for c, s in zip(names, shape)})

        R0, R1, R2, R3, R4, R5, R6, R7 = 0, 1152, 2304, 3456, 4608, 5760, 8352, 10080
        tm_x = view(R0, HT, NT, DIM)
        fm_x = view(R1, HT, 2, GT)
        tm_z = view(R2, HT, NT, DIM)
        fm_o = view(R3, HT + 1, 2, GT)
        k0 = view(R4, HT + 1, 2, GT)
        qg0 = [view(R5 + 864 * i, HT + 1, 2, PN * HEADS) for i in range(3)]
        probs0 = [view(R6 + 576 * i, RP + 1, PACK, TOK) for i in range(3)]
        q0 = view(R7, HT, 2, GT)
        v0 = view(R7 + 1152, T72, N72, DIM)
        y0 = view(R7 + 2688, T72, 2, DIM)
        y0_t, u0_t = [view(R7 + 3072 + 288 * i, HT, 2, TOK) for i in range(2)]
        at0 = [view(at, T72, 2, HEADS, T72) for at in (R0, R0 + 1728, R7 + 3648)]
        xe_tok = view(R0, SLOT_P, SLOTS // SLOT_P, DIM)
        xe = view(R3, HT, 2, SLOTS)
        eo = view(R3 + 2880, CAP // 2, 2 * EXPERTS, DIM)
        hid = [view(R7 + 1080 * i, 128, FT, CAP) for i in range(2)]
        back = view(R0, HT, NT, 2 * DIM)
        pt1 = [view(R0 + 576 * i, T72, 2, 2, TOK) for i in range(2)]
        q1 = [view(R2, 128, GT), view(R7 + 3456, 128, GT)]
        k1 = [view(R2 + 576, 128, GT), view(R7 + 4032, 128, GT)]
        v1 = [view(R5 + 1024 * i, T72, N72, 2, D1) for i in range(2)]
        p12 = [view(R6 + 576 * i, T72, 2, 2, TOK) for i in range(3)]
        ot1 = view(R7, 128, 6, GT)
        fm_r = view(R4, HT, 2, GT)
        e_t = view(R7, RHD, GT)
        h1_t = view(R7 + 576, RHD, GT)
        h2_t = view(R7 + 1152, RHD // 2 + 1, GT)
        q2 = view(R2, HT, 2, GT)
        k2 = view(R4, HT, 2, GT)
        v2 = view(R7 + 3456, T72, N72, DIM)
        at2 = [view(R7 + 1728 * i, T72, 2, HEADS, T72) for i in range(2)]
        ff = view(R7, 128, FT, GT)
        emb_w = view(R7, 128, 6, DIM)
        emb_x = [view(R0 + 768 * i, 128, 6, 128) for i in range(2)]
        emb_xt = view(R2, 128, 6, 128)
        emb_bias = view(1536, 128, DIM)
        emb_b = view(1536 + 192, 128, DIM)
        emb_out = [view(1920 + 192 * i, 128, DIM) for i in range(2)]
        zero_rows = view(R7 + 1152, SLOT_P, SLOTS // SLOT_P, DIM)
        ones_row = view(R7 + 3456, 1, PACK * TOK)

        stats = sb("stats", [HT, NT, 6])
        mean = sb("mean", [HT, NT])
        idle = sb("idle", [HT, NT])
        idle2 = sb("idle2", [HT, NT])
        mean2 = sb("mean2", [HT, NT])
        diff = sb("diff", [HT, NT])
        diff2 = sb("diff2", [HT, NT])
        var = sb("var", [HT, NT])
        var2 = sb("var2", [HT, NT])
        var_eps = sb("var_eps", [HT, NT])
        rstd = sb("rstd", [HT, NT])
        negmax = [sb(f"negmax{i}", [RP, 4]) for i in range(3)]
        rowsum = [sb(f"rowsum{i}", [RP, 4]) for i in range(3)]
        rinv = [sb(f"rinv{i}", [RP, 4]) for i in range(3)]
        lg = sb("lg", [HT, NT, EXPERTS])
        lg2 = sb("lg2", [HT, NT, EXPERTS])
        lgm = sb("lgm", [HT, NT])
        lgs = sb("lgs", [HT, NT])
        gate = sb("gate", [HT, NT, 2])
        key = sb("key", [HT, NT])
        picked = sb("picked", [HT, NT, 2, EXPERTS])
        picked_bf = sb("picked_bf", [HT, NT, 2 * EXPERTS], BF16)
        place = sb("place", [HT, NT, 2, EXPERTS])
        pos = sb("pos", [HT, NT, 2])
        row_of = sb("row_of", [HT, NT, 2])
        row_idx = sb("row_idx", [HT, NT, 2], U32)
        g_mean = sb("g_mean", [RHD, GB])
        g_bias = sb("g_bias", [RHD, GB])
        rl = sb("rl", [HT, NT, 2, 2])
        bits = sb("bits", [HT, NT, 2])
        nbits = sb("nbits", [HT, NT, 2])
        sel = sb("sel", [HT, NT, 3])
        table_out = sb("table_out", [HT, NT])

        ps_flat = [ctx.enter_context(nc.psum_tensor(f"ps{i}", [128, 1024], F32)) for i in range(4)]
        ps = [v[:, :].rearrange("p (a n) -> p a n", a=2) for v in ps_flat]

        psum_filled = sem("psum_filled")
        psum_emptied = [sem(f"psum_emptied{i}") for i in range(4)]
        w_tok, w_l0, w_moe, w_l1, w_ffn = (sem(n) for n in ("w_tok", "w_l0", "w_moe", "w_l1", "w_ffn"))
        mix_zeroed = sem("mix_zeroed")
        ones_set = sem("ones_set")
        mix_ready = sem("mix_ready")
        vec_setup = sem("vec_setup")
        pool_setup = sem("pool_setup")
        patches_in = [sem(f"patches_in{i}") for i in range(2)]
        emb_filled = sem("emb_filled")
        emb_emptied = sem("emb_emptied")
        emb_stored = [sem(f"emb_stored{i}") for i in range(2)]
        zeros_stored = sem("zeros_stored")
        h_loaded = sem("h_loaded")
        h_filled = sem("h_filled")
        out_stored = sem("out_stored")
        var_ready = sem("var_ready")
        rstd_ready = sem("rstd_ready")
        ln_ready = sem("ln_ready")
        vec_step = sem("vec_step")
        pool_step = sem("pool_step")
        qg_ready = sem("qg_ready")
        max_ready = [sem(f"max_ready{i}") for i in range(3)]
        probs_ready = [sem(f"probs_ready{i}") for i in range(3)]
        qg2_ready = sem("qg2_ready")
        y_scaled = sem("y_scaled")
        rows_chosen = sem("rows_chosen")
        picked_ready = sem("picked_ready")
        logit_exp = sem("logit_exp")
        scattered = sem("scattered")
        experts_in = [sem(f"experts_in{i}") for i in range(3)]
        results_out = sem("results_out")
        gathered = [sem(f"gathered{i}") for i in range(2)]
        bias1_added = sem("bias1_added")
        g_mean_ready = sem("g_mean_ready")
        h2_ones = sem("h2_ones")
        bits_ready = sem("bits_ready")
        ffn_base = sem("ffn_base")
        out_added = sem("out_added")

        def slot(key_):
            return ps[UNIT[key_] % 4]

        def tiles(key_, n=HALF):
            return ps_flat[UNIT[key_] % 4][0:HT, 0:n * TS].rearrange("p (j d) -> p j d", d=TS)[:, :, 0:DIM]

        def filled(eng, g, key_):
            eng.wait_ge(psum_filled, g * len(UNITS) + (UNIT[key_] + 1))

        def emptied(eng, g, *keys, but=None):
            for s in range(4):
                n = max((UNIT[k] // 4 + 1 for k in keys if UNIT[k] % 4 == s), default=0)
                if n and s != but:
                    eng.wait_ge(psum_emptied[s], g * SLOT_USES[s] + (n + 1))

        def to_empty(key_):
            return psum_emptied[UNIT[key_] % 4]

        def mixed_out(g, eng, copy, which, t):
            at = at0[t // 2 % 3] if which == 0 else at2[t // 2 % 2]
            c0 = t % 2 * PN
            if which == 0 and t < 2:
                eng.wait_ge(h_filled, g * 16 + 16)
            for mh in range(2):
                if mh == 0:
                    filled(eng, g, (f"M{which}", t))
                ins = copy(at[:, mh, :, c0:c0 + PN].rearrange("p g n -> p n g"),
                           slot((f"M{which}", t))[0:T72, mh, 0:PN * HEADS].rearrange("p (n g) -> p n g", g=HEADS))
            ins.then_inc(to_empty((f"M{which}", t)), 1)

        def exp_tiles(g, act, which, t):
            act.wait_ge(max_ready[which], g * GB * PACKS + (t + 1))
            s = slot((f"S{which}", t))
            for i in range(PACK):
                ins = nc.scalar.activation(probs0[t % 3][0:RP, i, :], s[0:RP, i // 2, (i % 2) * TOK:(i % 2 + 1) * TOK],
                                           ACT.Exp, bias=negmax[t % 3][:, i:i + 1], accum_out=rowsum[t % 3][:, i:i + 1])
            ins.then_inc(to_empty((f"S{which}", t)), 1)

        def exp_pair(g, act, which, s):
            act.wait_ge(max_ready[which], g * STEPS + (s + 1))
            name = "S1"
            for i in range(4):
                ins = nc.scalar.activation(p12[s % 3][:, i // 2, i % 2, :],
                                           slot((name, s))[0:T72, i // 2, (i % 2) * TOK:(i % 2 + 1) * TOK], ACT.Exp,
                                           bias=negmax[s % 3][0:T72, i:i + 1], accum_out=rowsum[s % 3][0:T72, i:i + 1])
            ins.then_inc(to_empty((name, s)), 1)

        block = ctx.enter_context(nc.Block())

        @block.sync
        def _(sp):
            sp.dma_start(emb_w, a["tok_w"]).then_inc(w_tok, 16)
            x_v = a["x"].rearrange("b (hp ph) (wp pc) -> (b hp) wp ph pc", ph=16, wp=4)
            for t in range(2):
                for wp in range(4):
                    sp.dma_start(emb_x[t][wp * 32:wp * 32 + 32].rearrange("p a b -> p (a b)").rearrange("p (ph pc) -> p ph pc", ph=16),
                                 x_v[t * 32:t * 32 + 32, wp]).then_inc(patches_in[t], 16)
            for wp in range(4):
                sp.dma_start(emb_bias[wp * 32:wp * 32 + 32], a["pos"][:, wp]).then_inc(w_tok, 16)
            sp.dma_start(emb_b, a["tok_b"].to_broadcast([128, DIM])).then_inc(w_tok, 16)
            for j in range(6):
                for hf in range(2):
                    sp.dma_start(mix_in[16 * j:16 * j + 16, hf, :],
                                 a["proj_l_w"][6 * hf + j:6 * hf + j + 1, :].to_broadcast([16, HEADS])).then_inc(w_l0, 16)
            sp.dma_start(qkv0_w[:], a["qkv0_w"]).then_inc(w_l0, 16)
            sp.dma_start(proj0_w[0:HT], a["proj0_w"]).then_inc(w_l0, 16)
            sp.dma_start(proj0_w[HT:HT + 1, 0, :], a["proj0_b"]).then_inc(w_l0, 16)
            sp.dma_start(coef_y[:], a["lamb"].to_broadcast([HT, HEADS])).then_inc(w_l0, 16)
            sp.dma_start(coef_z[:], a["lamb"].to_broadcast([HT, HEADS])).then_inc(w_l0, 16)
            for i in range(3):
                for hf in range(2):
                    sp.dma_start(qg0[i][HT:HT + 1, hf, :].rearrange("p (n g) -> p n g", g=HEADS),
                                 a["proj_l_b"].rearrange("o (n g) -> o n g", n=1).to_broadcast([1, PN, HEADS])).then_inc(w_l0, 16)
            sp.wait_ge(mix_zeroed, 1)
            for n in range(RN):
                sp.dma_start(mix_out[n * HEADS:(n + 1) * HEADS, n * HEADS:(n + 1) * HEADS], a["proj_w_w"]).then_inc(w_l0, 16)
            sp.dma_start(mix_out[RP:RP + 1, :].rearrange("p (n g) -> p n g", g=HEADS),
                         a["proj_w_b"].rearrange("o (n g) -> o n g", n=1).to_broadcast([1, RN, HEADS])).then_inc(w_l0, 16)
            sp.wait_ge(ones_set, 1)
            for i in range(3):
                sp.dma_start(probs0[i][RP:RP + 1].rearrange("p a b -> p (a b)"),
                             ones_row).then_inc(w_l0, 16)
            with sp.Fori(1, E_TILES // 2) as i:
                for t in range(2):
                    sp.wait_ge(emb_filled, i * 4 + (2 * t - 3))
                    for wp in range(4):
                        sp.dma_start(emb_x[t][wp * 32:wp * 32 + 32].rearrange("p a b -> p (a b)").rearrange("p (ph pc) -> p ph pc", ph=16),
                                     x_v[bass.ds(i * 64 + t * 32, 32), wp]).then_inc(patches_in[t], 16)
            out_v = out.rearrange("(g j p) d -> g p j d", g=GROUPS, p=HT)
            img_v = img_rows.rearrange("(g c b) t d -> g b t c d", g=GROUPS, b=2)
            txt_v = a["txt"].rearrange("(g c b) t d -> g b t c d", g=GROUPS, b=2)
            exp_v = expert_rows.rearrange("(c p) d -> p c d", p=SLOT_P)
            for t in range(2):
                sp.wait_ge(emb_stored[t], 16 * 4 * E_TILES // 2)

            def load(g):
                hv = tm_x.rearrange("p (c j) d -> p c j d", c=2)
                sp.dma_start(hv[0:16, :, 0], img_v[g, 0]).then_inc(h_loaded, 16)
                sp.dma_start(hv[16:96, :, 0], txt_v[g, 0, 0:80]).then_inc(h_loaded, 16)
                sp.dma_start(hv[0:48, :, 1], txt_v[g, 0, 80:128]).then_inc(h_loaded, 16)
                sp.dma_start(hv[48:64, :, 1], img_v[g, 1]).then_inc(h_loaded, 16)
                sp.dma_start(hv[64:96, :, 1], txt_v[g, 1, 0:32]).then_inc(h_loaded, 16)
                sp.dma_start(hv[0:96, :, 2], txt_v[g, 1, 32:128]).then_inc(h_loaded, 16)

            def experts(g):
                sp.wait_ge(scattered, g * 192 + 192)
                filled(sp, g, ("LN", 1, 1))
                for i in range(3):
                    sp.dma_start(xe_tok[:, 4 * i:4 * i + 4], exp_v[:, 4 * i:4 * i + 4]).then_inc(experts_in[i], 16)
                for e in range(EXPERTS):
                    emptied(sp, g, ("EO", e))
                    sp.dma_start(result_rows[e * CAP:(e + 1) * CAP].rearrange("(c p) d -> p c d", c=2),
                                 eo[:, 2 * e:2 * e + 2]).then_inc(results_out, 16)

            def store(g):
                emptied(sp, g, ("UP", 0), ("UP", 1))
                sp.dma_start(out_v[g], h[:]).then_inc(out_stored, 16)

            def fill_h(g):
                sp.wait_ge(h_loaded, g * 96 + 96)
                sp.dma_start(h[:], tm_x).then_inc(h_filled, 16)

            load(0)
            fill_h(0)
            with sp.Fori(0, GROUPS - 1) as g:
                experts(g)
                filled(sp, g, ("DT", 1))
                load(g + 1)
                store(g)
                sp.wait_ge(out_stored, g * 16 + 16)
                fill_h(g + 1)
            experts(GROUPS - 1)
            store(GROUPS - 1)
            sp.wait_ge(out_stored, GROUPS * 16)
            sp.wait_ge(results_out, GROUPS * EXPERTS * 16)

        @block.gpsimd
        def _(pool):
            done = [0]

            def link(ins):
                ins.then_inc(pool_setup, 1)
                done[0] += 1
                pool.wait_ge(pool_setup, done[0])

            nc.gpsimd.memset(mix_out[:], 0.0).then_inc(mix_zeroed, 1)
            nc.gpsimd.memset(own_head[:], float(D0) ** -0.5)
            nc.gpsimd.memset(ident[:], 0.0)
            nc.gpsimd.memset(ident_bf[:], 0.0)
            nc.gpsimd.memset(diag_bf[:], 0.0)
            nc.gpsimd.memset(ones_bf[:], 1.0)
            nc.gpsimd.memset(before_bf[:], 1.0)
            nc.gpsimd.memset(reserved[:], 0.0)
            nc.gpsimd.memset(eps_pow[:], -0.5)
            link(nc.gpsimd.memset(zero_rows, 0.0))
            nc.gpsimd.affine_select(out=ident[:], in_=ident[:], compare_op=ALU.not_equal, fill=1.0, base=0,
                                    pattern=[[-1, 128]], channel_multiplier=1)
            nc.gpsimd.affine_select(out=ident_bf[:], in_=ident_bf[:], compare_op=ALU.not_equal, fill=1.0, base=0,
                                    pattern=[[-1, T72]], channel_multiplier=1)
            nc.gpsimd.affine_select(out=diag_bf[:], in_=diag_bf[:], compare_op=ALU.not_equal, fill=MASKED, base=0,
                                    pattern=[[T72, 2], [-1, TOK]], channel_multiplier=1)
            nc.gpsimd.affine_select(out=before_bf[:], in_=before_bf[:], compare_op=ALU.is_gt, fill=0.0, base=0,
                                    pattern=[[1, HT]], channel_multiplier=-1)
            oh = own_head[:]
            nc.gpsimd.affine_select(out=oh, in_=oh, compare_op=ALU.is_ge, fill=0.0, base=0,
                                    pattern=[[HT, 2], [-D0, HEADS]], channel_multiplier=1)
            rv = reserved[:].rearrange("p (c j) -> p c j", c=2)
            nc.gpsimd.affine_select(out=rv[:, :, 0:2], in_=rv[:, :, 0:2], compare_op=ALU.not_equal, fill=1.0, base=0,
                                    pattern=[[0, 2], [-48, 2]], channel_multiplier=1)
            nc.gpsimd.iota(first_e[:], pattern=[[-1, EXPERTS]], base=EXPERTS, channel_multiplier=0,
                           allow_small_or_imprecise_dtypes=True)
            link(nc.gpsimd.iota(base_e[:], pattern=[[CAP, EXPERTS]], base=0, channel_multiplier=0,
                                allow_small_or_imprecise_dtypes=True))
            nc.gpsimd.affine_select(out=oh, in_=oh, compare_op=ALU.is_ge, fill=0.0, base=D0 - 1,
                                    pattern=[[-HT, 2], [D0, HEADS]], channel_multiplier=-1)
            pool.dma_start(expert_rows.rearrange("(c p) d -> p c d", p=SLOT_P), zero_rows).then_inc(zeros_stored, 16)
            pool.dma_start(result_rows[SLOTS:SLOTS + 1], zero_rows[0:1, 0, :]).then_inc(zeros_stored, 16)
            pool.wait_ge(zeros_stored, 32)
            nc.gpsimd.memset(fm_o[HT:HT + 1], 1.0)
            link(nc.gpsimd.memset(k0[HT:HT + 1], 1.0))
            pool.dma_start(router_w[:], a["router_w"]).then_inc(w_moe, 16)
            for e in range(EXPERTS):
                pool.dma_start(moe_wi[:, :, e], a["moe_wi"][e]).then_inc(w_moe, 16)
                pool.dma_start(moe_wo[:, e], a["moe_wo"][e]).then_inc(w_moe, 16)
            pool.dma_start(qkv1_w[:], a["qkv1_w"]).then_inc(w_l1, 16)
            for j in range(2):
                pool.dma_start(scale1[64 * j:64 * j + 64], a["scale1"][j:j + 1].to_broadcast([64, 6])).then_inc(w_l1, 16)
            pool.dma_start(proj1_w[:], a["proj1_w"]).then_inc(w_l1, 16)
            pool.dma_start(bias1[:], a["bias1"].to_broadcast([HT, DIM])).then_inc(w_l1, 16)
            for t_, n in ((wq2[:], "wq2"), (wk2[:], "wk2"), (bq2[:], "bq2"), (bk2[:], "bk2"), (wv2[:], "wv2"), (wo2[0:HT], "wo2"), (wo2[HT:HT + 1, 0, :], "bo2"), (ln_gb[:], "ln_gb"),
                          (fc1_w[:], "fc1_w"), (fc1_b[:], "fc1_b"), (fc2_w[:], "fc2_w"), (r_in_w[:], "r_in_w"),
                          (r_o1_w[:], "r_o1_w"), (r_o2_w[:], "r_o2_w"), (r_o3_w[:], "r_o3_w"),
                          (r_b[:, 0:2], "r_b"), (r_b[0:RHD // 2, 2:3], "r_o2_b"), (lra_dn[:], "lra_dn"), (lra_up[:], "lra_up")):
                pool.dma_start(t_, a[n]).then_inc(w_ffn, 16)
            pool.dma_start(bv2[:], a["bv2"].to_broadcast([T72, DIM])).then_inc(w_ffn, 16)
            pool.dma_start(fc2_b[:], a["fc2_b"].to_broadcast([HT, DIM])).then_inc(w_ffn, 16)

            last_slot = pool.to_reg(SLOTS - 1)
            zero_row = pool.to_reg(SLOTS)
            with pool.Fori(0, GROUPS) as g:
                n_ln = [0]

                def rsqrt():
                    for part in range(2):
                        n_ln[0] += 1
                        pool.wait_ge(var_ready, g * 12 + n_ln[0])
                        c = slice(HALF * part, HALF * part + HALF)
                        nc.gpsimd.tensor_tensor(rstd[:, c], var_eps[:, c], eps_pow[:, c], ALU.pow).then_inc(rstd_ready, 1)

                def expand(which, t):
                    if t >= 3:
                        filled(pool, g, (f"S{which}", t - 3))
                    elif t == 0:
                        emptied(pool, g, (f"Q{which}", 0), (f"Q{which}", 1))
                    c0 = t * PN
                    for hf in range(2):
                        ins = nc.gpsimd.tensor_tensor(
                            qg0[t % 3][0:HT, hf, :].rearrange("p (n g) -> p n g", g=HEADS),
                            (q0 if which == 0 else q2)[:, hf, c0:c0 + PN].unsqueeze(2).to_broadcast([HT, PN, HEADS]),
                            (mix_in if which == 0 else own_head)[:, hf, :].unsqueeze(1).to_broadcast([HT, PN, HEADS]), ALU.mult)
                    ins.then_inc(qg_ready if which == 0 else qg2_ready, 1)

                rsqrt()
                pool.wait_ge(mix_ready, 1)
                for t in range(GB * PACKS + 7):
                    if t < GB * PACKS:
                        expand(0, t)
                    if t >= 10 and t % 4 == 2:
                        b = (t - 10) // 4
                        emptied(pool, g, ("Y0", 2 * b), ("Y0", 2 * b + 1))
                        nc.gpsimd.tensor_tensor(u0_t, y0_t, feature_y[:].unsqueeze(2).to_broadcast([HT, 2, TOK]), ALU.mult)\
                            .then_inc(y_scaled, 1)
                rsqrt()
                pool.wait_ge(rows_chosen, g + 1)
                nc.gpsimd.tensor_tensor(idle[:], eps_pow[:], eps_pow[:], ALU.add)
                for j in range(NT):
                    for k in range(2):
                        pool.indirect_dma_start(
                            expert_rows[:, :], bass.IndirectOffsetOnAxis(ap=row_idx[:, j, k:k + 1], axis=0),
                            tm_x[:, j, :], None, bounds_check=last_slot, oob_is_err=False).then_inc(scattered, 16)
                pool.wait_ge(results_out, g * EXPERTS * 16 + EXPERTS * 16)
                nc.gpsimd.tensor_tensor(idle2[:], eps_pow[:], eps_pow[:], ALU.add)
                for j in range(NT):
                    for k in range(2):
                        pool.indirect_dma_start(
                            back[:, j, k * DIM:(k + 1) * DIM], None,
                            result_rows[:, :], bass.IndirectOffsetOnAxis(ap=row_idx[:, j, k:k + 1], axis=0),
                            bounds_check=zero_row, oob_is_err=False).then_inc(gathered[j // HALF], 16)
                rsqrt()
                pool.wait_ge(ln_ready, g * 12 + 6)
                pool.wait_ge(w_l1, 80)
                nc.gpsimd.tensor_tensor(h[:], h[:], bias1[:].unsqueeze(1).to_broadcast([HT, NT, DIM]), ALU.add)\
                    .then_inc(bias1_added, 1)
                rsqrt()
                rsqrt()
                for t in range(GB * PACKS):
                    expand(2, t)
                rsqrt()
                filled(pool, g, ("LN", 5, 1))
                pool.wait_ge(bits_ready, g + 1)
                nc.gpsimd.tensor_tensor(tm_x, bits[:, :, 1:2].to_broadcast([HT, NT, DIM]),
                                        fc2_b[:].unsqueeze(1).to_broadcast([HT, NT, DIM]), ALU.mult).then_inc(pool_step, 1)
                pool.wait_ge(pool_step, g + 1)
                nc.gpsimd.tensor_tensor(tm_x, tm_x, tm_z, ALU.add).then_inc(ffn_base, 1)
                emptied(pool, g, ("F2", 1))
                emptied(pool, g, ("F2", 0))
                nc.gpsimd.tensor_tensor(h[:], h[:], tm_z, ALU.add).then_inc(out_added, 1)

        @block.scalar
        def _(act):
            act.wait_ge(pool_setup, 3)

            def table_for(func):
                nc.scalar.activation(table_out[:], eps_pow[:], func)

            img_t = img_rows.rearrange("b (hp wp) d -> (b hp) wp d", wp=4)
            with act.Fori(0, E_TILES // 2) as i:
                for t in range(2):
                    act.wait_ge(emb_emptied, i * 4 + (2 * t + 2))
                    for wp in range(4):
                        act.dma_start(img_t[bass.ds(i * 64 + t * 32, 32), wp], emb_out[t][wp * 32:wp * 32 + 32])\
                            .then_inc(emb_stored[t], 16)
            with act.Fori(0, GROUPS) as g:
                def copy(key_, out_, in_):
                    filled(act, g, key_)
                    nc.scalar.copy(out_, in_).then_inc(to_empty(key_), 1)

                c288 = lambda key_, m: slot(key_)[0:m, :, 0:CH]
                fm = lambda buf, hf: buf[0:HT, hf].rearrange("p (c n) -> p c n", c=2)
                def chunk(key_, c):
                    copy(key_, fm_x[:, :, c * CH:(c + 1) * CH], slot(key_)[0:HT, :, 0:CH])

                def mixed(which):
                    for t in range(GB * PACKS + 2):
                        if t < GB * PACKS:
                            exp_tiles(g, act, which, t)
                        if t >= 2 and t % 2 == 0:
                            mixed_out(g, act, nc.scalar.copy, which, t - 2)

                chunk(("LN", 0, 1), 1)
                copy(("V0", 1), v0[:, 4:8].rearrange("p (c j) d -> p c (j d)", c=2),
                     slot(("V0", 1))[0:T72, :, 0:2 * DIM])
                copy(("Q0", 1), fm(q0, 1), c288(("Q0", 1), HT))
                copy(("K0", 1), fm(k0, 1), c288(("K0", 1), HT))
                mixed(0)
                chunk(("LN", 1, 1), 1)
                emptied(act, g, ("LG",))
                nc.scalar.activation(lg2[:], lg[:], ACT.Exp).then_inc(logit_exp, 1)
                copy(("XT", 1), xe[:, :, 480:960], slot(("XT", 1))[0:HT, :, 0:480])
                for e in range(EXPERTS):
                    filled(act, g, ("H", e, 0))
                    nc.scalar.activation(hid[e % 2][:, 0:4].rearrange("p (c j) n -> p c (j n)", c=2),
                                         slot(("H", e, 0))[:, :, 0:2 * CAP], ACT.Relu).then_inc(to_empty(("H", e, 0)), 1)
                chunk(("LN", 2, 1), 1)
                for s in range(STEPS + 3):
                    if s % 4 == 0 and s < STEPS:
                        hp = s // 4
                        copy(("K1", hp), k1[hp % 2].rearrange("p (c n) -> p c n", c=2), c288(("K1", hp), 128))
                    if s < STEPS:
                        exp_pair(g, act, 1, s)
                    if 2 <= s < STEPS + 2 and s % 2 == 0:
                        copy(("T1", s - 2), pt1[s % 2].rearrange("p a b n -> p a (b n)"), c288(("T1", s - 2), T72))
                table_for(ACT.Gelu)

                def affine(key_, dst, c, gain, last):
                    for hf in range(2):
                        ins = nc.scalar.activation(dst[0:HT, hf, c * CH:(c + 1) * CH], slot(key_)[0:HT, hf, 0:CH], ACT.Identity,
                                                   bias=ln_gb[:, hf, gain + 1:gain + 2], scale=ln_gb[:, hf, gain:gain + 1])
                    if last:
                        ins.then_inc(to_empty(key_), 1)

                filled(act, g, ("LN", 4, 1))
                affine(("LN", 4, 1), fm_r, 1, 4, False)
                affine(("LN", 4, 1), fm_x, 1, 0, True)
                filled(act, g, ("E1",))
                nc.scalar.activation(e_t.rearrange("p (c n) -> p c n", c=2), c288(("E1",), RHD), ACT.Gelu,
                                     bias=r_b[:, 0:1]).then_inc(to_empty(("E1",)), 1)
                filled(act, g, ("H1",))
                emptied(act, g, ("GC",))
                for b in range(GB):
                    ins = nc.scalar.activation(h1_t[:, b * TOK:(b + 1) * TOK],
                                               slot(("H1",))[:, b // 2, (b % 2) * TOK:(b % 2 + 1) * TOK], ACT.Gelu,
                                               bias=g_bias[:, b:b + 1])
                ins.then_inc(to_empty(("H1",)), 1)
                filled(act, g, ("H2",))
                nc.scalar.activation(h2_t[0:RHD // 2].rearrange("p (c n) -> p c n", c=2), c288(("H2",), RHD // 2),
                                     ACT.Gelu, bias=r_b[0:RHD // 2, 2:3]).then_inc(to_empty(("H2",)), 1)
                table_for(ACT.Exp)
                for half in range(2):
                    filled(act, g, ("K2", half))
                    nc.scalar.activation(fm(k2, half), c288(("K2", half), HT), ACT.Identity,
                                         bias=bk2[:, half:half + 1]).then_inc(to_empty(("K2", half)), 1)
                mixed(2)
                table_for(ACT.Gelu)
                filled(act, g, ("LN", 5, 1))
                affine(("LN", 5, 1), fm_x, 1, 2, True)
                for i in range(FT):
                    filled(act, g, ("F1", i))
                    nc.scalar.activation(ff[:, i].rearrange("p (c n) -> p c n", c=2), c288(("F1", i), 128), ACT.Gelu,
                                         bias=fc1_b[:, i:i + 1]).then_inc(to_empty(("F1", i)), 1)
                table_for(ACT.Exp)
                chunk(("OUT", 1), 1)
                copy(("DT", 1), fm_o[0:HT, :, CH:2 * CH], slot(("DT", 1))[0:HT, :, 0:CH])

        @block.vector
        def _(dve):
            done = [0]

            def link_setup(ins):
                ins.then_inc(vec_setup, 1)
                done[0] += 1
                dve.wait_ge(vec_setup, done[0])

            nc.vector.memset(ones_row, 1.0).then_inc(ones_set, 1)
            dve.wait_ge(w_tok, 96)
            link_setup(nc.vector.tensor_tensor(emb_bias, emb_bias, emb_b, ALU.add))
            for s in range(4):
                nc.vector.memset(negmax[0][:, s:s + 1], 0.0).then_inc(psum_emptied[s], 1)
            with dve.Fori(0, E_TILES // 2) as i:
                for t in range(2):
                    for hf in range(2):
                        dve.wait_ge(emb_filled, i * 4 + (2 * t + 1))
                        ins = nc.vector.tensor_copy(emb_xt[:, 3 * hf:3 * hf + 3], ps[0][:, hf, 0:384].rearrange("p (a b) -> p a b", a=3))
                    ins.then_inc(emb_emptied, 1)
                    dve.wait_ge(emb_filled, i * 4 + (2 * t + 2))
                    nc.vector.tensor_tensor(emb_out[t], ps[1][:, 0, 0:DIM], emb_bias, ALU.add).then_inc(emb_emptied, 1)
                for t in range(2):
                    dve.wait_ge(emb_stored[t], i * 64 + 64)
            dve.wait_ge(w_l0, W_L0)
            link_setup(nc.vector.tensor_scalar(coef_y[:], coef_y[:], -2.0, 1.0, ALU.mult, ALU.add))
            link_setup(nc.vector.tensor_scalar(coef_z[:], coef_z[:], 3.0, None, ALU.mult))
            dve.wait_ge(pool_setup, 3)
            for values_, sums, dims in ((coef_y, feature_y, None), (coef_z, feature_z, "p f (a e) -> p f e a"),
                                        (None, parity, "p f (a e) -> p f e a")):
                if values_ is None:
                    source = own_head
                else:
                    source = by_head
                    link_setup(nc.vector.tensor_tensor(by_head[:], own_head[:],
                                                       values_[:].unsqueeze(1).to_broadcast([HT, 2, HEADS]), ALU.mult))
                link_setup(nc.vector.tensor_reduce(sums[:], source[:].rearrange(dims, e=2) if dims else source[:], AX.X, ALU.add))
                link_setup(nc.vector.tensor_scalar(sums[:], sums[:], float(D0) ** 0.5, None, ALU.mult))
            nc.vector.tensor_scalar(mix_in[:], mix_in[:], float(D0) ** -0.5, None, ALU.mult).then_inc(mix_ready, 1)

            with dve.Fori(0, GROUPS) as g:
                n_step = [0]
                n_ln = [0]

                def link(ins):
                    n_step[0] += 1
                    ins.then_inc(vec_step, 1)
                    dve.wait_ge(vec_step, g * VEC_STEPS + n_step[0])

                def ln_stats(src, part):
                    c = slice(HALF * part, HALF * part + HALF)
                    for j in TILES_OF[part]:
                        ins = nc.vector.bn_stats(stats[:, j, :], src[:, j, :])
                    link(ins)
                    even, odd = stats[:, c, 0:3], stats[:, c, 3:6]
                    nc.vector.tensor_tensor(mean2[:, c], even[:, :, 1], odd[:, :, 1], ALU.add)
                    nc.vector.tensor_tensor(diff[:, c], even[:, :, 1], odd[:, :, 1], ALU.subtract)
                    link(nc.vector.tensor_tensor(var[:, c], even[:, :, 2], odd[:, :, 2], ALU.add))
                    nc.vector.tensor_scalar(mean[:, c], mean2[:, c], 0.5, None, ALU.mult)
                    nc.vector.tensor_scalar(var2[:, c], var[:, c], 1.0 / DIM, EPS, ALU.mult, ALU.add)
                    link(nc.vector.scalar_tensor_tensor(diff2[:, c], diff[:, c], 0.25, diff[:, c], ALU.mult, ALU.mult))
                    nc.vector.tensor_tensor(var_eps[:, c], var2[:, c], diff2[:, c], ALU.add).then_inc(var_ready, 1)

                def ln_apply(src, dst, part):
                    n_ln[0] += 1
                    dve.wait_ge(rstd_ready, g * 12 + n_ln[0])
                    for j in TILES_OF[part]:
                        ins = nc.vector.tensor_scalar(dst[:, j, :], src[:, j, :], mean[:, j:j + 1], rstd[:, j:j + 1],
                                                      ALU.subtract, ALU.mult)
                    ins.then_inc(ln_ready, 1)

                def layernorm(src, dst):
                    for part in range(2):
                        ln_stats(src, part)
                    for part in range(2):
                        ln_apply(src, dst, part)

                c288 = lambda key_, m: slot(key_)[0:m, :, 0:CH]
                fm = lambda buf, hf: buf[0:HT, hf].rearrange("p (c n) -> p c n", c=2)

                def copy(key_, out_, in_):
                    filled(dve, g, key_)
                    nc.vector.tensor_copy(out_, in_).then_inc(to_empty(key_), 1)

                def add_to(key_, i, dst, base):
                    filled(dve, g, key_)
                    c = slice(HALF * i, HALF * i + HALF)
                    nc.vector.tensor_tensor(dst[:, c], tiles(key_), base[:, c], ALU.add).then_inc(to_empty(key_), 1)

                def accumulate(name, i):
                    add_to((name, i), i, h, h)
                    emptied(dve, g, (name, i))
                    ln_stats(h, i)

                def chunk(key_, c):
                    copy(key_, fm_x[:, :, c * CH:(c + 1) * CH], slot(key_)[0:HT, :, 0:CH])

                def gated(name, bit, base):
                    for i in range(2):
                        filled(dve, g, (name, i))
                        for j in TILES_OF[i]:
                            ins = nc.vector.scalar_tensor_tensor(tm_z[:, j, :], tiles((name, i))[:, j % HALF], bits[:, j, bit:bit + 1],
                                                                 base[:, j, :], ALU.mult, ALU.add)
                        ins.then_inc(to_empty((name, i)), 1)
                        if name == "P2":
                            emptied(dve, g, (name, i))
                            ln_stats(tm_z, i)

                def mixed(which):
                    def own_rows(key_, dst, coef, base=None):
                        filled(dve, g, key_)
                        n = dst.shape[2]
                        src = slot(key_)[0:HT, :, 0:2 * n].rearrange("p f (e n) -> p f e n", e=2)
                        if base is None:
                            link(nc.vector.tensor_scalar(dst, src[:, :, 0], coef[:, 0, 0:1], None, ALU.mult))
                            ins = nc.vector.scalar_tensor_tensor(dst, src[:, :, 1], coef[:, 0, 1:2], dst, ALU.mult, ALU.add)
                        else:
                            for hf in range(2):
                                ins = nc.vector.scalar_tensor_tensor(base[:, hf], src[:, hf, 0], coef[:, hf, 0:1], base[:, hf],
                                                                     ALU.mult, ALU.add)
                            link(ins)
                            for hf in range(2):
                                ins = nc.vector.scalar_tensor_tensor(dst[:, hf], src[:, hf, 1], coef[:, hf, 1:2], base[:, hf],
                                                                     ALU.mult, ALU.add)
                        ins.then_inc(to_empty(key_), 1)

                    for t in range(GB * PACKS + (5 if which == 0 else 4)):
                        if which == 0 and t >= 8 and t % 4 == 0:
                            b = (t - 8) // 4
                            copy(("YT", b), y0, slot(("YT", b))[0:T72, :, 0:DIM])
                        if t < GB * PACKS:
                            filled(dve, g, (f"S{which}", t))
                            nc.vector.tensor_reduce(negmax[t % 3][:].rearrange("p (a b) -> p a b", a=2),
                                                    slot((f"S{which}", t))[0:RP, :, 0:CH].rearrange("p a (b n) -> p a b n", b=2),
                                                    AX.X, ALU.max, negate=True).then_inc(max_ready[which], 1)
                        if 1 <= t <= GB * PACKS:
                            emptied(dve, g, (f"S{which}", t - 1))
                            link(nc.vector.reciprocal(rinv[(t - 1) % 3][:], rowsum[(t - 1) % 3][:]))
                            e = probs0[(t - 1) % 3][0:RP]
                            nc.vector.tensor_tensor(e, e, rinv[(t - 1) % 3][:].unsqueeze(2).to_broadcast([RP, PACK, TOK]),
                                                    ALU.mult).then_inc(probs_ready[which], 1)
                        if t >= 5 and t % 2 == 1 and t < GB * PACKS + 4:
                            b, nh = divmod((t - 5) // 2, 2)
                            dst = (y0_t[:, :, nh * T72:(nh + 1) * T72] if which == 0 else
                                   fm_o[0:HT, :, b * TOK + nh * T72:b * TOK + (nh + 1) * T72])
                            own_rows((f"Y{which}", 2 * b + nh), dst, parity)
                        if which == 0 and t >= 8 and t % 4 == 0:
                            b = (t - 8) // 4
                            dve.wait_ge(y_scaled, g * GB + (b + 1))
                            own_rows(("Z0", b), fm_o[0:HT, :, b * TOK:(b + 1) * TOK], feature_z, u0_t)
                        if 2 <= t < GB * PACKS + 2 and t % 2 == 1:
                            mixed_out(g, dve, nc.vector.tensor_copy, which, t - 2)
                        if which == 0 and t == 14:
                            accumulate("P0", 0)

                dve.wait_ge(h_loaded, g * 96 + 96)
                layernorm(tm_x, tm_z)
                chunk(("LN", 0, 0), 0)
                copy(("V0", 0), v0[:, 0:4].rearrange("p (c j) d -> p c (j d)", c=2), slot(("V0", 0))[0:T72, :, 0:2 * DIM])
                copy(("Q0", 0), fm(q0, 0), c288(("Q0", 0), HT))
                copy(("K0", 0), fm(k0, 0), c288(("K0", 0), HT))
                mixed(0)
                accumulate("P0", 1)
                for part in range(2):
                    ln_apply(h, tm_x, part)

                chunk(("LN", 1, 0), 0)
                filled(dve, g, ("LG",))
                logits = slot(("LG",))[0:HT, 0, 0:NT * EXPERTS].rearrange("p (j e) -> p j e", e=EXPERTS)
                link(nc.vector.tensor_reduce(lgm[:], logits, AX.X, ALU.max))
                wide = lambda v: v.unsqueeze(2).to_broadcast([HT, NT, EXPERTS])
                nc.vector.tensor_tensor(lg[:], logits, wide(lgm[:]), ALU.subtract).then_inc(to_empty(("LG",)), 1)
                dve.wait_ge(logit_exp, g + 1)
                link(nc.vector.tensor_reduce(lgs[:], lg2[:], AX.X, ALU.add))
                link(nc.vector.reciprocal(lgs[:], lgs[:]))
                link(nc.vector.tensor_tensor(lg2[:], lg2[:], wide(lgs[:]), ALU.mult))
                by_e = lambda v: v.unsqueeze(1).to_broadcast([HT, NT, EXPERTS])
                for k in range(2):
                    link(nc.vector.tensor_reduce(gate[:, :, k], lg2[:], AX.X, ALU.max))
                    link(nc.vector.tensor_tensor(lg[:], lg2[:], wide(gate[:, :, k]), ALU.is_equal))
                    link(nc.vector.tensor_tensor(lg[:], lg[:], by_e(first_e[:]), ALU.mult))
                    link(nc.vector.tensor_reduce(key[:], lg[:], AX.X, ALU.max))
                    link(nc.vector.tensor_tensor(picked[:, :, k, :], lg[:], wide(key[:]), ALU.is_equal))
                    if k == 0:
                        link(nc.vector.scalar_tensor_tensor(lg2[:], picked[:, :, 0, :], -2.0, lg2[:], ALU.mult, ALU.add))
                nc.vector.tensor_copy(picked_bf[:], picked[:].rearrange("p j k e -> p j (k e)")).then_inc(picked_ready, 1)
                filled(dve, g, ("CT",))
                counts = slot(("CT",))[0:HT, 0, 0:NT * 2 * EXPERTS].rearrange("p (j k e) -> p j k e", k=2, e=EXPERTS)
                nc.vector.tensor_tensor(place[:], counts, picked[:], ALU.mult).then_inc(to_empty(("CT",)), 1)
                emptied(dve, g, ("CT",))
                link(nc.vector.tensor_reduce(pos[:], place[:], AX.X, ALU.add))
                for k in range(2):
                    ins = nc.vector.tensor_tensor(place[:, :, k], picked[:, :, k], by_e(base_e[:]), ALU.mult)
                link(ins)
                link(nc.vector.tensor_reduce(row_of[:], place[:], AX.X, ALU.add))
                link(nc.vector.tensor_tensor(row_of[:], row_of[:], pos[:], ALU.add))
                link(nc.vector.tensor_scalar(pos[:], pos[:], float(CAP) - 0.5, float(2 * SLOTS), ALU.is_gt, ALU.mult))
                link(nc.vector.tensor_tensor(row_of[:], row_of[:], pos[:], ALU.add))
                nc.vector.tensor_scalar(row_idx[:], row_of[:], float(SLOTS), None, ALU.min).then_inc(rows_chosen, 1)

                for i in (0, 2):
                    copy(("XT", i), xe[:, :, 480 * i:480 * i + 480], slot(("XT", i))[0:HT, :, 0:480])
                for e in range(EXPERTS + 1):
                    if e < EXPERTS:
                        filled(dve, g, ("H", e, 1))
                        nc.vector.tensor_scalar(hid[e % 2][:, 4:6].rearrange("p j n -> p (j n)"),
                                                slot(("H", e, 1))[:, 0, 0:2 * CAP], 0.0, None, ALU.max)\
                            .then_inc(to_empty(("H", e, 1)), 1)
                    if e >= 1:
                        copy(("EO", e - 1), eo[:, 2 * e - 2:2 * e].rearrange("p c d -> p (c d)"),
                             slot(("EO", e - 1))[0:CAP // 2, 0, 0:2 * DIM])
                for part in range(2):
                    dve.wait_ge(gathered[part], g * 96 + 96)
                    for k in range(2):
                        for j in TILES_OF[part]:
                            ins = nc.vector.scalar_tensor_tensor(h[:, j, :], back[:, j, k * DIM:(k + 1) * DIM],
                                                                 gate[:, j, k:k + 1], h[:, j, :], ALU.mult, ALU.add)
                        link(ins)
                    ln_stats(h, part)
                for part in range(2):
                    ln_apply(h, tm_x, part)
                chunk(("LN", 2, 0), 0)

                def max_pair(which, s):
                    name = "S1" if which == 1 else "S2"
                    filled(dve, g, (name, s))
                    nc.vector.tensor_reduce(negmax[s % 3][0:T72].rearrange("p (a b) -> p a b", a=2),
                                            slot((name, s))[0:T72, :, 0:CH].rearrange("p a (b n) -> p a b n", b=2),
                                            AX.X, ALU.max, negate=True).then_inc(max_ready[which], 1)

                for s in range(STEPS + 3):
                    if s % 4 == 0 and s < STEPS:
                        hp = s // 4
                        filled(dve, g, ("Q1", hp))
                        nc.vector.tensor_scalar(q1[hp % 2].rearrange("p (c n) -> p c n", c=2), c288(("Q1", hp), 128),
                                                scale1[:, hp:hp + 1], None, ALU.mult).then_inc(to_empty(("Q1", hp)), 1)
                        filled(dve, g, ("V1", hp))
                        for c in range(2):
                            ins = nc.vector.tensor_copy(v1[hp % 2][:, 4 * c:4 * c + 4],
                                                        slot(("V1", hp))[0:T72, c, :].rearrange("p (j a d) -> p j a d", j=4, a=2))
                        ins.then_inc(to_empty(("V1", hp)), 1)
                    if s < STEPS:
                        max_pair(1, s)
                    if 1 <= s <= STEPS:
                        emptied(dve, g, ("S1", s - 1))
                        link(nc.vector.reciprocal(rinv[(s - 1) % 3][0:T72], rowsum[(s - 1) % 3][0:T72]))
                        e = p12[(s - 1) % 3].rearrange("p a b n -> p (a b) n")
                        nc.vector.tensor_tensor(e, e, rinv[(s - 1) % 3][0:T72].unsqueeze(2).to_broadcast([T72, 4, TOK]),
                                                ALU.mult).then_inc(probs_ready[1], 1)
                    if 2 <= s < STEPS + 2 and s % 2 == 1:
                        copy(("T1", s - 2), pt1[s % 2].rearrange("p a b n -> p a (b n)"), c288(("T1", s - 2), T72))
                    if s >= 3:
                        hp, b = divmod(s - 3, 4)
                        copy(("O1", s - 3), ot1[:, hp, b * TOK:(b + 1) * TOK], slot(("O1", s - 3))[:, 0, 0:TOK])
                dve.wait_ge(bias1_added, g + 1)
                for part in range(2):
                    accumulate("P1", part)
                for part in range(2):
                    ln_apply(h, tm_x, part)

                for part in range(2):
                    dve.wait_ge(ln_ready, g * 12 + (7 + part))
                    ln_stats(tm_x, part)
                for part in range(2):
                    ln_apply(tm_x, tm_z, part)
                def affine(key_, dst, c, gain, last):
                    for hf in range(2):
                        ins = nc.vector.tensor_scalar(dst[0:HT, hf, c * CH:(c + 1) * CH], slot(key_)[0:HT, hf, 0:CH],
                                                      ln_gb[:, hf, gain:gain + 1], ln_gb[:, hf, gain + 1:gain + 2],
                                                      ALU.mult, ALU.add)
                    if last:
                        ins.then_inc(to_empty(key_), 1)

                filled(dve, g, ("LN", 4, 0))
                affine(("LN", 4, 0), fm_r, 0, 4, False)
                affine(("LN", 4, 0), fm_x, 0, 0, True)

                def queries(half):
                    filled(dve, g, ("Q2", half))
                    nc.vector.tensor_scalar(fm(q2, half), c288(("Q2", half), HT), bq2[:, half:half + 1], None, ALU.add)\
                        .then_inc(to_empty(("Q2", half)), 1)

                def values(i):
                    filled(dve, g, ("V2", i))
                    for c in range(2):
                        ins = nc.vector.tensor_tensor(v2[:, 4 * i + 2 * c:4 * i + 2 * c + 2],
                                                      slot(("V2", i))[0:T72, c, 0:2 * DIM].rearrange("p (j d) -> p j d", j=2),
                                                      bv2[:].unsqueeze(1).to_broadcast([T72, 2, DIM]), ALU.add)
                    ins.then_inc(to_empty(("V2", i)), 1)

                queries(0)
                emptied(dve, g, ("E1",))
                link(nc.vector.tensor_reduce(g_mean[:], e_t.rearrange("p (b n) -> p b n", b=GB)[:, :, 1:TOK], AX.X, ALU.add))
                nc.vector.tensor_scalar(g_mean[:], g_mean[:], 1.0 / (TOK - 1), None, ALU.mult).then_inc(g_mean_ready, 1)
                queries(1)
                filled(dve, g, ("GC",))
                nc.vector.tensor_scalar(g_bias[:], slot(("GC",))[0:RHD, 0, 0:GB], r_b[:, 1:2], None, ALU.add)\
                    .then_inc(to_empty(("GC",)), 1)
                nc.vector.memset(h2_t[RHD // 2:RHD // 2 + 1, :], 1.0).then_inc(h2_ones, 1)
                values(0)
                values(1)
                copy(("RL",), rl[:].rearrange("p j a b -> p (j a b)"), slot(("RL",))[0:HT, 0, 0:4 * NT])
                emptied(dve, g, ("RL",))
                link(nc.vector.tensor_tensor(bits[:], rl[:, :, :, 1], rl[:, :, :, 0], ALU.is_gt))
                link(nc.vector.tensor_tensor(bits[:], bits[:], reserved[:].unsqueeze(2).to_broadcast([HT, NT, 2]), ALU.max))
                link(nc.vector.tensor_scalar(nbits[:], bits[:], -1.0, 1.0, ALU.mult, ALU.add))
                nc.vector.tensor_tensor(sel[:, :, 0], nbits[:, :, 0], nbits[:, :, 1], ALU.mult)
                nc.vector.tensor_tensor(sel[:, :, 1], nbits[:, :, 0], bits[:, :, 1], ALU.mult)
                nc.vector.tensor_tensor(sel[:, :, 2], bits[:, :, 0], nbits[:, :, 1], ALU.mult).then_inc(bits_ready, 1)
                mixed(2)
                gated("P2", 0, tm_x)
                for part in range(2):
                    ln_apply(tm_z, tm_x, part)
                filled(dve, g, ("LN", 5, 0))
                affine(("LN", 5, 0), fm_x, 0, 2, True)
                dve.wait_ge(ffn_base, g + 1)
                gated("F2", 1, tm_x)
                chunk(("OUT", 0), 0)
                for i in range(2):
                    filled(dve, g, ("DN", i))
                    for j in TILES_OF[i]:
                        ins = nc.vector.tensor_tensor(tm_x[:, j].rearrange("p (k r) -> p k r", k=3),
                                                      tiles(("DN", i))[:, j % HALF].rearrange("p (k r) -> p k r", k=3),
                                                      sel[:, j].unsqueeze(2).to_broadcast([HT, 3, RANK]), ALU.mult)
                    ins.then_inc(to_empty(("DN", i)), 1)
                copy(("DT", 0), fm_o[0:HT, :, 0:CH], slot(("DT", 0))[0:HT, :, 0:CH])
                dve.wait_ge(out_added, g + 1)
                add_to(("UP", 0), 0, h, h)
                add_to(("UP", 1), 1, h, h)
                assert n_step[0] == VEC_STEPS, n_step[0]

        @block.tensor
        def _(pe):
            pe.wait_ge(w_tok, 96)
            pe.wait_ge(pool_setup, 3)
            with pe.Fori(0, E_TILES // 2) as i:
                for t in range(2):
                    pe.wait_ge(patches_in[t], i * 64 + 64)
                    for c in range(6):
                        ins = nc.tensor.transpose(ps[0][:, c // 3, (c % 3) * 128:(c % 3 + 1) * 128], emb_x[t][:, c, :], ident[:])
                    ins.then_inc(emb_filled, 1)
                    pe.wait_ge(emb_emptied, i * 4 + (2 * t + 1))
                    for c in range(6):
                        ins = nc.tensor.matmul(ps[1][:, 0, 0:DIM], emb_xt[:, c, :], emb_w[:, c, :], start=(c == 0), stop=(c == 5))
                    ins.then_inc(emb_filled, 1)
            pe.wait_ge(emb_emptied, 2 * E_TILES)

            with pe.Fori(0, GROUPS) as g:
                order = iter(UNITS)

                def begin(key_, reads=()):
                    assert next(order) == key_, key_
                    s, n = UNIT[key_] % 4, UNIT[key_] // 4
                    emptied(pe, g, *reads, but=s)
                    pe.wait_ge(psum_emptied[s], g * SLOT_USES[s] + (n + 1))
                    return slot(key_)

                def turn_tiles(k, src, reads=((), ()), after=None):
                    for c in range(2):
                        if after is not None:
                            pe.wait_ge(ln_ready, g * 12 + (2 * after + c + 1))
                        s = begin((*k, c), reads[c])
                        for hf in range(2):
                            for j in TILES_OF[c]:
                                ins = nc.tensor.transpose(s[0:HT, hf, (j % HALF) * HT:(j % HALF + 1) * HT],
                                                          src[:, j, hf * HT:(hf + 1) * HT], ident[0:HT, 0:HT])
                        ins.then_inc(psum_filled, 1)

                def by_feature(key_, w, m, x, reads=(), then=()):
                    s = begin(key_, reads)
                    for c in range(2):
                        if c == 1:
                            emptied(pe, g, *then)
                        for hf in range(2):
                            ins = nc.tensor.matmul(s[0:m, c, 0:CH], w(hf), x[0:HT, hf, c * CH:(c + 1) * CH],
                                                   start=(hf == 0), stop=(hf == 1))
                    ins.then_inc(psum_filled, 1)

                def by_token(key_, i, x, w, reads=(), bias=False, parts=2):
                    s = begin(key_, reads)
                    o = tiles(key_)
                    for j in TILES_OF[i]:
                        for f in range(parts):
                            k = 128 if parts > 2 else HT + 1 if bias and f == 0 else HT
                            ins = nc.tensor.matmul(o[:, j % HALF], x[0:k, f, j * HT:(j + 1) * HT], w[0:k, f, :],
                                                   start=(f == 0), stop=(f == parts - 1))
                    ins.then_inc(psum_filled, 1)

                def value_unit(name, i, w, reads):
                    s = begin((name, i), reads)
                    for j in range(4):
                        t = 4 * i + j
                        for hf in range(2):
                            ins = nc.tensor.matmul(s[0:T72, j // 2, (j % 2) * DIM:(j % 2 + 1) * DIM],
                                                   fm_x[:, hf, t * T72:(t + 1) * T72], w[:, hf, :],
                                                   start=(hf == 0), stop=(hf == 1))
                    ins.then_inc(psum_filled, 1)

                def mixed(which, k, v, at):
                    rows = HT + 1 if which == 0 else HT

                    def apply(s, at_col, n, p, x):
                        for hf in range(2):
                            for e in range(2):
                                for mh in range(2):
                                    for q in range(3):
                                        ins = nc.tensor.matmul(s[32 * q:32 * q + 32, hf, e * n + at_col:e * n + at_col + T72],
                                                               x(mh)[:, hf * HT + 32 * q:hf * HT + 32 * q + 32],
                                                               p[:, mh, 6 * hf + 2 * q + e, :],
                                                               start=(mh == 0), stop=(mh == 1))
                        return ins

                    for t in range(GB * PACKS + (5 if which == 0 else 4)):
                        if which == 0 and t >= 8 and t % 4 == 0:
                            b = (t - 8) // 4
                            s = begin(("YT", b), [("Y0", 2 * b), ("Y0", 2 * b + 1)])
                            for nh in range(2):
                                for hf in range(2):
                                    ins = nc.tensor.transpose(s[0:T72, nh, hf * HT:(hf + 1) * HT],
                                                              y0_t[:, hf, nh * T72:(nh + 1) * T72], ident[0:HT, 0:HT])
                            ins.then_inc(psum_filled, 1)
                        if t < GB * PACKS:
                            b = t // PACKS
                            pe.wait_ge(qg_ready if which == 0 else qg2_ready, g * GB * PACKS + (t + 1))
                            s = begin((f"S{which}", t), both(f"K{which}"))
                            for i in range(PACK):
                                for hf in range(2):
                                    r = rows if hf == 0 else HT
                                    ins = nc.tensor.matmul(s[0:RP, i // 2, (i % 2) * TOK:(i % 2 + 1) * TOK],
                                                           qg0[t % 3][0:r, hf, i * RP:(i + 1) * RP],
                                                           k[0:r, hf, b * TOK:(b + 1) * TOK], start=(hf == 0), stop=(hf == 1))
                            ins.then_inc(psum_filled, 1)
                        if t >= 5 and t % 2 == 1 and t < GB * PACKS + 4:
                            b, nh = divmod((t - 5) // 2, 2)
                            s = begin((f"Y{which}", 2 * b + nh), [(f"M{which}", 4 * b + 2 * nh + p) for p in range(2)] + both(f"V{which}"))
                            apply(s, 0, T72, at[(2 * b + nh) % len(at)], lambda mh: v[:, 2 * b + mh]).then_inc(psum_filled, 1)
                        if which == 0 and t >= 8 and t % 4 == 0:
                            b = (t - 8) // 4
                            s = begin(("Z0", b), [("YT", b)])
                            for nh in range(2):
                                ins = apply(s, nh * T72, TOK, at[(2 * b + nh) % len(at)], lambda mh: y0[:, mh])
                            ins.then_inc(psum_filled, 1)
                        if 2 <= t < GB * PACKS + 2:
                            pe.wait_ge(probs_ready[which], g * GB * PACKS + (t - 1))
                            s = begin((f"M{which}", t - 2))
                            for mh in range(2):
                                for i in range(PACK):
                                    o = s[0:T72, mh, i * RP:(i + 1) * RP]
                                    p = probs0[(t - 2) % 3]
                                    if which == 0:
                                        ins = nc.tensor.matmul(o, p[:, i, mh * T72:(mh + 1) * T72], mix_out[:], start=True, stop=True)
                                    else:
                                        ins = nc.tensor.transpose(o, p[0:RP, i, mh * T72:(mh + 1) * T72], ident[0:RP, 0:RP])
                            ins.then_inc(psum_filled, 1)
                        if which == 0 and t == 14:
                            by_token(("P0", 0), 0, fm_o, proj0_w, [("Z0", 0), ("Z0", 1)], bias=True)

                def both(*k):
                    return [(*k, 0), (*k, 1)]

                turn_tiles(("LN", 0), tm_z, after=0)
                pe.wait_ge(w_l0, W_L0)
                for i in range(2):
                    value_unit("V0", i, qkv0_w[:, :, 2 * DIM:3 * DIM], [("LN", 0, i)])
                for o, k in ((0, "Q0"), (DIM, "K0")):
                    for half in range(2):
                        by_feature((k, half), lambda hf: qkv0_w[:, hf, o + half * HT:o + (half + 1) * HT], HT, fm_x)
                mixed(0, k0, v0, at0)
                by_token(("P0", 1), 1, fm_o, proj0_w, [("Z0", 2), ("Z0", 3)], bias=True)

                turn_tiles(("LN", 1), tm_x, after=1)
                pe.wait_ge(w_moe, W_MOE)
                s = begin(("LG",), both("LN", 1))
                for j in range(NT):
                    for hf in range(2):
                        ins = nc.tensor.matmul(s[0:HT, 0, j * EXPERTS:(j + 1) * EXPERTS], fm_x[:, hf, j * HT:(j + 1) * HT],
                                               router_w[:, hf, :], start=(hf == 0), stop=(hf == 1))
                ins.then_inc(psum_filled, 1)
                pe.wait_ge(picked_ready, g + 1)
                s = begin(("CT",))
                E2 = 2 * EXPERTS
                for j in range(NT):
                    for i in range(j + 1):
                        nc.tensor.matmul(s[0:HT, 0, j * E2:(j + 1) * E2], (before_bf if i == j else ones_bf)[:],
                                         picked_bf[:, i, :], start=(i == 0), stop=False)
                    for i in range(NT):
                        ins = nc.tensor.matmul(s[0:HT, 0, j * E2 + EXPERTS:(j + 1) * E2], ones_bf[:],
                                               picked_bf[:, i, 0:EXPERTS], start=False, stop=(i == NT - 1))
                ins.then_inc(psum_filled, 1)

                for i in range(3):
                    pe.wait_ge(experts_in[i], g * 16 + 16)
                    s = begin(("XT", i))
                    for hf in range(2):
                        for c in range(4):
                            ins = nc.tensor.transpose(s[0:HT, hf, c * SLOT_P:(c + 1) * SLOT_P],
                                                      xe_tok[:, 4 * i + c, hf * HT:(hf + 1) * HT], ident[0:SLOT_P, 0:SLOT_P])
                    ins.then_inc(psum_filled, 1)
                for e in range(EXPERTS + 1):
                    if e < EXPERTS:
                        for part in range(2):
                            s = begin(("H", e, part), [("XT", i) for i in range(3)])
                            for f in (range(0, 4) if part == 0 else range(4, 6)):
                                for hf in range(2):
                                    ins = nc.tensor.matmul(s[:, (f % 4) // 2, (f % 2) * CAP:(f % 2 + 1) * CAP],
                                                           moe_wi[:, hf, e, f * 128:(f + 1) * 128],
                                                           xe[:, hf, e * CAP:(e + 1) * CAP], start=(hf == 0), stop=(hf == 1))
                            ins.then_inc(psum_filled, 1)
                    if e >= 1:
                        s = begin(("EO", e - 1), both("H", e - 1))
                        for c in range(2):
                            for f in range(FT):
                                ins = nc.tensor.matmul(s[0:CAP // 2, 0, c * DIM:(c + 1) * DIM],
                                                       hid[(e - 1) % 2][:, f, c * (CAP // 2):(c + 1) * (CAP // 2)],
                                                       moe_wo[:, e - 1, f, :], start=(f == 0), stop=(f == FT - 1))
                        ins.then_inc(psum_filled, 1)

                def score_pair(key_, q, k, rows, b, width, masked, reads):
                    s = begin(key_, reads)
                    for a_ in range(2):
                        r = rows[a_]
                        for nh in range(2):
                            o = s[0:T72, a_, nh * TOK:(nh + 1) * TOK]
                            ins = nc.tensor.matmul(o, q[r:r + width, b * TOK + nh * T72:b * TOK + (nh + 1) * T72],
                                                   k[r:r + width, b * TOK:(b + 1) * TOK], start=True, stop=not masked)
                            if masked:
                                ins = nc.tensor.matmul(o[:, nh * T72:(nh + 1) * T72], ident_bf[:], diag_bf[:, nh, nh * T72:(nh + 1) * T72], start=False, stop=True)
                    ins.then_inc(psum_filled, 1)

                def turn_probs(key_, p):
                    s = begin(key_)
                    for a_ in range(2):
                        for mh in range(2):
                            for nh in range(2):
                                ins = nc.tensor.transpose(s[0:T72, a_, mh * TOK + nh * T72:mh * TOK + (nh + 1) * T72],
                                                          p[:, a_, nh, mh * T72:(mh + 1) * T72], ident[0:T72, 0:T72])
                    ins.then_inc(psum_filled, 1)

                def attend(key_, pt, v, b, reads):
                    s = begin(key_, reads)
                    for mh in range(2):
                        for a_ in range(2):
                            ins = nc.tensor.matmul(s[D1 * a_:D1 * a_ + D1, 0, 0:TOK], v(2 * b + mh, a_), pt[:, a_, mh, :],
                                                   start=(mh == 0), stop=(mh == 1))
                    ins.then_inc(psum_filled, 1)

                turn_tiles(("LN", 2), tm_x, after=2)
                pe.wait_ge(w_l1, 80)
                for s_ in range(STEPS + 3):
                    if s_ % 4 == 0 and s_ < STEPS:
                        hp = s_ // 4
                        cols = slice(hp * 128, (hp + 1) * 128)
                        by_feature(("Q1", hp), lambda hf: qkv1_w[:, hf, 0, cols], 128, fm_x, [("LN", 2, 0)], [("LN", 2, 1)])
                        by_feature(("K1", hp), lambda hf: qkv1_w[:, hf, 1, cols], 128, fm_x)
                        s = begin(("V1", hp))
                        for t in range(N72):
                            for hf in range(2):
                                ins = nc.tensor.matmul(s[0:T72, t // 4, (t % 4) * 128:(t % 4 + 1) * 128],
                                                       fm_x[:, hf, t * T72:(t + 1) * T72], qkv1_w[:, hf, 2, cols],
                                                       start=(hf == 0), stop=(hf == 1))
                        ins.then_inc(psum_filled, 1)
                    if s_ < STEPS:
                        hp, b = divmod(s_, 4)
                        score_pair(("S1", s_), q1[hp % 2], k1[hp % 2], (0, D1), b, D1, True,
                                   [("Q1", hp), ("K1", hp)])
                    if 2 <= s_ < STEPS + 2:
                        pe.wait_ge(probs_ready[1], g * STEPS + (s_ - 1))
                        turn_probs(("T1", s_ - 2), p12[(s_ - 2) % 3])
                    if s_ >= 3:
                        hp, b = divmod(s_ - 3, 4)
                        attend(("O1", s_ - 3), pt1[(s_ - 3) % 2], lambda t, a_: v1[hp % 2][:, t, a_, :], b,
                               [("T1", s_ - 3), ("V1", hp)])
                for i in range(2):
                    by_token(("P1", i), i, ot1, proj1_w, [("O1", 4 * hp + 2 * i + j) for hp in range(6) for j in range(2)], parts=6)

                turn_tiles(("LN", 4), tm_z, after=4)
                pe.wait_ge(w_ffn, W_FFN)
                half_of = lambda w, half: lambda hf: w[:, hf, half * HT:(half + 1) * HT]
                by_feature(("E1",), lambda hf: r_in_w[:, hf, :], RHD, fm_r, [("LN", 4, 0)], [("LN", 4, 1)])
                by_feature(("Q2", 0), half_of(wq2, 0), HT, fm_x)
                by_feature(("Q2", 1), half_of(wq2, 1), HT, fm_x)
                pe.wait_ge(g_mean_ready, g + 1)
                s = begin(("GC",))
                nc.tensor.matmul(s[0:RHD, 0, 0:GB], r_o1_w[:, 1, :], g_mean[:], start=True, stop=True).then_inc(psum_filled, 1)
                value_unit("V2", 0, wv2, [])
                s = begin(("H1",))
                for c in range(2):
                    ins = nc.tensor.matmul(s[0:RHD, c, 0:CH], r_o1_w[:, 0, :], e_t[:, c * CH:(c + 1) * CH], start=True, stop=True)
                ins.then_inc(psum_filled, 1)
                value_unit("V2", 1, wv2, [])
                s = begin(("H2",), [("H1",)])
                for c in range(2):
                    ins = nc.tensor.matmul(s[0:RHD // 2, c, 0:CH], r_o2_w[:], h1_t[:, c * CH:(c + 1) * CH], start=True, stop=True)
                ins.then_inc(psum_filled, 1)
                by_feature(("K2", 0), half_of(wk2, 0), HT, fm_x)
                by_feature(("K2", 1), half_of(wk2, 1), HT, fm_x)
                pe.wait_ge(h2_ones, g + 1)
                s = begin(("RL",), [("H2",)])
                for j in range(NT):
                    ins = nc.tensor.matmul(s[0:HT, 0, 4 * j:4 * j + 4], h2_t[:, j * HT:(j + 1) * HT], r_o3_w[:], start=True, stop=True)
                ins.then_inc(psum_filled, 1)
                mixed(2, k2, v2, at2)
                for i in range(2):
                    by_token(("P2", i), i, fm_o, wo2, [("Y2", b) for b in range(2 * GB)], bias=True)

                turn_tiles(("LN", 5), tm_x, after=5)
                for i in range(FT):
                    by_feature(("F1", i), lambda hf: fc1_w[:, hf, i * 128:(i + 1) * 128], 128, fm_x,
                               [("LN", 5, 0)], [("LN", 5, 1)] if i == 0 else ())
                for i in range(2):
                    by_token(("F2", i), i, ff, fc2_w, [("F1", f) for f in range(FT)], parts=FT)
                turn_tiles(("OUT",), tm_z, ([("F2", 0)], [("F2", 1)]))
                for i in range(2):
                    by_token(("DN", i), i, fm_x, lra_dn, [("OUT", i)])
                turn_tiles(("DT",), tm_x, ([("DN", 0)], [("DN", 1)]))
                for i in range(2):
                    by_token(("UP", i), i, fm_o, lra_up, [("DT", i)])


_ORDER = ["x", "txt", "tok_w", "tok_b", "pos", "qkv0_w", "proj_l_w", "proj_l_b", "proj_w_w", "proj_w_b", "lamb", "proj0_w",
          "proj0_b", "router_w", "moe_wi", "moe_wo", "qkv1_w", "scale1", "proj1_w", "bias1", "wq2", "wk2", "bq2", "bk2",
          "wv2", "bv2", "wo2", "bo2", "ln_gb", "fc1_w", "fc1_b", "fc2_w", "fc2_b", "r_in_w", "r_o1_w", "r_o2_w", "r_o3_w",
          "r_b", "r_o2_b", "lra_dn", "lra_up"]


def laid_out(i):
    def by_part(w, p):
        return w.reshape(w.shape[0] // p, p, w.shape[1]).transpose(1, 0, 2)

    row = lambda v: v.reshape(1, -1)
    f = {k[len("L1_ffn_"):]: v for k, v in i.items() if k.startswith("L1_ffn_")}
    return {
        "x": i["x"].reshape(SEQS, 64, 192), "txt": i["txt"], "tok_w": by_part(i["L0_tok_W"], 128), "tok_b": row(i["L0_tok_b"]),
        "pos": np.tile(i["L0_tok_pos_emb"].reshape(4, 4, DIM), (8, 1, 1)),
        "qkv0_w": by_part(i["L0_attn_qkv_w"].T, HT), "proj_l_w": i["L0_attn_proj_l_w"].T, "proj_l_b": row(i["L0_attn_proj_l_b"]),
        "proj_w_w": i["L0_attn_proj_w_w"].T, "proj_w_b": row(i["L0_attn_proj_w_b"]), "lamb": row(i["L0_attn_lamb"]),
        "proj0_w": by_part(i["L0_attn_proj_out_w"].T, HT), "proj0_b": row(i["L0_attn_proj_out_b"]),
        "router_w": by_part(i["L0_ffn_w_router"], HT),
        "moe_wi": i["L0_ffn_wi"].reshape(EXPERTS, 2, HT, FF).transpose(0, 2, 1, 3),
        "moe_wo": i["L0_ffn_wo"].reshape(EXPERTS, FT, 128, DIM).transpose(0, 2, 1, 3),
        "qkv1_w": by_part(i["L1_attn_W_qkv"], HT).reshape(HT, 2, 3, HEADS * D1),
        "scale1": i["L1_attn_scale"].reshape(6, 2).T, "proj1_w": by_part(i["L1_attn_W_out"], 128), "bias1": row(i["L1_attn_b_out"]),
        "wq2": by_part(f["wq"].T, HT), "wk2": by_part(f["wk"].T, HT), "bq2": f["bq"].reshape(2, HT).T, "bk2": f["bk"].reshape(2, HT).T,
        "wv2": by_part(f["wv"].T, HT), "bv2": row(f["bv"]), "wo2": by_part(f["wo"].T, HT), "bo2": row(f["bo"]),
        "ln_gb": np.stack([f[n].reshape(2, HT).T for n in ("ln1_g", "ln1_b", "ln2_g", "ln2_b", "r_ln_g", "r_ln_b")], axis=2),
        "fc1_w": by_part(f["fc1_w"].T, HT), "fc1_b": f["fc1_b"].reshape(FT, 128).T, "fc2_w": by_part(f["fc2_w"].T, 128),
        "fc2_b": row(f["fc2_b"]), "r_in_w": by_part(f["r_in_w"].T, HT), "r_o1_w": by_part(f["r_o1_w"].T, RHD),
        "r_o2_w": f["r_o2_w"].T, "r_o3_w": np.concatenate([f["r_o3_w"].T, row(f["r_o3_b"])]),
        "r_b": np.stack([f["r_in_b"], f["r_o1_b"]], axis=1), "r_o2_b": f["r_o2_b"].reshape(-1, 1),
        "lra_dn": by_part(f["lra_down"].reshape(3 * RANK, DIM).T, HT),
        "lra_up": by_part(f["lra_up"].transpose(0, 2, 1).reshape(3 * RANK, DIM), HT),
    }


def kernel(**inputs):
    import concourse.bacc as bacc
    from concourse.bass_utils import run_bass_kernel_spmd

    nc = bacc.Bacc("TRN2", target_bir_lowering=False, num_devices=1)
    laid = laid_out({k: np.asarray(v) for k, v in inputs.items()})
    arrays, aps = {}, {}
    for name in _ORDER:
        v = np.ascontiguousarray(laid[name])
        arrays["in_" + name] = v
        aps[name] = nc.dram_tensor("in_" + name, v.shape, mybir.dt.from_np(v.dtype), kind="ExternalInput").ap()
    out = nc.dram_tensor("out", (SEQS, TOK, DIM), F32, kind="ExternalOutput").ap()
    program(nc, aps, out.rearrange("b n d -> (b n) d"))
    return run_bass_kernel_spmd(nc, [arrays], core_ids=[0]).results[0]["out"]
```

```python
from contextlib import ExitStack

import numpy as np
import concourse.bass as bass
from concourse import mybir

F32 = mybir.dt.float32
BF16 = mybir.dt.bfloat16
U32 = mybir.dt.uint32
ALU = mybir.AluOpType
ACT = mybir.ActivationFunctionType
AX = mybir.AxisListType

SEQS, TOK, IMG_TOK, DIM = 64, 144, 16, 192
TXT_TOK = TOK - IMG_TOK
GB = 4
GROUPS = SEQS // GB
GT = GB * TOK
HT = 96
NT = GT // HT
CH = 2 * TOK
T72 = TOK // 2
N72 = GT // T72
HEADS = 12
D0 = DIM // HEADS
D1 = 64
RN = 9
RP = RN * HEADS
PACK = 4
PN = RN * PACK
PACKS = TOK // PN
EXPERTS, FF = 8, 768
FT = FF // 128
CAP = 180
SLOTS = EXPERTS * CAP
SLOT_P = 120
RHD, RANK = 128, 64
EPS = 1e-5
STEPS = 6 * GB
MASKED = -1.0e30
E_TILES = SEQS * IMG_TOK // 128
E_BUFS = 4


def psum_units():
    u = [("LN", 0, 0), ("LN", 0, 1)]
    u += [("V0", 0), ("V0", 1)] + [("Q0", 0), ("Q0", 1), ("K0", 0), ("K0", 1)]
    for t in range(GB * PACKS + 5):
        if t >= 8 and t % 4 == 0:
            u.append(("YT", (t - 8) // 4))
        if t < GB * PACKS:
            u.append(("S0", t))
        if t >= 5 and t % 2 == 1 and t < GB * PACKS + 4:
            u.append(("Y0", (t - 5) // 2))
        if t >= 8 and t % 4 == 0:
            u.append(("Z0", (t - 8) // 4))
        if 2 <= t < GB * PACKS + 2:
            u.append(("M0", t - 2))
        if t == GB * PACKS - 2:
            u.append(("P0", 0))
    u.append(("P0", 1))
    u += [("LN", 1, 0), ("LN", 1, 1), ("LG",), ("CT", 0), ("CT", 1)]
    u += [("XT", i) for i in range(3)]
    for e in range(EXPERTS + 1):
        if e < EXPERTS:
            u += [("H", e, 0), ("H", e, 1)]
        if e >= 1:
            u.append(("EO", e - 1))
    u += [("LN", 2, 0), ("LN", 2, 1)]
    for s in range(STEPS + 3):
        if s % 4 == 0 and s < STEPS:
            u += [("Q1", s // 4), ("K1", s // 4), ("V1", s // 4)]
        if s < STEPS:
            u.append(("S1", s))
        if 2 <= s < STEPS + 2:
            u.append(("T1", s - 2))
        if s >= 3:
            u.append(("O1", s - 3))
    u += [("P1", 0), ("P1", 1), ("LN", 4, 0), ("LN", 4, 1)]
    u += [("E1",), ("Q2", 0), ("Q2", 1), ("GC",), ("V2", 0), ("H1",), ("V2", 1), ("H2",), ("K2", 0), ("K2", 1), ("RL",)]
    for t in range(GB * PACKS + 4):
        if t < GB * PACKS:
            u.append(("S2", t))
        if t >= 5 and t % 2 == 1 and t < GB * PACKS + 4:
            u.append(("Y2", (t - 5) // 2))
        if 2 <= t < GB * PACKS + 2:
            u.append(("M2", t - 2))
        if t == GB * PACKS + 1:
            u.append(("P2", 0))
    u += [("P2", 1), ("LN", 5, 0), ("LN", 5, 1)]
    u += [("F1", i) for i in range(FT)] + [("F2", 0), ("F2", 1)]
    u += [("OUT", 0), ("OUT", 1), ("DN", 0), ("DN", 1), ("DT", 0), ("DT", 1), ("UP", 0), ("UP", 1)]
    return u


UNITS = psum_units()
UNIT = {key: i for i, key in enumerate(UNITS)}
SLOT_USES = [len(range(s, len(UNITS), 4)) for s in range(4)]
VEC_STEPS = 154
W_L0 = 16 * 36
W_FFN = 16 * 21
W_MOE = 16 * (1 + 2 * EXPERTS)
HALF = NT // 2
TILES_OF = [range(0, HALF), range(HALF, NT)]
TS = 256


def program(nc, a, out):
    with ExitStack() as ctx:
        def sb(name, shape, dt=F32):
            return ctx.enter_context(nc.sbuf_tensor(name, shape, dt))

        def sem(name):
            return ctx.enter_context(nc.semaphore(name))

        img_rows = nc.dram_tensor("img_rows", (SEQS, IMG_TOK, DIM), F32, kind="Internal").ap()
        expert_rows = nc.dram_tensor("expert_rows", (SLOTS, DIM), F32, kind="Internal").ap()
        result_rows = nc.dram_tensor("result_rows", (SLOTS + 1, DIM), F32, kind="Internal").ap()

        moe_wi = sb("moe_wi", [HT, 2, EXPERTS, FF])
        moe_wo = sb("moe_wo", [128, EXPERTS, FT, DIM])
        router_w = sb("router_w", [HT, 2, EXPERTS])
        qkv0_w = sb("qkv0_w", [HT, 2, 3 * DIM])
        proj0_w = sb("proj0_w", [HT + 1, 2, DIM])
        mix_in = sb("mix_in", [HT, 2, HEADS])
        mix_out = sb("mix_out", [RP + 1, RP])
        coef_y = sb("coef_y", [HT, HEADS])
        coef_z = sb("coef_z", [HT, HEADS])
        by_head = sb("by_head", [HT, 2, HEADS])
        feature_y = sb("feature_y", [HT, 2])
        feature_z = sb("feature_z", [HT, 2, 2])
        parity = sb("parity", [HT, 2, 2])
        qkv1_w = sb("qkv1_w", [HT, 2, 3, HEADS * D1])
        scale1 = sb("scale1", [128, 6])
        proj1_w = sb("proj1_w", [128, 6, DIM])
        bias1 = sb("bias1", [HT, DIM])
        wq2 = sb("wq2", [HT, 2, DIM])
        wk2 = sb("wk2", [HT, 2, DIM])
        bq2 = sb("bq2", [HT, 2])
        bk2 = sb("bk2", [HT, 2])
        own_head = sb("own_head", [HT, 2, HEADS])
        wv2 = sb("wv2", [HT, 2, DIM])
        bv2 = sb("bv2", [T72, DIM])
        wo2 = sb("wo2", [HT + 1, 2, DIM])
        ln_gb = sb("ln_gb", [HT, 2, 6])
        fc1_w = sb("fc1_w", [HT, 2, FF])
        fc1_b = sb("fc1_b", [128, FT])
        fc2_w = sb("fc2_w", [128, FT, DIM])
        fc2_b = sb("fc2_b", [HT, DIM])
        r_in_w = sb("r_in_w", [HT, 2, RHD])
        r_o1_w = sb("r_o1_w", [RHD, 2, RHD])
        r_o2_w = sb("r_o2_w", [RHD, RHD // 2])
        r_o3_w = sb("r_o3_w", [RHD // 2 + 1, 4])
        r_b = sb("r_b", [RHD, 3])
        lra_dn = sb("lra_dn", [HT, 2, DIM])
        lra_up = sb("lra_up", [HT, 2, DIM])

        ident = sb("ident", [128, 128])
        ident_bf = sb("ident_bf", [T72, T72], BF16)
        diag_bf = sb("diag_bf", [T72, T72], BF16)
        before_bf = sb("before_bf", [HT, HT], BF16)
        ones_bf = sb("ones_bf", [HT, HT], BF16)
        first_e = sb("first_e", [HT, EXPERTS])
        base_e = sb("base_e", [HT, EXPERTS])
        reserved = sb("reserved", [HT, NT])
        minus_half = sb("minus_half", [HT, NT])

        h = sb("h", [HT, NT, DIM])
        ARENA = 15456
        arena = sb("arena", [128, ARENA])

        def view(at, rows, *shape):
            n = int(np.prod(shape))
            v = arena[0:rows, at:at + n]
            names = "abcd"[:len(shape)]
            if len(shape) == 1:
                return v
            return v.rearrange(f"p ({' '.join(names)}) -> p {' '.join(names)}",
                               **{c: s for c, s in zip(names, shape)})

        R0, R1, R2, R3, R4, R5, R6, R7 = 0, 1152, 2304, 3456, 4608, 5760, 8352, 10080
        tm_x = view(R0, HT, NT, DIM)
        fm_x = view(R1, HT, 2, GT)
        tm_z = view(R2, HT, NT, DIM)
        fm_o = view(R3, HT + 1, 2, GT)
        k0 = view(R4, HT + 1, 2, GT)
        qg0 = [view(R5 + 864 * i, HT + 1, 2, PN * HEADS) for i in range(3)]
        probs0 = [view(R6 + 576 * i, RP + 1, PACK, TOK) for i in range(3)]
        q0 = view(R7, HT, 2, GT)
        v0 = view(R7 + 1152, T72, N72, DIM)
        y0 = view(R7 + 2688, T72, 2, DIM)
        y0_t, u0_t = [view(R7 + 3072 + 288 * i, HT, 2, TOK) for i in range(2)]
        at0 = [view(at, T72, 2, HEADS, T72) for at in (R0, R0 + 1728, R7 + 3648)]
        xe_tok = view(R0, SLOT_P, SLOTS // SLOT_P, DIM)
        xe = view(R3, HT, 2, SLOTS)
        eo = view(R7 + 2160, 128, EXPERTS, DIM + HT)
        hid = [view(R7 + 1080 * i, 128, FT, CAP) for i in range(2)]
        back = view(R7, HT, NT, 2 * DIM)
        pt1 = [view(R0 + 576 * i, T72, 2, 2, TOK) for i in range(2)]
        q1 = [view(R2, 128, GT), view(R7 + 3456, 128, GT)]
        k1 = [view(R2 + 576, 128, GT), view(R7 + 4032, 128, GT)]
        v1 = [view(R5 + 1024 * i, T72, N72, 2, D1) for i in range(2)]
        p12 = [view(R6 + 576 * i, T72, 2, 2, TOK) for i in range(3)]
        ot1 = view(R7, 128, 6, GT)
        fm_r = view(R4, HT, 2, GT)
        e_t = view(R7, RHD, GT)
        h1_t = view(R7 + 576, RHD, GT)
        h2_t = view(R7 + 1152, RHD // 2 + 1, GT)
        q2 = view(R2, HT, 2, GT)
        k2 = view(R4, HT, 2, GT)
        v2 = view(R7 + 3456, T72, N72, DIM)
        at2 = [view(R7 + 1728 * i, T72, 2, HEADS, T72) for i in range(2)]
        ff = view(R7, 128, FT, GT)
        emb_w = view(R7, 128, 6, DIM)
        emb_x = [view(R0 + 768 * i, 128, 6, 128) for i in range(E_BUFS)]
        emb_out = [view(R0 + 768 * E_BUFS + DIM * i, 128, DIM) for i in range(2)]
        emb_xt = view(R7 + 4032, 128, 6, 128)
        emb_bias = view(R7 + 4800, 128, DIM)
        emb_b = view(R7 + 4992, 128, DIM)
        zero_rows = view(R7 + 1152, SLOT_P, SLOTS // SLOT_P, DIM)
        ones_row = view(R7 + 3456, 1, PACK * TOK)

        stats = sb("stats", [HT, NT, 6])
        mean = sb("mean", [HT, NT])
        carrier = sb("carrier", [HT, 3, NT])
        mean2 = sb("mean2", [HT, NT])
        diff = sb("diff", [HT, NT])
        diff2 = sb("diff2", [HT, NT])
        var = sb("var", [HT, NT])
        var2 = sb("var2", [HT, NT])
        var_eps = sb("var_eps", [HT, NT])
        rstd = sb("rstd", [HT, NT])
        var_only, var_r, var_rr, var_eps2, rstd2, rstd_both = [sb(n, [HT, NT]) for n in (
            "var_only", "var_r", "var_rr", "var_eps2", "rstd2", "rstd_both")]
        negmax = [sb(f"negmax{i}", [RP, 4]) for i in range(3)]
        rowsum = [sb(f"rowsum{i}", [RP, 4]) for i in range(3)]
        rinv = [sb(f"rinv{i}", [RP, 4]) for i in range(3)]
        lg = sb("lg", [HT, NT, EXPERTS])
        lg2 = sb("lg2", [HT, NT, EXPERTS])
        lgm = sb("lgm", [HT, NT])
        lgs = sb("lgs", [HT, NT])
        gate = sb("gate", [HT, NT, 2])
        key = sb("key", [HT, NT])
        picked = sb("picked", [HT, 2, NT, EXPERTS])
        picked_bf = sb("picked_bf", [HT, 2, NT, EXPERTS], BF16)
        place = sb("place", [HT, 2, NT, EXPERTS])
        base = sb("base", [HT, 2, NT, EXPERTS])
        pos = sb("pos", [HT, 2, NT])
        first_row = sb("first_row", [HT, 2, NT])
        row_of = sb("row_of", [HT, 2, NT])
        over = sb("over", [HT, 2, NT])
        row_to = sb("row_to", [HT, 2, NT])
        row_idx = sb("row_idx", [HT, 2, NT], U32)
        g_mean = sb("g_mean", [RHD, GB])
        g_bias = sb("g_bias", [RHD, GB])
        rl = sb("rl", [HT, NT, 2, 2])
        bits = sb("bits", [HT, NT, 2])
        nbits = sb("nbits", [HT, NT, 2])
        sel = sb("sel", [HT, NT, 3])
        table_out = sb("table_out", [HT, NT])

        ps_flat = [ctx.enter_context(nc.psum_tensor(f"ps{i}", [128, 1024], F32)) for i in range(4)]
        ps = [v[:, :].rearrange("p (a n) -> p a n", a=2) for v in ps_flat]

        psum_filled = sem("psum_filled")
        psum_emptied = [sem(f"psum_emptied{i}") for i in range(4)]
        w_tok, w_l0, w_moe, w_l1, w_ffn = (sem(n) for n in ("w_tok", "w_l0", "w_moe", "w_l1", "w_ffn"))
        mix_zeroed = sem("mix_zeroed")
        ones_set = sem("ones_set")
        mix_ready = sem("mix_ready")
        vec_setup = sem("vec_setup")
        pool_setup = sem("pool_setup")
        patches_in = [sem(f"patches_in{i}") for i in range(E_BUFS)]
        emb_filled = sem("emb_filled")
        emb_emptied = sem("emb_emptied")
        emb_stored = [sem(f"emb_stored{i}") for i in range(2)]
        zeros_stored = sem("zeros_stored")
        h_loaded = sem("h_loaded")
        h_filled = sem("h_filled")
        out_stored = sem("out_stored")
        var_ready = sem("var_ready")
        rstd_ready = sem("rstd_ready")
        ln_ready = sem("ln_ready")
        vec_step = sem("vec_step")
        pool_step = sem("pool_step")
        qg_ready = sem("qg_ready")
        max_ready = [sem(f"max_ready{i}") for i in range(3)]
        probs_ready = [sem(f"probs_ready{i}") for i in range(3)]
        qg2_ready = sem("qg2_ready")
        y_scaled = sem("y_scaled")
        rows_chosen = sem("rows_chosen")
        picked_ready = sem("picked_ready")
        logit_exp = sem("logit_exp")
        scattered = sem("scattered")
        experts_in = [sem(f"experts_in{i}") for i in range(3)]
        results_out = sem("results_out")
        gathered = [sem(f"gathered{j}") for j in range(NT)]
        bias1_added = sem("bias1_added")
        g_mean_ready = sem("g_mean_ready")
        h2_ones = sem("h2_ones")
        bits_ready = sem("bits_ready")
        ffn_base = sem("ffn_base")
        out_added = sem("out_added")

        def slot(key_):
            return ps[UNIT[key_] % 4]

        def tiles(key_, n=HALF):
            return ps_flat[UNIT[key_] % 4][0:HT, 0:n * TS].rearrange("p (j d) -> p j d", d=TS)[:, :, 0:DIM]

        def filled(eng, g, key_):
            eng.wait_ge(psum_filled, g * len(UNITS) + (UNIT[key_] + 1))

        def emptied(eng, g, *keys, but=None):
            for s in range(4):
                n = max((UNIT[k] // 4 + 1 for k in keys if UNIT[k] % 4 == s), default=0)
                if n and s != but:
                    eng.wait_ge(psum_emptied[s], g * SLOT_USES[s] + (n + 1))

        def to_empty(key_):
            return psum_emptied[UNIT[key_] % 4]

        def mixed_out(g, eng, copy, which, t):
            at = at0[t // 2 % 3] if which == 0 else at2[t // 2 % 2]
            c0 = t % 2 * PN
            if which == 0 and t < 2:
                eng.wait_ge(h_filled, g * 16 + 16)
            for mh in range(2):
                if mh == 0:
                    filled(eng, g, (f"M{which}", t))
                src = slot((f"M{which}", t))[0:T72, mh, 0:PN * HEADS]
                if which == 0:
                    ins = copy(at[:, mh, :, c0:c0 + PN].rearrange("p g n -> p n g"), src.rearrange("p (n g) -> p n g", g=HEADS))
                else:
                    ins = copy(at[:, mh, :, c0:c0 + PN].rearrange("p (f g) n -> p f n g", f=2),
                               src.rearrange("p (f n g) -> p f n g", f=2, g=HEADS // 2))
            ins.then_inc(to_empty((f"M{which}", t)), 1)

        def exp_tiles(g, act, which, t):
            act.wait_ge(max_ready[which], g * GB * PACKS + (t + 1))
            s = slot((f"S{which}", t))
            for i in range(PACK):
                ins = nc.scalar.activation(probs0[t % 3][0:RP, i, :], s[0:RP, i // 2, (i % 2) * TOK:(i % 2 + 1) * TOK],
                                           ACT.Exp, bias=negmax[t % 3][:, i:i + 1], accum_out=rowsum[t % 3][:, i:i + 1])
            ins.then_inc(to_empty((f"S{which}", t)), 1)

        def exp_pair(g, act, s):
            act.wait_ge(max_ready[1], g * STEPS + (s + 1))
            for i in range(4):
                ins = nc.scalar.activation(p12[s % 3][:, i // 2, i % 2, :],
                                           slot(("S1", s))[0:T72, i // 2, (i % 2) * TOK:(i % 2 + 1) * TOK], ACT.Exp,
                                           bias=negmax[s % 3][0:T72, i:i + 1], accum_out=rowsum[s % 3][0:T72, i:i + 1])
            ins.then_inc(to_empty(("S1", s)), 1)

        block = ctx.enter_context(nc.Block())

        @block.sync
        def _(sp):
            sp.dma_start(emb_w, a["tok_w"]).then_inc(w_tok, 16)
            x_v = a["x"].rearrange("b (hp ph) (wp pc) -> (b hp) wp ph pc", ph=16, wp=4)
            for t in range(E_BUFS):
                for wp in range(4):
                    sp.dma_start(emb_x[t][wp * 32:wp * 32 + 32].rearrange("p a b -> p (a b)").rearrange("p (ph pc) -> p ph pc", ph=16),
                                 x_v[t * 32:t * 32 + 32, wp]).then_inc(patches_in[t], 16)
            for wp in range(4):
                sp.dma_start(emb_bias[wp * 32:wp * 32 + 32], a["pos"][:, wp]).then_inc(w_tok, 16)
            sp.dma_start(emb_b, a["tok_b"].to_broadcast([128, DIM])).then_inc(w_tok, 16)
            for j in range(6):
                for hf in range(2):
                    sp.dma_start(mix_in[16 * j:16 * j + 16, hf, :],
                                 a["proj_l_w"][6 * hf + j:6 * hf + j + 1, :].to_broadcast([16, HEADS])).then_inc(w_l0, 16)
            sp.dma_start(qkv0_w[:], a["qkv0_w"]).then_inc(w_l0, 16)
            sp.dma_start(proj0_w[0:HT], a["proj0_w"]).then_inc(w_l0, 16)
            sp.dma_start(proj0_w[HT:HT + 1, 0, :], a["proj0_b"]).then_inc(w_l0, 16)
            sp.dma_start(coef_y[:], a["lamb"].to_broadcast([HT, HEADS])).then_inc(w_l0, 16)
            sp.dma_start(coef_z[:], a["lamb"].to_broadcast([HT, HEADS])).then_inc(w_l0, 16)
            for i in range(3):
                for hf in range(2):
                    sp.dma_start(qg0[i][HT:HT + 1, hf, :].rearrange("p (n g) -> p n g", g=HEADS),
                                 a["proj_l_b"].rearrange("o (n g) -> o n g", n=1).to_broadcast([1, PN, HEADS])).then_inc(w_l0, 16)
            sp.wait_ge(mix_zeroed, 1)
            for n in range(RN):
                sp.dma_start(mix_out[n * HEADS:(n + 1) * HEADS, n * HEADS:(n + 1) * HEADS], a["proj_w_w"]).then_inc(w_l0, 16)
            sp.dma_start(mix_out[RP:RP + 1, :].rearrange("p (n g) -> p n g", g=HEADS),
                         a["proj_w_b"].rearrange("o (n g) -> o n g", n=1).to_broadcast([1, RN, HEADS])).then_inc(w_l0, 16)
            sp.wait_ge(ones_set, 1)
            for i in range(3):
                sp.dma_start(probs0[i][RP:RP + 1].rearrange("p a b -> p (a b)"),
                             ones_row).then_inc(w_l0, 16)
            with sp.Fori(1, E_TILES // E_BUFS) as i:
                for t in range(E_BUFS):
                    sp.wait_ge(emb_filled, i * 2 * E_BUFS + (2 * t + 1 - 2 * E_BUFS))
                    for wp in range(4):
                        sp.dma_start(emb_x[t][wp * 32:wp * 32 + 32].rearrange("p a b -> p (a b)").rearrange("p (ph pc) -> p ph pc", ph=16),
                                     x_v[bass.ds(i * 32 * E_BUFS + t * 32, 32), wp]).then_inc(patches_in[t], 16)
            out_v = out.rearrange("(g j p) d -> g p j d", g=GROUPS, p=HT)
            img_v = img_rows.rearrange("(g c b) t d -> g b t c d", g=GROUPS, b=2)
            txt_v = a["txt"].rearrange("(g c b) t d -> g b t c d", g=GROUPS, b=2)
            exp_v = expert_rows.rearrange("(c p) d -> p c d", p=SLOT_P)
            for t in range(2):
                sp.wait_ge(emb_stored[t], 16 * 4 * E_TILES // 2)

            def load(g):
                hv = tm_x.rearrange("p (c j) d -> p c j d", c=2)
                sp.dma_start(hv[0:16, :, 0], img_v[g, 0]).then_inc(h_loaded, 16)
                sp.dma_start(hv[16:96, :, 0], txt_v[g, 0, 0:80]).then_inc(h_loaded, 16)
                sp.dma_start(hv[0:48, :, 1], txt_v[g, 0, 80:128]).then_inc(h_loaded, 16)
                sp.dma_start(hv[48:64, :, 1], img_v[g, 1]).then_inc(h_loaded, 16)
                sp.dma_start(hv[64:96, :, 1], txt_v[g, 1, 0:32]).then_inc(h_loaded, 16)
                sp.dma_start(hv[0:96, :, 2], txt_v[g, 1, 32:128]).then_inc(h_loaded, 16)

            def experts(g):
                sp.wait_ge(scattered, g * 192 + 192)
                filled(sp, g, ("LN", 1, 1))
                for i in range(3):
                    sp.dma_start(xe_tok[:, 4 * i:4 * i + 4], exp_v[:, 4 * i:4 * i + 4]).then_inc(experts_in[i], 16)
                for e in range(EXPERTS):
                    emptied(sp, g, ("EO", e))
                    rows = result_rows[e * CAP:(e + 1) * CAP]
                    late = 128 - (CAP - 64)
                    for at, dst in ((eo[:, e, 0:DIM], rows[0:128]), (eo[late:64, e, DIM:], rows[128:CAP, 0:HT]),
                                    (eo[64 + late:128, e, DIM:], rows[128:CAP, HT:])):
                        sp.dma_start(dst, at).then_inc(results_out, 16)

            def store(g):
                emptied(sp, g, ("UP", 1))
                sp.dma_start(out_v[g], h[:]).then_inc(out_stored, 16)

            def fill_h(g):
                sp.wait_ge(h_loaded, g * 96 + 96)
                sp.dma_start(h[:], tm_x).then_inc(h_filled, 16)

            load(0)
            fill_h(0)
            with sp.Fori(0, GROUPS - 1) as g:
                experts(g)
                filled(sp, g, ("DT", 1))
                load(g + 1)
                store(g)
                sp.wait_ge(out_stored, g * 16 + 16)
                fill_h(g + 1)
            experts(GROUPS - 1)
            store(GROUPS - 1)
            sp.wait_ge(out_stored, GROUPS * 16)
            sp.wait_ge(results_out, GROUPS * EXPERTS * 48)

        @block.gpsimd
        def _(pool):
            done = [0]

            def link(ins):
                ins.then_inc(pool_setup, 1)
                done[0] += 1
                pool.wait_ge(pool_setup, done[0])

            nc.gpsimd.memset(mix_out[:], 0.0).then_inc(mix_zeroed, 1)
            nc.gpsimd.memset(own_head[:], float(D0) ** -0.5)
            nc.gpsimd.memset(ident[:], 0.0)
            nc.gpsimd.memset(ident_bf[:], 0.0)
            nc.gpsimd.memset(diag_bf[:], 0.0)
            nc.gpsimd.memset(ones_bf[:], 1.0)
            nc.gpsimd.memset(before_bf[:], 1.0)
            nc.gpsimd.memset(reserved[:], 0.0)
            nc.gpsimd.memset(minus_half[:], -0.5)
            link(nc.gpsimd.memset(zero_rows, 0.0))
            nc.gpsimd.affine_select(out=ident[:], in_=ident[:], compare_op=ALU.not_equal, fill=1.0, base=0,
                                    pattern=[[-1, 128]], channel_multiplier=1)
            nc.gpsimd.affine_select(out=ident_bf[:], in_=ident_bf[:], compare_op=ALU.not_equal, fill=1.0, base=0,
                                    pattern=[[-1, T72]], channel_multiplier=1)
            nc.gpsimd.affine_select(out=diag_bf[:], in_=diag_bf[:], compare_op=ALU.not_equal, fill=MASKED, base=0,
                                    pattern=[[-1, T72]], channel_multiplier=1)
            nc.gpsimd.affine_select(out=before_bf[:], in_=before_bf[:], compare_op=ALU.is_gt, fill=0.0, base=0,
                                    pattern=[[1, HT]], channel_multiplier=-1)
            oh = own_head[:]
            nc.gpsimd.affine_select(out=oh, in_=oh, compare_op=ALU.is_ge, fill=0.0, base=0,
                                    pattern=[[HT, 2], [-D0, HEADS]], channel_multiplier=1)
            rv = reserved[:].rearrange("p (c j) -> p c j", c=2)
            nc.gpsimd.affine_select(out=rv[:, :, 0:2], in_=rv[:, :, 0:2], compare_op=ALU.not_equal, fill=1.0, base=0,
                                    pattern=[[0, 2], [-48, 2]], channel_multiplier=1)
            nc.gpsimd.iota(first_e[:], pattern=[[-1, EXPERTS]], base=EXPERTS, channel_multiplier=0,
                           allow_small_or_imprecise_dtypes=True)
            link(nc.gpsimd.iota(base_e[:], pattern=[[CAP, EXPERTS]], base=0, channel_multiplier=0,
                                allow_small_or_imprecise_dtypes=True))
            nc.gpsimd.affine_select(out=oh, in_=oh, compare_op=ALU.is_ge, fill=0.0, base=D0 - 1,
                                    pattern=[[-HT, 2], [D0, HEADS]], channel_multiplier=-1)
            pool.dma_start(expert_rows.rearrange("(c p) d -> p c d", p=SLOT_P), zero_rows).then_inc(zeros_stored, 16)
            pool.dma_start(result_rows[SLOTS:SLOTS + 1], zero_rows[0:1, 0, :]).then_inc(zeros_stored, 16)
            pool.wait_ge(zeros_stored, 32)
            nc.gpsimd.memset(fm_o[HT:HT + 1], 1.0)
            link(nc.gpsimd.memset(k0[HT:HT + 1], 1.0))
            pool.wait_ge(patches_in[E_BUFS - 1], 64 * E_TILES // E_BUFS)
            pool.dma_start(router_w[:], a["router_w"]).then_inc(w_moe, 16)
            for e in range(EXPERTS):
                pool.dma_start(moe_wi[:, :, e], a["moe_wi"][e]).then_inc(w_moe, 16)
                pool.dma_start(moe_wo[:, e], a["moe_wo"][e]).then_inc(w_moe, 16)
            pool.dma_start(qkv1_w[:], a["qkv1_w"]).then_inc(w_l1, 16)
            for j in range(2):
                pool.dma_start(scale1[64 * j:64 * j + 64], a["scale1"][j:j + 1].to_broadcast([64, 6])).then_inc(w_l1, 16)
            pool.dma_start(proj1_w[:], a["proj1_w"]).then_inc(w_l1, 16)
            pool.dma_start(bias1[:], a["bias1"].to_broadcast([HT, DIM])).then_inc(w_l1, 16)
            for t_, n in ((wq2[:], "wq2"), (wk2[:], "wk2"), (bq2[:], "bq2"), (bk2[:], "bk2"), (wv2[:], "wv2"), (wo2[0:HT], "wo2"), (wo2[HT:HT + 1, 0, :], "bo2"), (ln_gb[:], "ln_gb"),
                          (fc1_w[:], "fc1_w"), (fc1_b[:], "fc1_b"), (fc2_w[:], "fc2_w"), (r_in_w[:], "r_in_w"),
                          (r_o1_w[:], "r_o1_w"), (r_o2_w[:], "r_o2_w"), (r_o3_w[:], "r_o3_w"),
                          (r_b[:, 0:2], "r_b"), (r_b[0:RHD // 2, 2:3], "r_o2_b"), (lra_dn[:], "lra_dn"), (lra_up[:], "lra_up")):
                pool.dma_start(t_, a[n]).then_inc(w_ffn, 16)
            pool.dma_start(bv2[:], a["bv2"].to_broadcast([T72, DIM])).then_inc(w_ffn, 16)
            pool.dma_start(fc2_b[:], a["fc2_b"].to_broadcast([HT, DIM])).then_inc(w_ffn, 16)

            last_slot = pool.to_reg(SLOTS - 1)
            zero_row = pool.to_reg(SLOTS)
            with pool.Fori(0, GROUPS) as g:
                n_ln = [0]

                def rsqrt_part(part, second=False):
                    n_ln[0] += 1
                    pool.wait_ge(var_ready, g * 12 + n_ln[0])
                    c = slice(HALF * part, HALF * part + HALF)
                    nc.gpsimd.tensor_tensor((rstd2 if second else rstd)[:, c], (var_eps2 if second else var_eps)[:, c],
                                            minus_half[:, c], ALU.pow).then_inc(rstd_ready, 1)

                def rsqrt():
                    for part in range(2):
                        rsqrt_part(part)

                def expand(which, t):
                    if t >= 3:
                        filled(pool, g, (f"S{which}", t - 3))
                    elif t == 0:
                        emptied(pool, g, (f"Q{which}", 0), (f"Q{which}", 1))
                    c0 = t * PN
                    for hf in range(2):
                        if which == 0:
                            n, q, rows = HEADS, q0, mix_in[:, hf, :]
                        else:
                            n, q, rows = HEADS // 2, q2, own_head[:, hf, hf * HEADS // 2:(hf + 1) * HEADS // 2]
                        ins = nc.gpsimd.tensor_tensor(
                            qg0[t % 3][0:HT, hf, 0:PN * n].rearrange("p (n g) -> p n g", g=n),
                            q[:, hf, c0:c0 + PN].unsqueeze(2).to_broadcast([HT, PN, n]),
                            rows.unsqueeze(1).to_broadcast([HT, PN, n]), ALU.mult)
                    ins.then_inc(qg_ready if which == 0 else qg2_ready, 1)

                rsqrt()
                pool.wait_ge(mix_ready, 1)
                for t in range(GB * PACKS + 7):
                    if t < GB * PACKS:
                        expand(0, t)
                    if t >= 10 and t % 4 == 2:
                        b = (t - 10) // 4
                        emptied(pool, g, ("Y0", 2 * b), ("Y0", 2 * b + 1))
                        nc.gpsimd.tensor_tensor(u0_t, y0_t, feature_y[:].unsqueeze(2).to_broadcast([HT, 2, TOK]), ALU.mult)\
                            .then_inc(y_scaled, 1)
                rsqrt()
                for k in range(2):
                    pool.wait_ge(rows_chosen, g * 2 + (k + 1))
                    nc.gpsimd.tensor_tensor(carrier[:, k], minus_half[:], minus_half[:], ALU.add)
                    for j in range(NT):
                        pool.indirect_dma_start(
                            expert_rows[:, :], bass.IndirectOffsetOnAxis(ap=row_idx[:, k, j:j + 1], axis=0),
                            tm_x[:, j, :], None, bounds_check=last_slot, oob_is_err=False).then_inc(scattered, 16)
                pool.wait_ge(results_out, g * EXPERTS * 48 + EXPERTS * 48)
                nc.gpsimd.tensor_tensor(carrier[:, 2], minus_half[:], minus_half[:], ALU.add)
                for j in range(NT):
                    for k in range(2):
                        pool.indirect_dma_start(
                            back[:, j, k * DIM:(k + 1) * DIM], None,
                            result_rows[:, :], bass.IndirectOffsetOnAxis(ap=row_idx[:, k, j:j + 1], axis=0),
                            bounds_check=zero_row, oob_is_err=False).then_inc(gathered[j], 16)
                rsqrt()
                pool.wait_ge(ln_ready, g * 12 + 6)
                pool.wait_ge(w_l1, 80)
                nc.gpsimd.tensor_tensor(h[:], h[:], bias1[:].unsqueeze(1).to_broadcast([HT, NT, DIM]), ALU.add)\
                    .then_inc(bias1_added, 1)
                for part in range(2):
                    rsqrt_part(part)
                    rsqrt_part(part, second=True)
                for t in range(GB * PACKS):
                    expand(2, t)
                rsqrt()
                filled(pool, g, ("LN", 5, 1))
                pool.wait_ge(bits_ready, g + 1)
                nc.gpsimd.tensor_tensor(tm_x, bits[:, :, 1:2].to_broadcast([HT, NT, DIM]),
                                        fc2_b[:].unsqueeze(1).to_broadcast([HT, NT, DIM]), ALU.mult).then_inc(pool_step, 1)
                pool.wait_ge(pool_step, g + 1)
                nc.gpsimd.tensor_tensor(tm_x, tm_x, tm_z, ALU.add).then_inc(ffn_base, 1)
                emptied(pool, g, ("F2", 1))
                emptied(pool, g, ("F2", 0))
                nc.gpsimd.tensor_tensor(h[:], h[:], tm_z, ALU.add).then_inc(out_added, 1)

        @block.scalar
        def _(act):
            act.wait_ge(pool_setup, 3)

            def table_for(func):
                nc.scalar.activation(table_out[:], minus_half[:], func)

            img_t = img_rows.rearrange("b (hp wp) d -> (b hp) wp d", wp=4)
            with act.Fori(0, E_TILES // E_BUFS) as i:
                for t in range(E_BUFS):
                    act.wait_ge(emb_emptied, i * 2 * E_BUFS + (2 * t + 2))
                    for wp in range(4):
                        act.dma_start(img_t[bass.ds(i * 32 * E_BUFS + t * 32, 32), wp], emb_out[t % 2][wp * 32:wp * 32 + 32])\
                            .then_inc(emb_stored[t % 2], 16)
            with act.Fori(0, GROUPS) as g:
                def copy(key_, out_, in_):
                    filled(act, g, key_)
                    nc.scalar.copy(out_, in_).then_inc(to_empty(key_), 1)

                c288 = lambda key_, m: slot(key_)[0:m, :, 0:CH]
                fm = lambda buf, hf: buf[0:HT, hf].rearrange("p (c n) -> p c n", c=2)
                def chunk(key_, c):
                    copy(key_, fm_x[:, :, c * CH:(c + 1) * CH], slot(key_)[0:HT, :, 0:CH])

                def mixed(which):
                    for t in range(GB * PACKS + 2):
                        if t < GB * PACKS:
                            exp_tiles(g, act, which, t)
                        if t >= 2 and t % 2 == 0:
                            mixed_out(g, act, nc.scalar.copy, which, t - 2)

                chunk(("LN", 0, 1), 1)
                copy(("V0", 1), v0[:, 4:8].rearrange("p (c j) d -> p c (j d)", c=2),
                     slot(("V0", 1))[0:T72, :, 0:2 * DIM])
                copy(("Q0", 1), fm(q0, 1), c288(("Q0", 1), HT))
                copy(("K0", 1), fm(k0, 1), c288(("K0", 1), HT))
                mixed(0)
                chunk(("LN", 1, 1), 1)
                emptied(act, g, ("LG",))
                nc.scalar.activation(lg2[:], lg[:], ACT.Exp).then_inc(logit_exp, 1)
                copy(("XT", 1), xe[:, :, 480:960], slot(("XT", 1))[0:HT, :, 0:480])
                for e in range(EXPERTS):
                    filled(act, g, ("H", e, 0))
                    nc.scalar.activation(hid[e % 2][:, 0:4].rearrange("p (c j) n -> p c (j n)", c=2),
                                         slot(("H", e, 0))[:, :, 0:2 * CAP], ACT.Relu).then_inc(to_empty(("H", e, 0)), 1)
                chunk(("LN", 2, 1), 1)
                for s in range(STEPS + 3):
                    if s % 4 == 0 and s < STEPS:
                        hp = s // 4
                        copy(("K1", hp), k1[hp % 2].rearrange("p (c n) -> p c n", c=2), c288(("K1", hp), 128))
                    if s < STEPS:
                        exp_pair(g, act, s)
                    if 2 <= s < STEPS + 2 and s % 2 == 0:
                        copy(("T1", s - 2), pt1[s % 2].rearrange("p a b n -> p a (b n)"), c288(("T1", s - 2), T72))
                    if s >= 3 and s % 2 == 1:
                        hp, b = divmod(s - 3, 4)
                        copy(("O1", s - 3), ot1[:, hp, b * TOK:(b + 1) * TOK], slot(("O1", s - 3))[:, 0, 0:TOK])
                table_for(ACT.Gelu)

                def affine(key_, dst, c, gain, last):
                    for hf in range(2):
                        ins = nc.scalar.activation(dst[0:HT, hf, c * CH:(c + 1) * CH], slot(key_)[0:HT, hf, 0:CH], ACT.Identity,
                                                   bias=ln_gb[:, hf, gain + 1:gain + 2], scale=ln_gb[:, hf, gain:gain + 1])
                    if last:
                        ins.then_inc(to_empty(key_), 1)

                filled(act, g, ("LN", 4, 1))
                affine(("LN", 4, 1), fm_r, 1, 4, False)
                affine(("LN", 4, 1), fm_x, 1, 0, True)
                filled(act, g, ("E1",))
                nc.scalar.activation(e_t.rearrange("p (c n) -> p c n", c=2), c288(("E1",), RHD), ACT.Gelu,
                                     bias=r_b[:, 0:1]).then_inc(to_empty(("E1",)), 1)
                filled(act, g, ("H1",))
                emptied(act, g, ("GC",))
                for b in range(GB):
                    ins = nc.scalar.activation(h1_t[:, b * TOK:(b + 1) * TOK],
                                               slot(("H1",))[:, b // 2, (b % 2) * TOK:(b % 2 + 1) * TOK], ACT.Gelu,
                                               bias=g_bias[:, b:b + 1])
                ins.then_inc(to_empty(("H1",)), 1)
                filled(act, g, ("H2",))
                nc.scalar.activation(h2_t[0:RHD // 2].rearrange("p (c n) -> p c n", c=2), c288(("H2",), RHD // 2),
                                     ACT.Gelu, bias=r_b[0:RHD // 2, 2:3]).then_inc(to_empty(("H2",)), 1)
                table_for(ACT.Exp)
                for half in range(2):
                    filled(act, g, ("K2", half))
                    nc.scalar.activation(fm(k2, half), c288(("K2", half), HT), ACT.Identity,
                                         bias=bk2[:, half:half + 1]).then_inc(to_empty(("K2", half)), 1)
                mixed(2)
                table_for(ACT.Gelu)
                filled(act, g, ("LN", 5, 1))
                affine(("LN", 5, 1), fm_x, 1, 2, True)
                for i in range(FT):
                    filled(act, g, ("F1", i))
                    nc.scalar.activation(ff[:, i].rearrange("p (c n) -> p c n", c=2), c288(("F1", i), 128), ACT.Gelu,
                                         bias=fc1_b[:, i:i + 1]).then_inc(to_empty(("F1", i)), 1)
                table_for(ACT.Exp)
                chunk(("OUT", 1), 1)
                copy(("DT", 1), fm_o[0:HT, :, CH:2 * CH], slot(("DT", 1))[0:HT, :, 0:CH])

        @block.vector
        def _(dve):
            done = [0]

            def link_setup(ins):
                ins.then_inc(vec_setup, 1)
                done[0] += 1
                dve.wait_ge(vec_setup, done[0])

            nc.vector.memset(ones_row, 1.0).then_inc(ones_set, 1)
            dve.wait_ge(w_tok, 96)
            link_setup(nc.vector.tensor_tensor(emb_bias, emb_bias, emb_b, ALU.add))
            for s in range(4):
                nc.vector.memset(negmax[0][:, s:s + 1], 0.0).then_inc(psum_emptied[s], 1)
            with dve.Fori(0, E_TILES // E_BUFS) as i:
                for t in range(E_BUFS):
                    for hf in range(2):
                        dve.wait_ge(emb_filled, i * 2 * E_BUFS + (2 * t + 1))
                        ins = nc.vector.tensor_copy(emb_xt[:, 3 * hf:3 * hf + 3], ps[0][:, hf, 0:384].rearrange("p (a b) -> p a b", a=3))
                    ins.then_inc(emb_emptied, 1)
                    dve.wait_ge(emb_filled, i * 2 * E_BUFS + (2 * t + 2))
                    if t >= 2:
                        dve.wait_ge(emb_stored[t % 2], i * 32 * E_BUFS + 64 * (t // 2))
                    nc.vector.tensor_tensor(emb_out[t % 2], ps[1][:, 0, 0:DIM], emb_bias, ALU.add).then_inc(emb_emptied, 1)
                for t in range(2):
                    dve.wait_ge(emb_stored[t], i * 32 * E_BUFS + 32 * E_BUFS)
            dve.wait_ge(w_l0, W_L0)
            link_setup(nc.vector.tensor_scalar(coef_y[:], coef_y[:], -2.0, 1.0, ALU.mult, ALU.add))
            link_setup(nc.vector.tensor_scalar(coef_z[:], coef_z[:], 3.0, None, ALU.mult))
            dve.wait_ge(pool_setup, 3)
            for values_, sums, dims in ((coef_y, feature_y, None), (coef_z, feature_z, "p f (a e) -> p f e a"),
                                        (None, parity, "p f (a e) -> p f e a")):
                if values_ is None:
                    source = own_head
                else:
                    source = by_head
                    link_setup(nc.vector.tensor_tensor(by_head[:], own_head[:],
                                                       values_[:].unsqueeze(1).to_broadcast([HT, 2, HEADS]), ALU.mult))
                link_setup(nc.vector.tensor_reduce(sums[:], source[:].rearrange(dims, e=2) if dims else source[:], AX.X, ALU.add))
                link_setup(nc.vector.tensor_scalar(sums[:], sums[:], float(D0) ** 0.5, None, ALU.mult))
            nc.vector.tensor_scalar(mix_in[:], mix_in[:], float(D0) ** -0.5, None, ALU.mult).then_inc(mix_ready, 1)

            with dve.Fori(0, GROUPS) as g:
                n_step = [0]
                n_ln = [0]

                def link(ins):
                    n_step[0] += 1
                    ins.then_inc(vec_step, 1)
                    dve.wait_ge(vec_step, g * VEC_STEPS + n_step[0])

                def ln_stats(src, part, ins=None):
                    c = slice(HALF * part, HALF * part + HALF)
                    for j in TILES_OF[part] if ins is None else ():
                        ins = nc.vector.bn_stats(stats[:, j, :], src[:, j, :])
                    link(ins)
                    even, odd = stats[:, c, 0:3], stats[:, c, 3:6]
                    nc.vector.tensor_tensor(mean2[:, c], even[:, :, 1], odd[:, :, 1], ALU.add)
                    nc.vector.tensor_tensor(diff[:, c], even[:, :, 1], odd[:, :, 1], ALU.subtract)
                    link(nc.vector.tensor_tensor(var[:, c], even[:, :, 2], odd[:, :, 2], ALU.add))
                    nc.vector.tensor_scalar(mean[:, c], mean2[:, c], 0.5, None, ALU.mult)
                    nc.vector.tensor_scalar(var2[:, c], var[:, c], 1.0 / DIM, EPS, ALU.mult, ALU.add)
                    link(nc.vector.scalar_tensor_tensor(diff2[:, c], diff[:, c], 0.25, diff[:, c], ALU.mult, ALU.mult))
                    nc.vector.tensor_tensor(var_eps[:, c], var2[:, c], diff2[:, c], ALU.add).then_inc(var_ready, 1)

                def ln_apply(src, dst, part):
                    n_ln[0] += 1
                    dve.wait_ge(rstd_ready, g * 12 + n_ln[0])
                    for j in TILES_OF[part]:
                        ins = nc.vector.tensor_scalar(dst[:, j, :], src[:, j, :], mean[:, j:j + 1], rstd[:, j:j + 1],
                                                      ALU.subtract, ALU.mult)
                    ins.then_inc(ln_ready, 1)

                def layernorm(src, dst):
                    for part in range(2):
                        ln_stats(src, part)
                    for part in range(2):
                        ln_apply(src, dst, part)

                c288 = lambda key_, m: slot(key_)[0:m, :, 0:CH]
                fm = lambda buf, hf: buf[0:HT, hf].rearrange("p (c n) -> p c n", c=2)

                def copy(key_, out_, in_):
                    filled(dve, g, key_)
                    nc.vector.tensor_copy(out_, in_).then_inc(to_empty(key_), 1)

                def add_to(key_, i, dst, base):
                    filled(dve, g, key_)
                    c = slice(HALF * i, HALF * i + HALF)
                    nc.vector.tensor_tensor(dst[:, c], tiles(key_), base[:, c], ALU.add).then_inc(to_empty(key_), 1)

                def accumulate(name, i):
                    add_to((name, i), i, h, h)
                    emptied(dve, g, (name, i))
                    ln_stats(h, i)

                def chunk(key_, c):
                    copy(key_, fm_x[:, :, c * CH:(c + 1) * CH], slot(key_)[0:HT, :, 0:CH])

                def gated(name, bit, base, parts):
                    for i in parts:
                        filled(dve, g, (name, i))
                        for j in TILES_OF[i]:
                            ins = nc.vector.scalar_tensor_tensor(tm_z[:, j, :], tiles((name, i))[:, j % HALF], bits[:, j, bit:bit + 1],
                                                                 base[:, j, :], ALU.mult, ALU.add)
                        ins.then_inc(to_empty((name, i)), 1)
                        if name == "P2":
                            emptied(dve, g, (name, i))
                            ln_stats(tm_z, i)

                def mixed(which):
                    def own_rows(key_, dst, coef, base=None):
                        filled(dve, g, key_)
                        n = dst.shape[2]
                        src = slot(key_)[0:HT, :, 0:2 * n].rearrange("p f (e n) -> p f e n", e=2)
                        if base is None:
                            link(nc.vector.tensor_scalar(dst, src[:, :, 0], coef[:, 0, 0:1], None, ALU.mult))
                            ins = nc.vector.scalar_tensor_tensor(dst, src[:, :, 1], coef[:, 0, 1:2], dst, ALU.mult, ALU.add)
                        else:
                            for hf in range(2):
                                ins = nc.vector.scalar_tensor_tensor(base[:, hf], src[:, hf, 0], coef[:, hf, 0:1], base[:, hf],
                                                                     ALU.mult, ALU.add)
                            link(ins)
                            for hf in range(2):
                                ins = nc.vector.scalar_tensor_tensor(dst[:, hf], src[:, hf, 1], coef[:, hf, 1:2], base[:, hf],
                                                                     ALU.mult, ALU.add)
                        ins.then_inc(to_empty(key_), 1)

                    for t in range(GB * PACKS + (5 if which == 0 else 4)):
                        if which == 0 and t >= 8 and t % 4 == 0:
                            b = (t - 8) // 4
                            copy(("YT", b), y0, slot(("YT", b))[0:T72, :, 0:DIM])
                        if t < GB * PACKS:
                            filled(dve, g, (f"S{which}", t))
                            nc.vector.tensor_reduce(negmax[t % 3][:].rearrange("p (a b) -> p a b", a=2),
                                                    slot((f"S{which}", t))[0:RP, :, 0:CH].rearrange("p a (b n) -> p a b n", b=2),
                                                    AX.X, ALU.max, negate=True).then_inc(max_ready[which], 1)
                        if 1 <= t <= GB * PACKS:
                            emptied(dve, g, (f"S{which}", t - 1))
                            link(nc.vector.reciprocal(rinv[(t - 1) % 3][:], rowsum[(t - 1) % 3][:]))
                            e = probs0[(t - 1) % 3][0:RP]
                            nc.vector.tensor_tensor(e, e, rinv[(t - 1) % 3][:].unsqueeze(2).to_broadcast([RP, PACK, TOK]),
                                                    ALU.mult).then_inc(probs_ready[which], 1)
                        if t >= 5 and t % 2 == 1 and t < GB * PACKS + 4:
                            b, nh = divmod((t - 5) // 2, 2)
                            dst = (y0_t[:, :, nh * T72:(nh + 1) * T72] if which == 0 else
                                   fm_o[0:HT, :, b * TOK + nh * T72:b * TOK + (nh + 1) * T72])
                            own_rows((f"Y{which}", 2 * b + nh), dst, parity)
                        if which == 0 and t >= 8 and t % 4 == 0:
                            b = (t - 8) // 4
                            dve.wait_ge(y_scaled, g * GB + (b + 1))
                            own_rows(("Z0", b), fm_o[0:HT, :, b * TOK:(b + 1) * TOK], feature_z, u0_t)
                        if 2 <= t < GB * PACKS + 2 and t % 2 == 1:
                            mixed_out(g, dve, nc.vector.tensor_copy, which, t - 2)
                        if which == 0 and t == GB * PACKS - 2:
                            accumulate("P0", 0)
                        if which == 2 and t == GB * PACKS + 1:
                            gated("P2", 0, tm_x, (0,))

                dve.wait_ge(h_loaded, g * 96 + 96)
                layernorm(tm_x, tm_z)
                chunk(("LN", 0, 0), 0)
                copy(("V0", 0), v0[:, 0:4].rearrange("p (c j) d -> p c (j d)", c=2), slot(("V0", 0))[0:T72, :, 0:2 * DIM])
                copy(("Q0", 0), fm(q0, 0), c288(("Q0", 0), HT))
                copy(("K0", 0), fm(k0, 0), c288(("K0", 0), HT))
                mixed(0)
                accumulate("P0", 1)
                for part in range(2):
                    ln_apply(h, tm_x, part)

                chunk(("LN", 1, 0), 0)
                filled(dve, g, ("LG",))
                logits = slot(("LG",))[0:HT, 0, 0:NT * EXPERTS].rearrange("p (j e) -> p j e", e=EXPERTS)
                link(nc.vector.tensor_reduce(lgm[:], logits, AX.X, ALU.max))
                wide = lambda v: v.unsqueeze(2).to_broadcast([HT, NT, EXPERTS])
                nc.vector.tensor_tensor(lg[:], logits, wide(lgm[:]), ALU.subtract).then_inc(to_empty(("LG",)), 1)
                dve.wait_ge(logit_exp, g + 1)
                link(nc.vector.tensor_reduce(lgs[:], lg2[:], AX.X, ALU.add))
                link(nc.vector.reciprocal(lgs[:], lgs[:]))
                link(nc.vector.tensor_tensor(lg2[:], lg2[:], wide(lgs[:]), ALU.mult))
                by_e = lambda v: v.unsqueeze(1).to_broadcast([HT, NT, EXPERTS])
                for k in range(2):
                    link(nc.vector.tensor_reduce(gate[:, :, k], lg2[:], AX.X, ALU.max))
                    link(nc.vector.tensor_tensor(lg[:], lg2[:], wide(gate[:, :, k]), ALU.is_equal))
                    link(nc.vector.tensor_tensor(lg[:], lg[:], by_e(first_e[:]), ALU.mult))
                    link(nc.vector.tensor_reduce(key[:], lg[:], AX.X, ALU.max))
                    link(nc.vector.tensor_tensor(picked[:, k], lg[:], wide(key[:]), ALU.is_equal))
                    nc.vector.tensor_copy(picked_bf[:, k], picked[:, k]).then_inc(picked_ready, 1)
                    if k == 0:
                        nc.vector.scalar_tensor_tensor(lg2[:], picked[:, 0], -2.0, lg2[:], ALU.mult, ALU.add)
                    link(nc.vector.tensor_tensor(base[:, k], picked[:, k], by_e(base_e[:]), ALU.mult))
                    link(nc.vector.tensor_reduce(first_row[:, k], base[:, k], AX.X, ALU.add))
                    filled(dve, g, ("CT", k))
                    counts = slot(("CT", k))[0:HT, 0, 0:NT * EXPERTS].rearrange("p (j e) -> p j e", e=EXPERTS)
                    nc.vector.tensor_tensor(place[:, k], counts, picked[:, k], ALU.mult).then_inc(to_empty(("CT", k)), 1)
                    emptied(dve, g, ("CT", k))
                    link(nc.vector.tensor_reduce(pos[:, k], place[:, k], AX.X, ALU.add))
                    nc.vector.tensor_tensor(row_of[:, k], first_row[:, k], pos[:, k], ALU.add)
                    link(nc.vector.tensor_scalar(over[:, k], pos[:, k], float(CAP) - 0.5, float(2 * SLOTS), ALU.is_gt, ALU.mult))
                    link(nc.vector.tensor_tensor(row_to[:, k], row_of[:, k], over[:, k], ALU.add))
                    nc.vector.tensor_scalar(row_idx[:, k], row_to[:, k], float(SLOTS), None, ALU.min).then_inc(rows_chosen, 1)

                for i in (0, 2):
                    copy(("XT", i), xe[:, :, 480 * i:480 * i + 480], slot(("XT", i))[0:HT, :, 0:480])
                for e in range(EXPERTS + 1):
                    if e < EXPERTS:
                        filled(dve, g, ("H", e, 1))
                        nc.vector.tensor_scalar(hid[e % 2][:, 4:6].rearrange("p j n -> p (j n)"),
                                                slot(("H", e, 1))[:, 0, 0:2 * CAP], 0.0, None, ALU.max)\
                            .then_inc(to_empty(("H", e, 1)), 1)
                    if e >= 1:
                        copy(("EO", e - 1), eo[:, e - 1], slot(("EO", e - 1))[:, 0, 0:DIM + HT])
                for part in range(2):
                    for j in TILES_OF[part]:
                        dve.wait_ge(gathered[j], g * 32 + 32)
                        for k in range(2):
                            link(nc.vector.scalar_tensor_tensor(h[:, j, :], back[:, j, k * DIM:(k + 1) * DIM],
                                                                gate[:, j, k:k + 1], h[:, j, :], ALU.mult, ALU.add))
                        ins = nc.vector.bn_stats(stats[:, j, :], h[:, j, :])
                    ln_stats(h, part, ins)
                    ln_apply(h, tm_z, part)
                    if part == 0:
                        chunk(("LN", 2, 0), 0)

                def max_pair(s):
                    filled(dve, g, ("S1", s))
                    nc.vector.tensor_reduce(negmax[s % 3][0:T72].rearrange("p (a b) -> p a b", a=2),
                                            slot(("S1", s))[0:T72, :, 0:CH].rearrange("p a (b n) -> p a b n", b=2),
                                            AX.X, ALU.max, negate=True).then_inc(max_ready[1], 1)

                for s in range(STEPS + 3):
                    if s % 4 == 0 and s < STEPS:
                        hp = s // 4
                        filled(dve, g, ("Q1", hp))
                        nc.vector.tensor_scalar(q1[hp % 2].rearrange("p (c n) -> p c n", c=2), c288(("Q1", hp), 128),
                                                scale1[:, hp:hp + 1], None, ALU.mult).then_inc(to_empty(("Q1", hp)), 1)
                        filled(dve, g, ("V1", hp))
                        for c in range(2):
                            ins = nc.vector.tensor_copy(v1[hp % 2][:, 4 * c:4 * c + 4],
                                                        slot(("V1", hp))[0:T72, c, :].rearrange("p (j a d) -> p j a d", j=4, a=2))
                        ins.then_inc(to_empty(("V1", hp)), 1)
                    if s < STEPS:
                        max_pair(s)
                    if 1 <= s <= STEPS:
                        emptied(dve, g, ("S1", s - 1))
                        link(nc.vector.reciprocal(rinv[(s - 1) % 3][0:T72], rowsum[(s - 1) % 3][0:T72]))
                        e = p12[(s - 1) % 3].rearrange("p a b n -> p (a b) n")
                        nc.vector.tensor_tensor(e, e, rinv[(s - 1) % 3][0:T72].unsqueeze(2).to_broadcast([T72, 4, TOK]),
                                                ALU.mult).then_inc(probs_ready[1], 1)
                    if 2 <= s < STEPS + 2 and s % 2 == 1:
                        copy(("T1", s - 2), pt1[s % 2].rearrange("p a b n -> p a (b n)"), c288(("T1", s - 2), T72))
                    if s >= 3 and s % 2 == 0:
                        hp, b = divmod(s - 3, 4)
                        copy(("O1", s - 3), ot1[:, hp, b * TOK:(b + 1) * TOK], slot(("O1", s - 3))[:, 0, 0:TOK])
                dve.wait_ge(bias1_added, g + 1)

                def affine(key_, dst, c, gain, last):
                    for hf in range(2):
                        ins = nc.vector.tensor_scalar(dst[0:HT, hf, c * CH:(c + 1) * CH], slot(key_)[0:HT, hf, 0:CH],
                                                      ln_gb[:, hf, gain:gain + 1], ln_gb[:, hf, gain + 1:gain + 2],
                                                      ALU.mult, ALU.add)
                    if last:
                        ins.then_inc(to_empty(key_), 1)

                for part in range(2):
                    accumulate("P1", part)
                    c = slice(HALF * part, HALF * part + HALF)
                    link(nc.vector.scalar_tensor_tensor(var_only[:, c], var[:, c], 1.0 / DIM, diff2[:, c], ALU.mult, ALU.add))
                    if part == 1:
                        filled(dve, g, ("LN", 4, 0))
                        affine(("LN", 4, 0), fm_r, 0, 4, False)
                        affine(("LN", 4, 0), fm_x, 0, 0, True)
                    n_ln[0] += 1
                    dve.wait_ge(rstd_ready, g * 12 + n_ln[0])
                    link(nc.vector.tensor_tensor(var_r[:, c], var_only[:, c], rstd[:, c], ALU.mult))
                    link(nc.vector.tensor_tensor(var_rr[:, c], var_r[:, c], rstd[:, c], ALU.mult))
                    nc.vector.tensor_scalar(var_eps2[:, c], var_rr[:, c], EPS, None, ALU.add).then_inc(var_ready, 1)
                    n_ln[0] += 1
                    dve.wait_ge(rstd_ready, g * 12 + n_ln[0])
                    link(nc.vector.tensor_tensor(rstd_both[:, c], rstd[:, c], rstd2[:, c], ALU.mult))
                    for j in TILES_OF[part]:
                        ins = nc.vector.tensor_scalar(tm_z[:, j, :], h[:, j, :], mean[:, j:j + 1], rstd_both[:, j:j + 1],
                                                      ALU.subtract, ALU.mult)
                    ins.then_inc(ln_ready, 1)
                for j in range(NT):
                    ins = nc.vector.tensor_scalar(tm_x[:, j, :], h[:, j, :], mean[:, j:j + 1], rstd[:, j:j + 1],
                                                  ALU.subtract, ALU.mult)
                ins.then_inc(ln_ready, 2)

                def queries(half):
                    filled(dve, g, ("Q2", half))
                    nc.vector.tensor_scalar(fm(q2, half), c288(("Q2", half), HT), bq2[:, half:half + 1], None, ALU.add)\
                        .then_inc(to_empty(("Q2", half)), 1)

                def values(i):
                    filled(dve, g, ("V2", i))
                    for c in range(2):
                        ins = nc.vector.tensor_tensor(v2[:, 4 * i + 2 * c:4 * i + 2 * c + 2],
                                                      slot(("V2", i))[0:T72, c, 0:2 * DIM].rearrange("p (j d) -> p j d", j=2),
                                                      bv2[:].unsqueeze(1).to_broadcast([T72, 2, DIM]), ALU.add)
                    ins.then_inc(to_empty(("V2", i)), 1)

                queries(0)
                emptied(dve, g, ("E1",))
                link(nc.vector.tensor_reduce(g_mean[:], e_t.rearrange("p (b n) -> p b n", b=GB)[:, :, 1:TOK], AX.X, ALU.add))
                nc.vector.tensor_scalar(g_mean[:], g_mean[:], 1.0 / (TOK - 1), None, ALU.mult).then_inc(g_mean_ready, 1)
                queries(1)
                filled(dve, g, ("GC",))
                nc.vector.tensor_scalar(g_bias[:], slot(("GC",))[0:RHD, 0, 0:GB], r_b[:, 1:2], None, ALU.add)\
                    .then_inc(to_empty(("GC",)), 1)
                nc.vector.memset(h2_t[RHD // 2:RHD // 2 + 1, :], 1.0).then_inc(h2_ones, 1)
                values(0)
                values(1)
                copy(("RL",), rl[:].rearrange("p j a b -> p (j a b)"), slot(("RL",))[0:HT, 0, 0:4 * NT])
                emptied(dve, g, ("RL",))
                link(nc.vector.tensor_tensor(bits[:], rl[:, :, :, 1], rl[:, :, :, 0], ALU.is_gt))
                link(nc.vector.tensor_tensor(bits[:], bits[:], reserved[:].unsqueeze(2).to_broadcast([HT, NT, 2]), ALU.max))
                link(nc.vector.tensor_scalar(nbits[:], bits[:], -1.0, 1.0, ALU.mult, ALU.add))
                nc.vector.tensor_tensor(sel[:, :, 0], nbits[:, :, 0], nbits[:, :, 1], ALU.mult)
                nc.vector.tensor_tensor(sel[:, :, 1], nbits[:, :, 0], bits[:, :, 1], ALU.mult)
                nc.vector.tensor_tensor(sel[:, :, 2], bits[:, :, 0], nbits[:, :, 1], ALU.mult).then_inc(bits_ready, 1)
                mixed(2)
                gated("P2", 0, tm_x, (1,))
                for part in range(2):
                    ln_apply(tm_z, tm_x, part)
                filled(dve, g, ("LN", 5, 0))
                affine(("LN", 5, 0), fm_x, 0, 2, True)
                dve.wait_ge(ffn_base, g + 1)
                gated("F2", 1, tm_x, (0, 1))
                chunk(("OUT", 0), 0)
                for i in range(2):
                    filled(dve, g, ("DN", i))
                    for j in TILES_OF[i]:
                        ins = nc.vector.tensor_tensor(tm_x[:, j].rearrange("p (k r) -> p k r", k=3),
                                                      tiles(("DN", i))[:, j % HALF].rearrange("p (k r) -> p k r", k=3),
                                                      sel[:, j].unsqueeze(2).to_broadcast([HT, 3, RANK]), ALU.mult)
                    ins.then_inc(to_empty(("DN", i)), 1)
                copy(("DT", 0), fm_o[0:HT, :, 0:CH], slot(("DT", 0))[0:HT, :, 0:CH])
                dve.wait_ge(out_added, g + 1)
                add_to(("UP", 0), 0, h, h)
                add_to(("UP", 1), 1, h, h)
                assert n_step[0] == VEC_STEPS, n_step[0]

        @block.tensor
        def _(pe):
            pe.wait_ge(w_tok, 96)
            pe.wait_ge(pool_setup, 3)
            with pe.Fori(0, E_TILES // E_BUFS) as i:
                for t in range(E_BUFS):
                    pe.wait_ge(patches_in[t], i * 64 + 64)
                    for c in range(6):
                        ins = nc.tensor.transpose(ps[0][:, c // 3, (c % 3) * 128:(c % 3 + 1) * 128], emb_x[t][:, c, :], ident[:])
                    ins.then_inc(emb_filled, 1)
                    pe.wait_ge(emb_emptied, i * 2 * E_BUFS + (2 * t + 1))
                    for c in range(6):
                        ins = nc.tensor.matmul(ps[1][:, 0, 0:DIM], emb_xt[:, c, :], emb_w[:, c, :], start=(c == 0), stop=(c == 5))
                    ins.then_inc(emb_filled, 1)
            pe.wait_ge(emb_emptied, 2 * E_TILES)

            with pe.Fori(0, GROUPS) as g:
                order = iter(UNITS)

                def begin(key_, reads=()):
                    assert next(order) == key_, key_
                    s, n = UNIT[key_] % 4, UNIT[key_] // 4
                    emptied(pe, g, *reads, but=s)
                    pe.wait_ge(psum_emptied[s], g * SLOT_USES[s] + (n + 1))
                    return slot(key_)

                def turn_tile(s, c, src):
                    for hf in range(2):
                        for j in TILES_OF[c]:
                            ins = nc.tensor.transpose(s[0:HT, hf, (j % HALF) * HT:(j % HALF + 1) * HT],
                                                      src[:, j, hf * HT:(hf + 1) * HT], ident[0:HT, 0:HT])
                    ins.then_inc(psum_filled, 1)

                def turn_tiles(k, src, reads=((), ()), after=None):
                    for c in range(2):
                        if after is not None:
                            pe.wait_ge(ln_ready, g * 12 + (2 * after + c + 1))
                        turn_tile(begin((*k, c), reads[c]), c, src)

                def by_feature(key_, w, m, x, reads=(), then=()):
                    s = begin(key_, reads)
                    for c in range(2):
                        if c == 1:
                            emptied(pe, g, *then)
                        for hf in range(2):
                            ins = nc.tensor.matmul(s[0:m, c, 0:CH], w(hf), x[0:HT, hf, c * CH:(c + 1) * CH],
                                                   start=(hf == 0), stop=(hf == 1))
                    ins.then_inc(psum_filled, 1)

                def by_token(key_, i, x, w, reads=(), bias=False, parts=2):
                    s = begin(key_, reads)
                    o = tiles(key_)
                    for j in TILES_OF[i]:
                        for f in range(parts):
                            k = 128 if parts > 2 else HT + 1 if bias and f == 0 else HT
                            ins = nc.tensor.matmul(o[:, j % HALF], x[0:k, f, j * HT:(j + 1) * HT], w[0:k, f, :],
                                                   start=(f == 0), stop=(f == parts - 1))
                    ins.then_inc(psum_filled, 1)

                def value_unit(name, i, w, reads):
                    s = begin((name, i), reads)
                    for j in range(4):
                        t = 4 * i + j
                        for hf in range(2):
                            ins = nc.tensor.matmul(s[0:T72, j // 2, (j % 2) * DIM:(j % 2 + 1) * DIM],
                                                   fm_x[:, hf, t * T72:(t + 1) * T72], w[:, hf, :],
                                                   start=(hf == 0), stop=(hf == 1))
                    ins.then_inc(psum_filled, 1)

                def mixed(which, k, v, at):
                    def apply(s, at_col, n, p, x):
                        for hf in range(2):
                            for e in range(2):
                                for mh in range(2):
                                    for q in range(3):
                                        ins = nc.tensor.matmul(s[32 * q:32 * q + 32, hf, e * n + at_col:e * n + at_col + T72],
                                                               x(mh)[:, hf * HT + 32 * q:hf * HT + 32 * q + 32],
                                                               p[:, mh, 6 * hf + 2 * q + e, :],
                                                               start=(mh == 0), stop=(mh == 1))
                        return ins

                    for t in range(GB * PACKS + (5 if which == 0 else 4)):
                        if which == 0 and t >= 8 and t % 4 == 0:
                            b = (t - 8) // 4
                            s = begin(("YT", b), [("Y0", 2 * b), ("Y0", 2 * b + 1)])
                            for nh in range(2):
                                for hf in range(2):
                                    ins = nc.tensor.transpose(s[0:T72, nh, hf * HT:(hf + 1) * HT],
                                                              y0_t[:, hf, nh * T72:(nh + 1) * T72], ident[0:HT, 0:HT])
                            ins.then_inc(psum_filled, 1)
                        if t < GB * PACKS:
                            b = t // PACKS
                            pe.wait_ge(qg_ready if which == 0 else qg2_ready, g * GB * PACKS + (t + 1))
                            s = begin((f"S{which}", t), both(f"K{which}"))
                            for i in range(PACK):
                                if which == 2:
                                    hf, c = i // 2, i % 2
                                    ins = nc.tensor.matmul(s[0:RP, hf, c * TOK:(c + 1) * TOK], qg0[t % 3][0:HT, hf, c * RP:(c + 1) * RP],
                                                           k[0:HT, hf, b * TOK:(b + 1) * TOK], start=True, stop=True)
                                    continue
                                for hf in range(2):
                                    r = HT + 1 if hf == 0 else HT
                                    ins = nc.tensor.matmul(s[0:RP, i // 2, (i % 2) * TOK:(i % 2 + 1) * TOK],
                                                           qg0[t % 3][0:r, hf, i * RP:(i + 1) * RP],
                                                           k[0:r, hf, b * TOK:(b + 1) * TOK], start=(hf == 0), stop=(hf == 1))
                            ins.then_inc(psum_filled, 1)
                        if t >= 5 and t % 2 == 1 and t < GB * PACKS + 4:
                            b, nh = divmod((t - 5) // 2, 2)
                            s = begin((f"Y{which}", 2 * b + nh), [(f"M{which}", 4 * b + 2 * nh + p) for p in range(2)] + both(f"V{which}"))
                            apply(s, 0, T72, at[(2 * b + nh) % len(at)], lambda mh: v[:, 2 * b + mh]).then_inc(psum_filled, 1)
                        if which == 0 and t >= 8 and t % 4 == 0:
                            b = (t - 8) // 4
                            s = begin(("Z0", b), [("YT", b)])
                            for nh in range(2):
                                ins = apply(s, nh * T72, TOK, at[(2 * b + nh) % len(at)], lambda mh: y0[:, mh])
                            ins.then_inc(psum_filled, 1)
                        if 2 <= t < GB * PACKS + 2:
                            pe.wait_ge(probs_ready[which], g * GB * PACKS + (t - 1))
                            s = begin((f"M{which}", t - 2))
                            for mh in range(2):
                                for i in range(PACK):
                                    o = s[0:T72, mh, i * RP:(i + 1) * RP]
                                    p = probs0[(t - 2) % 3]
                                    if which == 0:
                                        ins = nc.tensor.matmul(o, p[:, i, mh * T72:(mh + 1) * T72], mix_out[:], start=True, stop=True)
                                    else:
                                        ins = nc.tensor.transpose(o, p[0:RP, i, mh * T72:(mh + 1) * T72], ident[0:RP, 0:RP])
                            ins.then_inc(psum_filled, 1)
                        if which == 0 and t == GB * PACKS - 2:
                            by_token(("P0", 0), 0, fm_o, proj0_w, [("Z0", 0), ("Z0", 1)], bias=True)
                        if which == 2 and t == GB * PACKS + 1:
                            by_token(("P2", 0), 0, fm_o, wo2, [("Y2", b) for b in range(GB)], bias=True)

                def both(*k):
                    return [(*k, 0), (*k, 1)]

                turn_tiles(("LN", 0), tm_z, after=0)
                pe.wait_ge(w_l0, W_L0)
                for i in range(2):
                    value_unit("V0", i, qkv0_w[:, :, 2 * DIM:3 * DIM], [("LN", 0, i)])
                for o, k in ((0, "Q0"), (DIM, "K0")):
                    for half in range(2):
                        by_feature((k, half), lambda hf: qkv0_w[:, hf, o + half * HT:o + (half + 1) * HT], HT, fm_x)
                mixed(0, k0, v0, at0)
                by_token(("P0", 1), 1, fm_o, proj0_w, [("Z0", 2), ("Z0", 3)], bias=True)

                turn_tiles(("LN", 1), tm_x, after=1)
                pe.wait_ge(w_moe, W_MOE)
                s = begin(("LG",), [("LN", 1, 0)])
                for j in range(NT):
                    if j == HALF:
                        emptied(pe, g, ("LN", 1, 1))
                    for hf in range(2):
                        ins = nc.tensor.matmul(s[0:HT, 0, j * EXPERTS:(j + 1) * EXPERTS], fm_x[:, hf, j * HT:(j + 1) * HT],
                                               router_w[:, hf, :], start=(hf == 0), stop=(hf == 1))
                ins.then_inc(psum_filled, 1)
                for k in range(2):
                    pe.wait_ge(picked_ready, g * 2 + (k + 1))
                    s = begin(("CT", k))
                    counts = s[0:HT, 0, 0:NT * EXPERTS].rearrange("p (j e) -> p j e", e=EXPERTS)
                    nc.tensor.matmul(counts, before_bf[:], picked_bf[:, k], start=True, stop=False)
                    for d in range(1, NT):
                        ins = nc.tensor.matmul(counts[:, d:NT], ones_bf[:], picked_bf[:, k, 0:NT - d], start=False, stop=(k == 0 and d == NT - 1))
                    if k == 1:
                        for i in range(NT):
                            ins = nc.tensor.matmul(counts, ones_bf[:], picked_bf[:, 0, i].unsqueeze(1).to_broadcast([HT, NT, EXPERTS]),
                                                   start=False, stop=(i == NT - 1))
                    ins.then_inc(psum_filled, 1)

                for i in range(3):
                    pe.wait_ge(experts_in[i], g * 16 + 16)
                    s = begin(("XT", i))
                    for hf in range(2):
                        for c in range(4):
                            ins = nc.tensor.transpose(s[0:HT, hf, c * SLOT_P:(c + 1) * SLOT_P],
                                                      xe_tok[:, 4 * i + c, hf * HT:(hf + 1) * HT], ident[0:SLOT_P, 0:SLOT_P])
                    ins.then_inc(psum_filled, 1)
                def hidden(e, part):
                    s = begin(("H", e, part), [("XT", i) for i in range(((e + 1) * CAP - 1) // 480 + 1)])
                    for f in (range(0, 4) if part == 0 else range(4, 6)):
                        for hf in range(2):
                            ins = nc.tensor.matmul(s[:, (f % 4) // 2, (f % 2) * CAP:(f % 2 + 1) * CAP],
                                                   moe_wi[:, hf, e, f * 128:(f + 1) * 128],
                                                   xe[:, hf, e * CAP:(e + 1) * CAP], start=(hf == 0), stop=(hf == 1))
                    ins.then_inc(psum_filled, 1)

                for e in range(EXPERTS + 1):
                    if e < EXPERTS:
                        hidden(e, 0)
                        hidden(e, 1)
                    if e >= 1:
                        s = begin(("EO", e - 1), both("H", e - 1))
                        for starts, width in (((0, 64), DIM), ((CAP - 64, CAP - 64), HT)):
                            for f in range(FT):
                                for c in range(2):
                                    at = 0 if width == DIM else c * HT
                                    to = 0 if width == DIM else DIM
                                    ins = nc.tensor.matmul(s[64 * c:64 * c + 64, 0, to:to + width],
                                                           hid[(e - 1) % 2][:, f, starts[c]:starts[c] + 64],
                                                           moe_wo[:, e - 1, f, at:at + width], start=(f == 0), stop=(f == FT - 1))
                        ins.then_inc(psum_filled, 1)

                def score_pair(s_):
                    hp, b = divmod(s_, GB)
                    s = begin(("S1", s_), [("Q1", hp), ("K1", hp)])
                    q, k = q1[hp % 2], k1[hp % 2]
                    for nh in range(2):
                        for a_ in range(2):
                            r = a_ * D1
                            o = s[0:T72, a_, nh * TOK:(nh + 1) * TOK]
                            nc.tensor.matmul(o, q[r:r + D1, b * TOK + nh * T72:b * TOK + (nh + 1) * T72],
                                             k[r:r + D1, b * TOK:(b + 1) * TOK], start=True, stop=False)
                            ins = nc.tensor.matmul(o[:, nh * T72:(nh + 1) * T72], ident_bf[:], diag_bf[:], start=False, stop=True)
                    ins.then_inc(psum_filled, 1)

                def turn_probs(key_, p):
                    s = begin(key_)
                    for a_ in range(2):
                        for mh in range(2):
                            for nh in range(2):
                                ins = nc.tensor.transpose(s[0:T72, a_, mh * TOK + nh * T72:mh * TOK + (nh + 1) * T72],
                                                          p[:, a_, nh, mh * T72:(mh + 1) * T72], ident[0:T72, 0:T72])
                    ins.then_inc(psum_filled, 1)

                def attend(key_, pt, v, b, reads):
                    s = begin(key_, reads)
                    for mh in range(2):
                        for a_ in range(2):
                            ins = nc.tensor.matmul(s[D1 * a_:D1 * a_ + D1, 0, 0:TOK], v(2 * b + mh, a_), pt[:, a_, mh, :],
                                                   start=(mh == 0), stop=(mh == 1))
                    ins.then_inc(psum_filled, 1)

                pe.wait_ge(ln_ready, g * 12 + 5)
                turn_tile(begin(("LN", 2, 0)), 0, tm_z)
                pe.wait_ge(w_l1, 80)

                def project1(name, hp, s, c):
                    cols = slice(hp * 128, (hp + 1) * 128)
                    if name == "V1":
                        for t in range(4 * c, 4 * c + 4):
                            for hf in range(2):
                                ins = nc.tensor.matmul(s[0:T72, c, (t % 4) * 128:(t % 4 + 1) * 128],
                                                       fm_x[:, hf, t * T72:(t + 1) * T72], qkv1_w[:, hf, 2, cols],
                                                       start=(hf == 0), stop=(hf == 1))
                    else:
                        for hf in range(2):
                            ins = nc.tensor.matmul(s[0:128, c, 0:CH], qkv1_w[:, hf, 0 if name == "Q1" else 1, cols],
                                                   fm_x[:, hf, c * CH:(c + 1) * CH], start=(hf == 0), stop=(hf == 1))
                    if c == 1:
                        ins.then_inc(psum_filled, 1)

                for s_ in range(STEPS + 3):
                    if s_ % 4 == 0 and s_ < STEPS:
                        hp = s_ // 4
                        units = ("Q1", "K1", "V1")
                        if hp == 0:
                            turned = begin(("LN", 2, 1))
                            slots = [begin((name, hp), [("LN", 2, 0)]) for name in units]
                            for name, s in zip(units, slots):
                                project1(name, hp, s, 0)
                            pe.wait_ge(ln_ready, g * 12 + 6)
                            turn_tile(turned, 1, tm_z)
                            emptied(pe, g, ("LN", 2, 1))
                            for name, s in zip(units, slots):
                                project1(name, hp, s, 1)
                        else:
                            for name in units:
                                s = begin((name, hp))
                                for c in range(2):
                                    project1(name, hp, s, c)
                    if s_ < STEPS:
                        score_pair(s_)
                    if 2 <= s_ < STEPS + 2:
                        pe.wait_ge(probs_ready[1], g * STEPS + (s_ - 1))
                        turn_probs(("T1", s_ - 2), p12[(s_ - 2) % 3])
                    if s_ >= 3:
                        hp, b = divmod(s_ - 3, 4)
                        attend(("O1", s_ - 3), pt1[(s_ - 3) % 2], lambda t, a_: v1[hp % 2][:, t, a_, :], b,
                               [("T1", s_ - 3), ("V1", hp)])
                for i in range(2):
                    by_token(("P1", i), i, ot1, proj1_w, [("O1", 4 * hp + 2 * i + j) for hp in range(6) for j in range(2)], parts=6)

                turn_tiles(("LN", 4), tm_z, after=3)
                pe.wait_ge(w_ffn, W_FFN)
                half_of = lambda w, half: lambda hf: w[:, hf, half * HT:(half + 1) * HT]
                by_feature(("E1",), lambda hf: r_in_w[:, hf, :], RHD, fm_r, [("LN", 4, 0)], [("LN", 4, 1)])
                by_feature(("Q2", 0), half_of(wq2, 0), HT, fm_x)
                by_feature(("Q2", 1), half_of(wq2, 1), HT, fm_x)
                pe.wait_ge(g_mean_ready, g + 1)
                s = begin(("GC",))
                nc.tensor.matmul(s[0:RHD, 0, 0:GB], r_o1_w[:, 1, :], g_mean[:], start=True, stop=True).then_inc(psum_filled, 1)
                value_unit("V2", 0, wv2, [])
                s = begin(("H1",))
                for c in range(2):
                    ins = nc.tensor.matmul(s[0:RHD, c, 0:CH], r_o1_w[:, 0, :], e_t[:, c * CH:(c + 1) * CH], start=True, stop=True)
                ins.then_inc(psum_filled, 1)
                value_unit("V2", 1, wv2, [])
                s = begin(("H2",), [("H1",)])
                for c in range(2):
                    ins = nc.tensor.matmul(s[0:RHD // 2, c, 0:CH], r_o2_w[:], h1_t[:, c * CH:(c + 1) * CH], start=True, stop=True)
                ins.then_inc(psum_filled, 1)
                by_feature(("K2", 0), half_of(wk2, 0), HT, fm_x)
                by_feature(("K2", 1), half_of(wk2, 1), HT, fm_x)
                pe.wait_ge(h2_ones, g + 1)
                s = begin(("RL",), [("H2",)])
                for j in range(NT):
                    ins = nc.tensor.matmul(s[0:HT, 0, 4 * j:4 * j + 4], h2_t[:, j * HT:(j + 1) * HT], r_o3_w[:], start=True, stop=True)
                ins.then_inc(psum_filled, 1)
                mixed(2, k2, v2, at2)
                by_token(("P2", 1), 1, fm_o, wo2, [("Y2", b) for b in range(GB, 2 * GB)], bias=True)

                turn_tiles(("LN", 5), tm_x, after=5)
                for i in range(FT):
                    by_feature(("F1", i), lambda hf: fc1_w[:, hf, i * 128:(i + 1) * 128], 128, fm_x,
                               [("LN", 5, 0)], [("LN", 5, 1)] if i == 0 else ())
                for i in range(2):
                    by_token(("F2", i), i, ff, fc2_w, [("F1", f) for f in range(FT)], parts=FT)
                turn_tiles(("OUT",), tm_z, ([("F2", 0)], [("F2", 1)]))
                for i in range(2):
                    by_token(("DN", i), i, fm_x, lra_dn, [("OUT", i)])
                turn_tiles(("DT",), tm_x, ([("DN", 0)], [("DN", 1)]))
                for i in range(2):
                    by_token(("UP", i), i, fm_o, lra_up, [("DT", i)])


_ORDER = ["x", "txt", "tok_w", "tok_b", "pos", "qkv0_w", "proj_l_w", "proj_l_b", "proj_w_w", "proj_w_b", "lamb", "proj0_w",
          "proj0_b", "router_w", "moe_wi", "moe_wo", "qkv1_w", "scale1", "proj1_w", "bias1", "wq2", "wk2", "bq2", "bk2",
          "wv2", "bv2", "wo2", "bo2", "ln_gb", "fc1_w", "fc1_b", "fc2_w", "fc2_b", "r_in_w", "r_o1_w", "r_o2_w", "r_o3_w",
          "r_b", "r_o2_b", "lra_dn", "lra_up"]


def laid_out(i):
    def by_part(w, p):
        return w.reshape(w.shape[0] // p, p, w.shape[1]).transpose(1, 0, 2)

    row = lambda v: v.reshape(1, -1)
    f = {k[len("L1_ffn_"):]: v for k, v in i.items() if k.startswith("L1_ffn_")}
    return {
        "x": i["x"].reshape(SEQS, 64, 192), "txt": i["txt"], "tok_w": by_part(i["L0_tok_W"], 128), "tok_b": row(i["L0_tok_b"]),
        "pos": np.tile(i["L0_tok_pos_emb"].reshape(4, 4, DIM), (8, 1, 1)),
        "qkv0_w": by_part(i["L0_attn_qkv_w"].T, HT), "proj_l_w": i["L0_attn_proj_l_w"].T, "proj_l_b": row(i["L0_attn_proj_l_b"]),
        "proj_w_w": i["L0_attn_proj_w_w"].T, "proj_w_b": row(i["L0_attn_proj_w_b"]), "lamb": row(i["L0_attn_lamb"]),
        "proj0_w": by_part(i["L0_attn_proj_out_w"].T, HT), "proj0_b": row(i["L0_attn_proj_out_b"]),
        "router_w": by_part(i["L0_ffn_w_router"], HT),
        "moe_wi": i["L0_ffn_wi"].reshape(EXPERTS, 2, HT, FF).transpose(0, 2, 1, 3),
        "moe_wo": i["L0_ffn_wo"].reshape(EXPERTS, FT, 128, DIM).transpose(0, 2, 1, 3),
        "qkv1_w": by_part(i["L1_attn_W_qkv"], HT).reshape(HT, 2, 3, HEADS * D1),
        "scale1": i["L1_attn_scale"].reshape(6, 2).T, "proj1_w": by_part(i["L1_attn_W_out"], 128), "bias1": row(i["L1_attn_b_out"]),
        "wq2": by_part(f["wq"].T, HT), "wk2": by_part(f["wk"].T, HT), "bq2": f["bq"].reshape(2, HT).T, "bk2": f["bk"].reshape(2, HT).T,
        "wv2": by_part(f["wv"].T, HT), "bv2": row(f["bv"]), "wo2": by_part(f["wo"].T, HT), "bo2": row(f["bo"]),
        "ln_gb": np.stack([f[n].reshape(2, HT).T for n in ("ln1_g", "ln1_b", "ln2_g", "ln2_b", "r_ln_g", "r_ln_b")], axis=2),
        "fc1_w": by_part(f["fc1_w"].T, HT), "fc1_b": f["fc1_b"].reshape(FT, 128).T, "fc2_w": by_part(f["fc2_w"].T, 128),
        "fc2_b": row(f["fc2_b"]), "r_in_w": by_part(f["r_in_w"].T, HT), "r_o1_w": by_part(f["r_o1_w"].T, RHD),
        "r_o2_w": f["r_o2_w"].T, "r_o3_w": np.concatenate([f["r_o3_w"].T, row(f["r_o3_b"])]),
        "r_b": np.stack([f["r_in_b"], f["r_o1_b"]], axis=1), "r_o2_b": f["r_o2_b"].reshape(-1, 1),
        "lra_dn": by_part(f["lra_down"].reshape(3 * RANK, DIM).T, HT),
        "lra_up": by_part(f["lra_up"].transpose(0, 2, 1).reshape(3 * RANK, DIM), HT),
    }


def kernel(**inputs):
    import concourse.bacc as bacc
    from concourse.bass_utils import run_bass_kernel_spmd

    nc = bacc.Bacc("TRN2", target_bir_lowering=False, num_devices=1)
    laid = laid_out({k: np.asarray(v) for k, v in inputs.items()})
    arrays, aps = {}, {}
    for name in _ORDER:
        v = np.ascontiguousarray(laid[name])
        arrays["in_" + name] = v
        aps[name] = nc.dram_tensor("in_" + name, v.shape, mybir.dt.from_np(v.dtype), kind="ExternalInput").ap()
    out = nc.dram_tensor("out", (SEQS, TOK, DIM), F32, kind="ExternalOutput").ap()
    program(nc, aps, out.rearrange("b n d -> (b n) d"))
    return run_bass_kernel_spmd(nc, [arrays], core_ids=[0]).results[0]["out"]
```
